# Optimizing a Trainium2 kernel written in Bass

```python
import numpy as np
import jax
import jax.numpy as jnp

def _softmax(x, axis=-1):
    return jax.nn.softmax(x, axis=axis)

def _gelu(x):
    return jax.nn.gelu(x, approximate=True)

def _silu(x):
    return jax.nn.silu(x)

def _sigmoid(x):
    return jax.nn.sigmoid(x)

def _layernorm(x, axis=-1, eps=1e-05):
    m = jnp.mean(x, axis=axis, keepdims=True)
    v = jnp.var(x, axis=axis, keepdims=True)
    return (x - m) / jnp.sqrt(v + eps)

def _scatter_add(tgt, idx, src, axis=0):
    return tgt.at[idx].add(src)

def _segment_sum(src, seg, n):
    return jax.ops.segment_sum(src, seg, n)
kernel_name = 'mk_cond_seq_d4_seqx_r8_aeb3c9'

def setup_inputs(seed: int=0):
    np.random.seed(seed)
    _w = jnp.asarray

    def _rec_inputs():
        import jax
        import jax.numpy as jnp
        _rk = jax.random.key(seed)
        x = -0.0002928 + 1 * jax.random.normal(jax.random.fold_in(_rk, 1), (32, 32, 128), jnp.float32)
        _lenS = 32 - jax.random.randint(jax.random.fold_in(_rk, 7), (32,), 0, max(1, 32 // 4) + 1, jnp.int32)
        _lenS2 = 32 - jax.random.randint(jax.random.fold_in(_rk, 8), (32,), 0, max(1, 32 // 4) + 1, jnp.int32)
        itok_B_0_7 = jax.random.randint(jax.random.fold_in(_rk, 11), (32,), 0, 8, jnp.int32)
        condB_theta = jax.random.uniform(jax.random.fold_in(_rk, 12), (32,), jnp.float32, 0.0, 0.983423)
        condB_phi = jax.random.uniform(jax.random.fold_in(_rk, 13), (32,), jnp.float32, 0.0, 0.961312)
        itok_B_6_14 = jax.random.randint(jax.random.fold_in(_rk, 14), (32,), 6, 15, jnp.int32)
        itok_B_34_63 = jax.random.randint(jax.random.fold_in(_rk, 16), (32,), 34, 64, jnp.int32)
        fside_Bx16xSxS_0 = -1.47943e-05 + 1.00017 * jax.random.normal(jax.random.fold_in(_rk, 17), (32, 16, 32, 32), jnp.float32)
        _validS = jnp.arange(32)[None, :] < _lenS[:, None]
        _validS2 = jnp.arange(32)[None, :] < _lenS2[:, None]
        _causal = jnp.tril(jnp.ones((32, 32), dtype=bool))
        mask_Bx1xSxS_bk0 = jnp.logical_not(jnp.broadcast_to(_validS[:, None, None, :], (32, 1, 32, 32)))
        return (x, itok_B_0_7, condB_theta, condB_phi, itok_B_6_14, itok_B_34_63, fside_Bx16xSxS_0, mask_Bx1xSxS_bk0)
    x, itok_B_0_7, condB_theta, condB_phi, itok_B_6_14, itok_B_34_63, fside_Bx16xSxS_0, mask_Bx1xSxS_bk0 = _rec_inputs()

    def _L0_cond_setup():
        import jax, jax.numpy as jnp
        import numpy as np
        E, H, I = (8, 128, 512)
        B, S = (4, 128)
        LN_EPS = 1e-12
        key = jax.random.key(seed)
        ks = jax.random.split(key, 8)
        x = jax.random.normal(ks[0], (B, S, H), dtype=jnp.float32)
        expert_idx = jax.random.randint(ks[1], (B,), 0, E, dtype=jnp.int64)
        Wi = jax.random.normal(ks[2], (E, H, I), dtype=jnp.float32) * 0.02
        bi = jnp.zeros((E, I), dtype=jnp.float32)
        Wo = jax.random.normal(ks[3], (E, I, H), dtype=jnp.float32) * 0.02
        bo = jnp.zeros((E, H), dtype=jnp.float32)
        gamma = jnp.ones((E, H), dtype=jnp.float32)
        beta = jnp.zeros((E, H), dtype=jnp.float32)
        return {'input_tensor': x, 'expert_idx': expert_idx, 'Wi': Wi, 'bi': bi, 'Wo': Wo, 'bo': bo, 'gamma': gamma, 'beta': beta}
    _L0_cond_all = _L0_cond_setup()
    _L0_cond_in = {k: v for k, v in _L0_cond_all.items() if k in ('Wi', 'bi', 'Wo', 'bo', 'gamma', 'beta')}
    del _L0_cond_all

    def _L1_cond_setup():
        import jax, jax.numpy as jnp
        import numpy as np
        key = jax.random.key(seed)
        k1, k2, k3 = jax.random.split(key, 3)
        B, N, D = (16, 512, 128)
        embeddings = jax.random.normal(k1, (B, N, D), dtype=jnp.float32)
        theta = jax.random.uniform(k2, (B,), dtype=jnp.float32)
        phi = jax.random.uniform(k3, (B,), dtype=jnp.float32)
        return {'embeddings': embeddings, 'theta': theta, 'phi': phi}
    _L1_cond_all = _L1_cond_setup()
    _L1_cond_in = {k: v for k, v in _L1_cond_all.items() if k in ()}
    del _L1_cond_all

    def _L2_cond_setup():
        import jax, jax.numpy as jnp
        import numpy as np
        D = 128
        E = 8
        FF = 512
        TOPK = 2
        S = 32
        SE = 64
        SH = 128
        B, T = (2, 256)

        def _forward(x, subject_ids, ln_g, ln_b, subj_emb, hyp_w1, hyp_b1, hyp_w2, hyp_b2, sty_w1, sty_b1, sty_w2, sty_b2, router_w, exp_w1, exp_b1, exp_w2, exp_b2):
            mu = x.mean(-1, keepdims=True)
            var = x.var(-1, keepdims=True)
            h = (x - mu) * jax.lax.rsqrt(var + 1e-05) * ln_g + ln_b
            m_t = h.mean(1, keepdims=True)
            v_t = h.var(1, keepdims=True)
            h_norm = (h - m_t) * jax.lax.rsqrt(v_t + 1e-08)
            se = subj_emb[subject_ids]
            hyp = jax.nn.relu(se @ hyp_w1 + hyp_b1) @ hyp_w2 + hyp_b2
            sty = jax.nn.relu(hyp @ sty_w1 + sty_b1) @ sty_w2 + sty_b2
            gamma, beta = jnp.split(sty, 2, axis=-1)
            gamma = jax.nn.softplus(gamma) + 1e-08
            h = h_norm * gamma[:, None, :] + beta[:, None, :]
            h_flat = h.reshape(-1, D)
            probs = jax.nn.softmax(h_flat @ router_w, axis=-1)
            gates, idx = jax.lax.top_k(probs, TOPK)
            gates = gates / gates.sum(-1, keepdims=True)
            N = h_flat.shape[0]
            combine = jnp.zeros((N, E), h_flat.dtype).at[jnp.arange(N)[:, None], idx].add(gates)
            hid = jax.nn.relu(jnp.einsum('nd,edf->nef', h_flat, exp_w1) + exp_b1)
            eout = jnp.einsum('nef,efd->ned', hid, exp_w2) + exp_b2
            y = jnp.einsum('ned,ne->nd', eout, combine)
            return x + y.reshape(x.shape)
        key = jax.random.key(seed)
        ks = jax.random.split(key, 16)
        n = lambda k, sh, s=0.02: jax.random.normal(k, sh, dtype=jnp.float32) * s
        return {'x': jax.random.normal(ks[0], (B, T, D), dtype=jnp.float32), 'subject_ids': jax.random.randint(ks[1], (B,), 0, S), 'ln_g': jnp.ones((D,), jnp.float32), 'ln_b': jnp.zeros((D,), jnp.float32), 'subj_emb': n(ks[2], (S, SE)), 'hyp_w1': n(ks[3], (SE, SH), 1.0 / np.sqrt(SE)), 'hyp_b1': jnp.zeros((SH,), jnp.float32), 'hyp_w2': n(ks[4], (SH, SH), 1.0 / np.sqrt(SH)), 'hyp_b2': jnp.zeros((SH,), jnp.float32), 'sty_w1': n(ks[5], (SH, SH // 2), 1.0 / np.sqrt(SH)), 'sty_b1': jnp.zeros((SH // 2,), jnp.float32), 'sty_w2': n(ks[6], (SH // 2, 2 * D), 1.0 / np.sqrt(SH // 2)), 'sty_b2': jnp.zeros((2 * D,), jnp.float32), 'router_w': n(ks[7], (D, E), 1.0 / np.sqrt(D)), 'exp_w1': n(ks[8], (E, D, FF), 1.0 / np.sqrt(D)), 'exp_b1': jnp.zeros((E, FF), jnp.float32), 'exp_w2': n(ks[9], (E, FF, D), 1.0 / np.sqrt(FF)), 'exp_b2': jnp.zeros((E, D), jnp.float32)}
    _L2_cond_all = _L2_cond_setup()
    _L2_cond_in = {k: v for k, v in _L2_cond_all.items() if k in ('ln_g', 'ln_b', 'subj_emb', 'hyp_w1', 'hyp_b1', 'hyp_w2', 'hyp_b2', 'sty_w1', 'sty_b1', 'sty_w2', 'sty_b2', 'router_w', 'exp_w1', 'exp_b1', 'exp_w2', 'exp_b2')}
    del _L2_cond_all

    def _L3_cond_setup():
        import jax, jax.numpy as jnp
        import numpy as np
        import math
        D_MODEL = 128
        N_HEAD = 16
        HEAD_DIM = D_MODEL // N_HEAD
        D_FF = 512
        NUM_STEPS = 100.0
        RESCALE = 4000.0
        EPS = 1e-05

        def _sin_emb(t):
            half = D_MODEL // 2
            x = t.astype(jnp.float32) / NUM_STEPS * RESCALE
            freqs = jnp.exp(jnp.arange(half, dtype=jnp.float32) * (-math.log(10000.0) / (half - 1)))
            e = x[:, None] * freqs[None, :]
            return jnp.concatenate([jnp.sin(e), jnp.cos(e)], axis=-1)

        def _ln(x):
            m = jnp.mean(x, axis=-1, keepdims=True)
            v = jnp.var(x, axis=-1, keepdims=True)
            return (x - m) / jnp.sqrt(v + EPS)

        def _gelu2(x):
            return x * jax.nn.sigmoid(1.702 * x)
        key = jax.random.key(seed)
        ks = jax.random.split(key, 24)
        B, S, D, F = (4, 64, D_MODEL, D_FF)
        std = 0.02
        inp = {'src': jax.random.normal(ks[0], (B, S, D), dtype=jnp.float32), 'src_mask': jax.random.randint(ks[1], (B, 1, S, S), 0, 2).astype(bool), 'timestep': jax.random.randint(ks[2], (B,), 0, 100, dtype=jnp.int32), 'attention_bias': jax.random.normal(ks[3], (B, N_HEAD, S, S), dtype=jnp.float32), 'W_ada': jax.random.normal(ks[4], (D, 2 * D), dtype=jnp.float32) * std, 'b_ada': jnp.zeros((2 * D,), dtype=jnp.float32), 'Wq': jax.random.normal(ks[5], (D, D), dtype=jnp.float32) * std, 'bq': jnp.zeros((D,), dtype=jnp.float32), 'Wk': jax.random.normal(ks[6], (D, D), dtype=jnp.float32) * std, 'bk': jnp.zeros((D,), dtype=jnp.float32), 'Wv': jax.random.normal(ks[7], (D, D), dtype=jnp.float32) * std, 'bv': jnp.zeros((D,), dtype=jnp.float32), 'Wo': jax.random.normal(ks[8], (D, D), dtype=jnp.float32) * std, 'bo': jnp.zeros((D,), dtype=jnp.float32), 'W1': jax.random.normal(ks[9], (D, F), dtype=jnp.float32) * std, 'b1': jnp.zeros((F,), dtype=jnp.float32), 'W2': jax.random.normal(ks[10], (F, D), dtype=jnp.float32) * std, 'b2': jnp.zeros((D,), dtype=jnp.float32), 'g2': jnp.ones((D,), dtype=jnp.float32), 'beta2': jnp.zeros((D,), dtype=jnp.float32)}
        return inp
    _L3_cond_all = _L3_cond_setup()
    _L3_cond_in = {k: v for k, v in _L3_cond_all.items() if k in ('W_ada', 'b_ada', 'Wq', 'bq', 'Wk', 'bk', 'Wv', 'bv', 'Wo', 'bo', 'W1', 'b1', 'W2', 'b2', 'g2', 'beta2')}
    del _L3_cond_all
    return {'x': x, 'itok_B_0_7': itok_B_0_7, 'condB_theta': condB_theta, 'condB_phi': condB_phi, 'itok_B_6_14': itok_B_6_14, 'itok_B_34_63': itok_B_34_63, 'fside_Bx16xSxS_0': fside_Bx16xSxS_0, 'mask_Bx1xSxS_bk0': mask_Bx1xSxS_bk0, 'L0_cond_Wi': _L0_cond_in['Wi'], 'L0_cond_bi': _L0_cond_in['bi'], 'L0_cond_Wo': _L0_cond_in['Wo'], 'L0_cond_bo': _L0_cond_in['bo'], 'L0_cond_gamma': _L0_cond_in['gamma'], 'L0_cond_beta': _L0_cond_in['beta'], 'L2_cond_ln_g': _L2_cond_in['ln_g'], 'L2_cond_ln_b': _L2_cond_in['ln_b'], 'L2_cond_subj_emb': _L2_cond_in['subj_emb'], 'L2_cond_hyp_w1': _L2_cond_in['hyp_w1'], 'L2_cond_hyp_b1': _L2_cond_in['hyp_b1'], 'L2_cond_hyp_w2': _L2_cond_in['hyp_w2'], 'L2_cond_hyp_b2': _L2_cond_in['hyp_b2'], 'L2_cond_sty_w1': _L2_cond_in['sty_w1'], 'L2_cond_sty_b1': _L2_cond_in['sty_b1'], 'L2_cond_sty_w2': _L2_cond_in['sty_w2'], 'L2_cond_sty_b2': _L2_cond_in['sty_b2'], 'L2_cond_router_w': _L2_cond_in['router_w'], 'L2_cond_exp_w1': _L2_cond_in['exp_w1'], 'L2_cond_exp_b1': _L2_cond_in['exp_b1'], 'L2_cond_exp_w2': _L2_cond_in['exp_w2'], 'L2_cond_exp_b2': _L2_cond_in['exp_b2'], 'L3_cond_W_ada': _L3_cond_in['W_ada'], 'L3_cond_b_ada': _L3_cond_in['b_ada'], 'L3_cond_Wq': _L3_cond_in['Wq'], 'L3_cond_bq': _L3_cond_in['bq'], 'L3_cond_Wk': _L3_cond_in['Wk'], 'L3_cond_bk': _L3_cond_in['bk'], 'L3_cond_Wv': _L3_cond_in['Wv'], 'L3_cond_bv': _L3_cond_in['bv'], 'L3_cond_Wo': _L3_cond_in['Wo'], 'L3_cond_bo': _L3_cond_in['bo'], 'L3_cond_W1': _L3_cond_in['W1'], 'L3_cond_b1': _L3_cond_in['b1'], 'L3_cond_W2': _L3_cond_in['W2'], 'L3_cond_b2': _L3_cond_in['b2'], 'L3_cond_g2': _L3_cond_in['g2'], 'L3_cond_beta2': _L3_cond_in['beta2']}

def reference(x, itok_B_0_7, condB_theta, condB_phi, itok_B_6_14, itok_B_34_63, fside_Bx16xSxS_0, mask_Bx1xSxS_bk0, L0_cond_Wi, L0_cond_bi, L0_cond_Wo, L0_cond_bo, L0_cond_gamma, L0_cond_beta, L2_cond_ln_g, L2_cond_ln_b, L2_cond_subj_emb, L2_cond_hyp_w1, L2_cond_hyp_b1, L2_cond_hyp_w2, L2_cond_hyp_b2, L2_cond_sty_w1, L2_cond_sty_b1, L2_cond_sty_w2, L2_cond_sty_b2, L2_cond_router_w, L2_cond_exp_w1, L2_cond_exp_b1, L2_cond_exp_w2, L2_cond_exp_b2, L3_cond_W_ada, L3_cond_b_ada, L3_cond_Wq, L3_cond_bq, L3_cond_Wk, L3_cond_bk, L3_cond_Wv, L3_cond_bv, L3_cond_Wo, L3_cond_bo, L3_cond_W1, L3_cond_b1, L3_cond_W2, L3_cond_b2, L3_cond_g2, L3_cond_beta2):
    import jax
    import jax.numpy as jnp

    def _L0_cond_ref(input_tensor, expert_idx, Wi, bi, Wo, bo, gamma, beta):
        import jax, jax.numpy as jnp
        import numpy as np
        E, H, I = (8, 128, 512)
        B, S = (4, 128)
        LN_EPS = 1e-12
        Wi_b = Wi[expert_idx]
        bi_b = bi[expert_idx]
        Wo_b = Wo[expert_idx]
        bo_b = bo[expert_idx]
        g_b = gamma[expert_idx]
        be_b = beta[expert_idx]
        h = jax.nn.gelu(jnp.einsum('bsh,bhi->bsi', input_tensor, Wi_b) + bi_b[:, None, :], approximate=False)
        o = jnp.einsum('bsi,bih->bsh', h, Wo_b) + bo_b[:, None, :]
        r = o + input_tensor
        mu = jnp.mean(r, axis=-1, keepdims=True)
        var = jnp.mean(jnp.square(r - mu), axis=-1, keepdims=True)
        y = (r - mu) * jax.lax.rsqrt(var + LN_EPS)
        return y * g_b[:, None, :] + be_b[:, None, :]

    def _L1_cond_ref(embeddings, theta, phi):
        import jax, jax.numpy as jnp
        import numpy as np
        B, N, D = embeddings.shape
        e = embeddings.reshape(B, N, D // 4, 4)
        ct = jnp.cos(theta)[:, None, None]
        st = jnp.sin(theta)[:, None, None]
        cp = jnp.cos(phi)[:, None, None]
        sp = jnp.sin(phi)[:, None, None]
        x0, x1, x2, x3 = (e[..., 0], e[..., 1], e[..., 2], e[..., 3])
        out = jnp.stack([x0 * ct + x1 * st, -x0 * st + x1 * ct, x2 * cp + x3 * sp, -x2 * sp + x3 * cp], axis=-1)
        return out.reshape(B, N, D)

    def _L2_cond_ref(x, subject_ids, ln_g, ln_b, subj_emb, hyp_w1, hyp_b1, hyp_w2, hyp_b2, sty_w1, sty_b1, sty_w2, sty_b2, router_w, exp_w1, exp_b1, exp_w2, exp_b2):
        import jax, jax.numpy as jnp
        import numpy as np
        D = 128
        E = 8
        FF = 512
        TOPK = 2
        S = 32
        SE = 64
        SH = 128
        B, T = (2, 256)

        def _forward(x, subject_ids, ln_g, ln_b, subj_emb, hyp_w1, hyp_b1, hyp_w2, hyp_b2, sty_w1, sty_b1, sty_w2, sty_b2, router_w, exp_w1, exp_b1, exp_w2, exp_b2):
            mu = x.mean(-1, keepdims=True)
            var = x.var(-1, keepdims=True)
            h = (x - mu) * jax.lax.rsqrt(var + 1e-05) * ln_g + ln_b
            m_t = h.mean(1, keepdims=True)
            v_t = h.var(1, keepdims=True)
            h_norm = (h - m_t) * jax.lax.rsqrt(v_t + 1e-08)
            se = subj_emb[subject_ids]
            hyp = jax.nn.relu(se @ hyp_w1 + hyp_b1) @ hyp_w2 + hyp_b2
            sty = jax.nn.relu(hyp @ sty_w1 + sty_b1) @ sty_w2 + sty_b2
            gamma, beta = jnp.split(sty, 2, axis=-1)
            gamma = jax.nn.softplus(gamma) + 1e-08
            h = h_norm * gamma[:, None, :] + beta[:, None, :]
            h_flat = h.reshape(-1, D)
            probs = jax.nn.softmax(h_flat @ router_w, axis=-1)
            gates, idx = jax.lax.top_k(probs, TOPK)
            gates = gates / gates.sum(-1, keepdims=True)
            N = h_flat.shape[0]
            combine = jnp.zeros((N, E), h_flat.dtype).at[jnp.arange(N)[:, None], idx].add(gates)
            hid = jax.nn.relu(jnp.einsum('nd,edf->nef', h_flat, exp_w1) + exp_b1)
            eout = jnp.einsum('nef,efd->ned', hid, exp_w2) + exp_b2
            y = jnp.einsum('ned,ne->nd', eout, combine)
            return x + y.reshape(x.shape)
        return _forward(x, subject_ids, ln_g, ln_b, subj_emb, hyp_w1, hyp_b1, hyp_w2, hyp_b2, sty_w1, sty_b1, sty_w2, sty_b2, router_w, exp_w1, exp_b1, exp_w2, exp_b2)

    def _L3_cond_ref(src, src_mask, timestep, attention_bias, W_ada, b_ada, Wq, bq, Wk, bk, Wv, bv, Wo, bo, W1, b1, W2, b2, g2, beta2):
        import jax, jax.numpy as jnp
        import numpy as np
        import math
        D_MODEL = 128
        N_HEAD = 16
        HEAD_DIM = D_MODEL // N_HEAD
        D_FF = 512
        NUM_STEPS = 100.0
        RESCALE = 4000.0
        EPS = 1e-05

        def _sin_emb(t):
            half = D_MODEL // 2
            x = t.astype(jnp.float32) / NUM_STEPS * RESCALE
            freqs = jnp.exp(jnp.arange(half, dtype=jnp.float32) * (-math.log(10000.0) / (half - 1)))
            e = x[:, None] * freqs[None, :]
            return jnp.concatenate([jnp.sin(e), jnp.cos(e)], axis=-1)

        def _ln(x):
            m = jnp.mean(x, axis=-1, keepdims=True)
            v = jnp.var(x, axis=-1, keepdims=True)
            return (x - m) / jnp.sqrt(v + EPS)

        def _gelu2(x):
            return x * jax.nn.sigmoid(1.702 * x)
        B, S, D = src.shape
        emb = jax.nn.silu(_sin_emb(timestep)) @ W_ada + b_ada
        scale, shift = jnp.split(emb[:, None, :], 2, axis=-1)
        x = _ln(src) * (1.0 + scale) + shift
        q = (x @ Wq + bq).reshape(B, S, N_HEAD, HEAD_DIM).transpose(0, 2, 1, 3)
        k = (x @ Wk + bk).reshape(B, S, N_HEAD, HEAD_DIM).transpose(0, 2, 1, 3)
        v = (x @ Wv + bv).reshape(B, S, N_HEAD, HEAD_DIM).transpose(0, 2, 1, 3)
        scores = jnp.einsum('bhqd,bhkd->bhqk', q / math.sqrt(HEAD_DIM), k)
        scores = scores + attention_bias
        scores = jnp.where(src_mask, -jnp.inf, scores.astype(jnp.float32))
        probs = jax.nn.softmax(scores, axis=-1).astype(v.dtype)
        ctx = jnp.einsum('bhqk,bhkd->bhqd', probs, v)
        ctx = ctx.transpose(0, 2, 1, 3).reshape(B, S, D)
        x = x + (ctx @ Wo + bo)
        h = _ln(x) * g2 + beta2
        ff = _gelu2(h @ W1 + b1) @ W2 + b2
        return x + ff
    x = _L0_cond_ref(x, itok_B_0_7, L0_cond_Wi, L0_cond_bi, L0_cond_Wo, L0_cond_bo, L0_cond_gamma, L0_cond_beta)
    x = _L1_cond_ref(x, condB_theta, condB_phi)
    x = _L2_cond_ref(x, itok_B_6_14, L2_cond_ln_g, L2_cond_ln_b, L2_cond_subj_emb, L2_cond_hyp_w1, L2_cond_hyp_b1, L2_cond_hyp_w2, L2_cond_hyp_b2, L2_cond_sty_w1, L2_cond_sty_b1, L2_cond_sty_w2, L2_cond_sty_b2, L2_cond_router_w, L2_cond_exp_w1, L2_cond_exp_b1, L2_cond_exp_w2, L2_cond_exp_b2)
    x = _L3_cond_ref(x, mask_Bx1xSxS_bk0, itok_B_34_63, fside_Bx16xSxS_0, L3_cond_W_ada, L3_cond_b_ada, L3_cond_Wq, L3_cond_bq, L3_cond_Wk, L3_cond_bk, L3_cond_Wv, L3_cond_bv, L3_cond_Wo, L3_cond_bo, L3_cond_W1, L3_cond_b1, L3_cond_W2, L3_cond_b2, L3_cond_g2, L3_cond_beta2)
    return x

_drawn_inputs = setup_inputs


def setup_inputs(seed=0):
    import zlib

    import numpy as np

    out = dict(_drawn_inputs(seed))
    spreads = {'L0_cond_bi': (0.0, 0.1),
     'L0_cond_bo': (0.0, 0.1),
     'L0_cond_gamma': (1.0, 0.2),
     'L0_cond_beta': (0.0, 0.1),
     'L2_cond_ln_g': (1.0, 0.6),
     'L2_cond_ln_b': (0.0, 0.8),
     'L2_cond_hyp_b1': (0.0, 0.1),
     'L2_cond_hyp_b2': (0.0, 0.1),
     'L2_cond_sty_b1': (0.0, 0.1),
     'L2_cond_sty_b2': (0.0, 0.1),
     'L2_cond_exp_b1': (0.0, 0.1),
     'L2_cond_exp_b2': (0.0, 0.1),
     'L3_cond_b_ada': (0.0, 0.1),
     'L3_cond_bq': (0.0, 0.8),
     'L3_cond_bk': (0.0, 0.8),
     'L3_cond_bv': (0.0, 0.388),
     'L3_cond_bo': (0.0, 0.1),
     'L3_cond_b1': (0.0, 0.357),
     'L3_cond_b2': (0.0, 0.1),
     'L3_cond_g2': (1.0, 0.6),
     'L3_cond_beta2': (0.0, 0.8)}
    factors = {'fside_Bx16xSxS_0': 5.447, 'L3_cond_Wq': 8.0, 'L3_cond_Wk': 8.0, 'L3_cond_Wv': 3.172}
    for name, (base, spread) in spreads.items():
        noise = np.random.default_rng([zlib.crc32(name.encode()), seed]).standard_normal(out[name].shape)
        drawn = base * np.exp(spread * noise) if base else spread * noise
        out[name] = jnp.asarray(drawn.astype(out[name].dtype))
    for name, factor in factors.items():
        out[name] = (out[name] * factor).astype(out[name].dtype)
    return out
```

```python
from contextlib import ExitStack

import concourse.bass as bass
import numpy as np
from concourse import mybir

F32 = mybir.dt.float32
F32R = mybir.dt.float32r
I32 = mybir.dt.int32
U8 = mybir.dt.uint8
ACT = mybir.ActivationFunctionType
ALU = mybir.AluOpType
AX = mybir.AxisListType

P = 128
B, S, D = 32, 32, 128
N = B * S
T = N // P
J = P // S
E = 8
F = 512
C = F // P
H, DH = 16, 8
HG, H4 = 4, 4
HALF = N // 2
BH = B // 2
BANK = 512
LO = 32
K2 = LO + E
MASKED = P + S
TWO_PI_INV = float(np.float32(1.0 / (2.0 * np.pi)))
TWO_PI_A = 6.28125
TWO_PI_B = 0.0019350051879882812
TWO_PI_C = float(2.0 * np.pi - 6.28125 - 0.0019350051879882812)
ROUND = 12582912.0
MASKED_SCORE = -1.0e38
PI_SAFE = 3.1415925



def layout(parts):
    at, out = 0, {}
    for name, width in parts:
        out[name] = (at, at + width)
        at += width
    return out, at


COLS, NCOLS = layout([
    ("exp_b1", E * C), ("ffn_b1", C), ("ln_g", 1), ("ln_b", 1), ("hyp_b1", 1), ("hyp_b2", 1), ("sty_b1", 1),
    ("sty_b2", 2), ("b_ada", 2), ("bq", 1), ("bk", 1), ("bv", 1), ("bo", 1), ("g2", 1), ("beta2", 1)])
ANG = B + 4
EARLY, EARLY_W = layout([
    ("ident", P), ("expert_row", 1), ("sample_row", 1), ("freq", 1), ("turn", ANG), ("quarter", ANG),
    ("prefer", E), ("pick", E), ("angles", 2), ("cols", NCOLS), ("subj_emb", 64), ("hyp_w1", P), ("hyp_w2", P),
    ("sty_w1", 64), ("sty_w2", 2 * P), ("w_ada", 2 * P), ("router_w", E), ("exp_b2", P)])
LATE, LATE_W = layout([
    ("head", H4), ("block", P), ("wq", P), ("wk", P), ("wv", P), ("wo", P), ("w1", F), ("w2", F), ("b2", P)])
TABLE = F + 3 * D


def build(nc, x_tm_d, x_t_d, ids_d, early_d, late_d, tables_d, wi_d, wo_d, w1_d, w2_d, fside_d, mask_d, out_d):
    ctx = ExitStack()
    with ctx:
        free = [(nc.sbuf_base + 63) // 64 * 64]

        def sb(name, shape, dt=F32, at=None):
            size = (int(np.prod(shape[1:])) * (1 if dt == U8 else 4) + 31) // 32 * 32
            region = free if at is None else at
            offset, region[0] = region[0], region[0] + size
            return nc.alloc_sbuf_tensor_at(name, shape, dt, offset=offset)

        def sem(name):
            return ctx.enter_context(nc.semaphore(name))

        early = sb("early", [P, EARLY_W])
        ids = sb("ids", [P, 3 * B], I32)
        ids_f = sb("ids_f", [P, 3 * B])
        region_x = [free[0]]
        x_t = sb("x_t", [P, N])
        x_tm = sb("x_tm", [P, T, D])
        rot_tm = sb("rot_tm", [P, T, D])
        nrm_tm = sb("nrm_tm", [P, T, D])
        affine = sb("affine", [P, 4, B])
        stat = sb("stat", [P, 2, 8])
        rstd = sb("rstd", [P, 2])
        stat4 = sb("stat4", [P, 4, 8])
        rstd4 = sb("rstd4", [P, 4])
        sums = sb("sums", [P, 3, BH])
        veps, minus_half = sb("veps", [P, BH]), sb("minus_half", [P, BH])
        region_a = [free[0]]
        wi_hi = sb("wi_hi", [P, E * F], F32R)
        wi_lo = sb("wi_lo", [P, E * F], F32R)
        region_b = [free[0]]
        wo_hi = sb("wo_hi", [P, E * F], F32R)
        wo_lo = sb("wo_lo", [P, E * F], F32R)
        region_c = [free[0]]
        xm_hi = sb("xm_hi", [P, 2, J * MASKED], F32R)
        xm_lo = sb("xm_lo", [P, 2, J * MASKED], F32R)
        hm_hi = sb("hm_hi", [P, C, J * MASKED], F32R)
        hm_lo = sb("hm_lo", [P, C, J * MASKED], F32R)
        gel = sb("gel", [P, 2, F])
        rows_tm = sb("rows_tm", [P, T, 3 * D])
        region_d = [free[0]]
        w1_hi = sb("w1_hi", [P, E * F], F32R)
        w1_lo = sb("w1_lo", [P, E * F], F32R)
        w2_region = [free[0]]
        w2 = sb("w2", [P, E * F])
        region_f = [free[0]]
        stage = sb("stage", [P, 4, 1024])
        onehot = sb("onehot", [K2, N], F32R)
        table = sb("table", [K2, TABLE], F32R)
        trig = sb("trig", [P, 2, ANG])
        rot_c = sb("rot_c", [P, T, 8])
        pick = sb("pick", [K2, E], F32R)
        turned = sb("turned", [P, D])
        row = sb("row", [P, D])
        assert free[0] <= nc.sbuf_usable_end, (free[0], nc.sbuf_usable_end)
        at = list(region_d)
        table_raw = sb("table_raw", [K2, TABLE], at=at)
        ang = sb("ang", [P, 3, ANG], at=at)
        rot_row = sb("rot_row", [B, 8], at=at)
        subj = sb("subj", [B, B], at=at)
        hyp = sb("hyp", [P, 6, B], at=at)
        time_emb = sb("time_emb", [P, B], at=at)
        of_sample = sb("of_sample", [B, N], at=at)
        at = list(region_a)
        x3_rep = sb("x3_rep", [P, B, J, S], at=list(region_a))
        cen = sb("cen", [P, N], at=at)
        sq = sb("sq", [P, N], at=list(region_x))
        hf = sb("hf", [P, N], at=at)
        hf_hi = sb("hf_hi", [P, N], F32R, at=at)
        hf_lo = sb("hf_lo", [P, N], F32R, at=at)
        act_r = sb("act_r", [P, 3, BANK], at=at)
        act_g = sb("act_g", [P, 3, BANK], at=at)
        comb_t = sb("comb_t", [K2, N], F32R, at=at)
        assert at[0] <= region_b[0], (at[0], region_b[0])
        at = list(region_f)
        rt = sb("rt", [P, 12, HALF // P * E], at=at)
        rt_s = sb("rt_s", [P, 8, HALF // P], at=at)
        comb_hl = sb("comb_hl", [P, HALF // P, K2], at=at)
        comb_hi = sb("comb_hi", [P, HALF // P * E], F32R, at=at)
        at = list(region_b)
        bias = sb("bias", [P, HG, B, S], at=at)
        sc = sb("sc", [P, HG, B, S], at=at)
        at = list(region_c)
        late = sb("late", [P, LATE_W], at=at)
        mask = sb("mask", [P, B * S], U8, at=at)
        mask_f = sb("mask_f", [P, B * S], at=at)
        y_t = sb("y_t", [P, N], at=at)
        x3_t = sb("x3_t", [P, N], at=at)
        k_t = sb("k_t", [P, N], at=at)
        ctx_t = sb("ctx_t", [P, N], at=at)
        x4_t = sb("x4_t", [P, N], at=at)
        x4_tm = sb("x4_tm", [P, T, D], at=at)
        h_t = sb("h_t", [P, N], at=at)
        rsum = sb("rsum", [P, HALF], at=at)
        head_b = sb("head_b", [P, H4], at=at)
        assert at[0] <= region_d[0], (at[0], region_d[0])
        at = list(region_d)
        qx = sb("qx", [P, B, H4, S], at=at)
        vb = sb("vb", [P, B, P], at=at)
        at = list(w2_region)
        pt = sb("pt", [P, HG, B, S], at=at)
        at = list(region_f)
        smax = sb("smax", [P, 2 * HG, BH], at=at)
        ffn_h = sb("ffn_h", [P, C, HALF], at=list(region_b))
        out_tm = sb("out_tm", [P, T, D], at=at)

        bank = [ctx.enter_context(nc.psum_tensor(f"bank{i}", [P, BANK], F32)) for i in range(8)]

        ident = early[:, EARLY["ident"][0]:EARLY["ident"][1]]

        def small(name, rows=P, k=0, n=None):
            a, b = EARLY[name]
            return early[0:rows, a + k:(a + k + n if n else b)]

        def col(name, k=0, rows=P):
            a = EARLY["cols"][0] + COLS[name][0] + k
            return early[0:rows, a:a + 1]

        def lt(name, k=0, n=None):
            a, b = LATE[name]
            return late[:, a + k:(a + k + n if n else b)]

        def per_sample(a):
            return a.unsqueeze(2).broadcast_to([a.shape[0], a.shape[1], S])

        def by_sample(a):
            return a.rearrange("p (b s) -> p b s", s=S)

        def diag(a):
            if len(a.shape) == 3:
                return a.rearrange("p c (j u) -> p c j u", u=MASKED)[:, :, :, 0:S]
            return a.rearrange("p (j u) -> p j u", u=MASKED)[:, :, 0:S]

        def by_chunk(a):
            return a.rearrange("p (c j s) -> p c j s", j=J, s=S)

        def by_tile(a):
            return a.rearrange("p (t d) -> p t d", d=P)


        d_ids, d_early, d_table, d_xt, d_xtm = sem("d_ids"), sem("d_early"), sem("d_table"), sem("d_xt"), sem("d_xtm")
        d_wi = [sem(f"d_wi{k}") for k in range(4)]
        d_wo = [sem(f"d_wo{k}") for k in range(4)]
        d_w1 = [sem(f"d_w1{k}") for k in range(4)]
        d_w2, d_late, d_mask, d_bias, d_out = sem("d_w2"), sem("d_late"), sem("d_mask"), sem("d_bias"), sem("d_out")
        dve_link = sem("dve_link")
        onehot_ready, table_ready, subj_ready = sem("onehot_ready"), sem("table_ready"), sem("subj_ready")
        of_sample_ready = sem("of_sample_ready")
        angles_ready, rot_row_ready = sem("angles_ready"), sem("rot_row_ready")
        wi_lo_ready = sem("wi_lo_ready")
        xm_ready, hm_lo_ready, o_read, var_ready = sem("xm_ready"), sem("hm_lo_ready"), sem("o_read"), sem("var_ready")
        nrm_ready = sem("nrm_ready")
        var4_ready, rstd4_ready = sem("var4_ready"), sem("rstd4_ready")
        softplus_in, gates_z, cen_ready, svar_ready = sem("softplus_in"), sem("gates_z"), sem("cen_ready"), sem("svar_ready")
        hf_ready, hf_lo_ready, comb_ready = sem("hf_ready"), sem("hf_lo_ready"), sem("comb_ready")
        gated = sem("gated")
        x3_ready, k_ready, v_ready, score_read = sem("x3_ready"), sem("k_ready"), sem("v_ready"), sem("score_read")
        smax_ready, pt_ready, ctx_div, x4_ready = sem("smax_ready"), sem("pt_ready"), sem("ctx_div"), sem("x4_ready")
        x4_tm_ready, out_ready = sem("x4_tm_ready"), sem("out_ready")
        act_link = sem("act_link")
        trig_ready, time_ready, rows_ready, hyp_ready = sem("trig_ready"), sem("time_ready"), sem("rows_ready"), sem("hyp_ready")
        softplus_ln = sem("softplus_ln")
        wi_hi_ready, wo_hi_ready, w1_hi_ready = sem("wi_hi_ready"), sem("wo_hi_ready"), sem("w1_hi_ready")
        gel_ready, hm_hi_ready, h_ready, sq_ready = sem("gel_ready"), sem("hm_hi_ready"), sem("h_ready"), sem("sq_ready")
        hf_hi_ready, gates_e, comb_t_ready, relu_ready = sem("hf_hi_ready"), sem("gates_e"), sem("comb_t_ready"), sem("relu_ready")
        y_ready, qx_ready, exp_ready, ctx_ready = sem("y_ready"), sem("qx_ready"), sem("exp_ready"), sem("ctx_ready")
        h4_ready, ffn_ready = sem("h4_ready"), sem("ffn_ready")
        zeroed, xbo_ready, wo_lo_ready, w1_lo_ready = sem("zeroed"), sem("xbo_ready"), sem("wo_lo_ready"), sem("w1_lo_ready")
        rstd_ready, srstd_ready, pool_link, bias_ready = sem("rstd_ready"), sem("srstd_ready"), sem("pool_link"), sem("bias_ready")
        sub_ready, x3_rep_ready = sem("sub_ready"), sem("x3_rep_ready")
        rows_done, rot_done, hyp_done, ada_done = sem("rows_done"), sem("rot_done"), sem("hyp_done"), sem("ada_done")
        h_done, t_done, o_done, nt_done = sem("h_done"), sem("t_done"), sem("o_done"), sem("nt_done")
        logits_done, comb_done, combb_done, s1_done = sem("logits_done"), sem("comb_done"), sem("combb_done"), sem("s1_done")
        s2_done = sem("s2_done")
        ytm_done, nt3_done, q_done, k_done = sem("ytm_done"), sem("nt3_done"), sem("q_done"), sem("k_done")
        v_done, score_done, ctx_done, wo_done = sem("v_done"), sem("score_done"), sem("ctx_done"), sem("wo_done")
        x4tm_done, n4_done, f1_done, f2_done = sem("x4tm_done"), sem("n4_done"), sem("f1_done"), sem("f2_done")

        H_BANK, T_BANK, O_BANK, NT_BANK = (0, 1), (2, 3), (4, 5), (6, 7)
        HID_BANK, GATE_BANK, Y_BANK = (0, 1, 2, 3), (4, 5), (6, 7)
        YTM_BANK, N3_BANK = (6, 7), (6, 7)
        Q_BANK, K_BANK, V_BANK = (6, 7), (5, 6), ((3, 4), (4, 5))
        SCORE_BANK, CTX_BANK, SUM_BANK = (0, 1, 2, 3), (4, 4), (5, 5)
        WO_BANK, X4_BANK, N4_BANK = (7, 2), (6, 3), (7, 2)
        F1_BANK, F2_BANK = (0, 1), (6, 7)

        block = ctx.enter_context(nc.Block())

        @block.sync
        def _(sp):
            sp.dma_start(ids[:, :], ids_d).then_inc(d_ids, 16)
            sp.dma_start(early[:, :], early_d).then_inc(d_early, 16)
            sp.dma_start(table_raw[:, :], tables_d).then_inc(d_table, 16)
            for k in range(4):
                sp.dma_start(stage[:, k, :], wi_d[:, k * 1024:(k + 1) * 1024]).then_inc(d_wi[k], 16)
                if k == 0:
                    sp.dma_start(x_t[:, :], x_t_d).then_inc(d_xt, 16)
                    sp.dma_start(x_tm[:, :, :], x_tm_d).then_inc(d_xtm, 16)
            for k in range(4):
                sp.wait_ge(wi_lo_ready, k + 1)
                sp.dma_start(stage[:, k, :], wo_d[:, k * 1024:(k + 1) * 1024]).then_inc(d_wo[k], 16)
            for k in range(4):
                sp.wait_ge(wo_lo_ready, k + 1)
                sp.dma_start(stage[:, k, :], w1_d[:, k * 1024:(k + 1) * 1024]).then_inc(d_w1[k], 16)
            sp.dma_start(w2[:, :], w2_d).then_inc(d_w2, 16)
            sp.wait_ge(nrm_ready, T)
            sp.dma_start(bias[:, :, :, :], fside_d).then_inc(d_bias, 16)
            sp.dma_start(late[:, :], late_d).then_inc(d_late, 16)
            sp.dma_start(mask[:, :], mask_d).then_inc(d_mask, 16)
            for hv in range(2):
                sp.wait_ge(out_ready, hv + 1)
                sp.dma_start(out_d[:, hv * 4:hv * 4 + 4, :], out_tm[:, hv * 4:hv * 4 + 4, :]).then_inc(d_out, 16)
            sp.wait_ge(d_out, 32)

        @block.gpsimd
        def _(pool):
            def link(ins):
                link.n += 1
                ins.then_inc(pool_link, 1)
                pool.wait_ge(pool_link, link.n)
            link.n = 0

            for a in (xm_hi, xm_lo):
                pool.memset(a[:, :, :].bitcast(F32), 0.0).then_inc(zeroed, 1)
            for a in (hm_hi, hm_lo):
                pool.memset(a[:, :, :].bitcast(F32), 0.0).then_inc(zeroed, 1)
            link(pool.memset(minus_half[:, :], -0.5))
            pool.wait_ge(d_xtm, 16)
            for t in range(T):
                pool.wait_ge(rows_ready, t + 1)
                pool.tensor_tensor(x_tm[:, t, :], x_tm[:, t, :], rows_tm[:, t, 0:D], ALU.add).then_inc(xbo_ready, 1)
            for k in range(4):
                w = slice(k * 1024, (k + 1) * 1024)
                pool.wait_ge(wo_hi_ready, k + 1)
                pool.tensor_tensor(wo_lo[:, w], stage[:, k, :], wo_hi[:, w].bitcast(F32), ALU.subtract)\
                    .then_inc(wo_lo_ready, 1)

            def power(out, in_, eps, ready):
                n = in_.shape[1]
                link(pool.tensor_scalar(veps[:, 0:n], in_, eps, None, ALU.add))
                pool.tensor_tensor(out, veps[:, 0:n], minus_half[:, 0:n], ALU.pow).then_inc(ready, 1)

            for t in range(T):
                if t >= 4:
                    for p in (2 * t - 8, 2 * t - 7):
                        w = slice(p * F, (p + 1) * F)
                        pool.wait_ge(w1_hi_ready, p + 1)
                        pool.tensor_tensor(w1_lo[:, w], stage[:, p // 2, p % 2 * F:p % 2 * F + F],
                                           w1_hi[:, w].bitcast(F32), ALU.subtract).then_inc(w1_lo_ready, 1)
                for n, eps in ((0, 1e-12), (1, 1e-5)):
                    pool.wait_ge(var_ready, 2 * t + n + 1)
                    power(rstd[:, n:n + 1], stat[:, n, 7:8], eps, rstd_ready)
                if t >= T - 2:
                    pool.wait_ge(svar_ready, t - T + 3)
                    power(sums[:, 2, :], sums[:, 1, :], 1e-8, srstd_ready)
            pool.wait_ge(d_mask, 16)
            pool.wait_ge(d_bias, 16)
            link(pool.tensor_scalar(mask_f[:, :], mask[:, :], MASKED_SCORE, None, ALU.mult))
            for hg in range(HG):
                pool.tensor_tensor(bias[:, hg, :, :], bias[:, hg, :, :], by_sample(mask_f[:, :]), ALU.add)\
                    .then_inc(bias_ready, 1)

            def norms(n):
                pool.wait_ge(var4_ready, n + 1)
                power(rstd4[:, :], stat4[:, :, 7], 1e-5, rstd4_ready)

            def subtract(hv):
                for hg in range(HG):
                    n = hv * HG + hg
                    pool.wait_ge(smax_ready, n + 1)
                    a = sc[:, hg, hv * BH:(hv + 1) * BH, :]
                    pool.tensor_tensor(a, a, per_sample(smax[:, n, :]), ALU.subtract).then_inc(sub_ready, 1)

            def repeat(hv):
                w = slice(hv * BH, (hv + 1) * BH)
                pool.wait_ge(x3_ready, hv + 1)
                pool.wait_ge(s2_done, (hv + 1) * E * C)
                pool.tensor_copy(x3_rep[:, w, :, :], by_sample(x3_t[:, hv * HALF:(hv + 1) * HALF]).unsqueeze(2)
                                 .broadcast_to([P, BH, J, S])).then_inc(x3_rep_ready, 1)

            norms(0)
            repeat(0)
            norms(1)
            repeat(1)
            subtract(0)
            subtract(1)
            norms(2)
            norms(3)

        @block.scalar
        def _(act):
            act.wait_ge(angles_ready, 1)
            act.activation(trig[:, 0, :], ang[:, 0, :], ACT.Sin).then_inc(trig_ready, 1)
            act.wait_ge(trig_ready, 1)
            act.activation(time_emb[:, :], trig[:, 0, 0:B], ACT.Silu).then_inc(time_ready, 1)
            for t in range(T):
                act.wait_ge(rows_done, t + 1)
                act.activation(rows_tm[:, t, :], bank[4 + t % 2][:, 0:3 * D], ACT.Copy).then_inc(rows_ready, 1)
            b7 = bank[7]
            act.wait_ge(hyp_done, 1)
            act.activation(hyp[0:64, 0, :], b7[0:64, 0:32], ACT.Copy).then_inc(hyp_ready, 1)
            act.wait_ge(hyp_done, 2)
            act.activation(hyp[:, 1, :], b7[:, 32:64], ACT.Relu, bias=col("hyp_b1")).then_inc(hyp_ready, 1)
            act.wait_ge(hyp_done, 3)
            act.activation(hyp[:, 2, :], b7[:, 64:96], ACT.Identity, bias=col("hyp_b2")).then_inc(hyp_ready, 1)
            act.wait_ge(hyp_done, 4)
            act.activation(hyp[0:64, 3, :], b7[0:64, 96:128], ACT.Relu, bias=col("sty_b1", rows=64)).then_inc(hyp_ready, 1)
            for k in range(4):
                w = slice(k * 1024, (k + 1) * 1024)
                act.wait_ge(d_wi[k], 16)
                act.activation(wi_hi[:, w], stage[:, k, :], ACT.Copy).then_inc(wi_hi_ready, 1)
            act.wait_ge(softplus_in, 1)
            act.activation(hyp[:, 5, :], hyp[:, 5, :], ACT.Exp).then_inc(act_link, 1)
            act.wait_ge(act_link, 1)
            act.activation(hyp[:, 5, :], hyp[:, 5, :], ACT.Ln, bias=1.0).then_inc(softplus_ln, 1)
            for k in range(4):
                w = slice(k * 1024, (k + 1) * 1024)
                act.wait_ge(d_wo[k], 16)
                act.activation(wo_hi[:, w], stage[:, k, :], ACT.Copy).then_inc(wo_hi_ready, 1)

            def gelu(t):
                act.wait_ge(h_done, t + 1)
                if t >= 2:
                    act.wait_ge(t_done, t - 1)
                act.activation(gel[:, t % 2, :], bank[H_BANK[t % 2]][:, :], ACT.Gelu).then_inc(gel_ready, 1)

            act.wait_ge(zeroed, 4)
            gelu(0)
            for t in range(T):
                act.wait_ge(t_done, t + 1)
                if t >= 1:
                    act.wait_ge(o_done, t)
                act.activation(diag(hm_hi[:, :, :]), by_chunk(bank[T_BANK[t % 2]][:, :]), ACT.Copy)\
                    .then_inc(hm_hi_ready, 1)
                if t + 1 < T:
                    gelu(t + 1)
                if t >= 4:
                    for p in (2 * t - 8, 2 * t - 7):
                        act.wait_ge(d_w1[p // 2], 16)
                        act.activation(w1_hi[:, p * F:(p + 1) * F], stage[:, p // 2, p % 2 * F:p % 2 * F + F],
                                       ACT.Copy).then_inc(w1_hi_ready, 1)

            def l2(hv):
                c0, c1 = hv * HALF, (hv + 1) * HALF
                act.wait_ge(nt_done, 4 * hv + 4)
                act.wait_ge(h_done, T)
                act.activation(cen[:, c0:c1], bank[NT_BANK[hv]][:, :], ACT.Identity,
                               scale=col("ln_g"), bias=col("ln_b")).then_inc(h_ready, 1)
                act.wait_ge(cen_ready, hv + 1)
                act.activation(sq[:, c0:c1], cen[:, c0:c1], ACT.Square).then_inc(sq_ready, 1)
                act.wait_ge(hf_ready, hv + 1)
                act.activation(hf_hi[:, c0:c1], hf[:, c0:c1], ACT.Copy).then_inc(hf_hi_ready, 1)

            def router_exp(hv):
                act.wait_ge(gates_z, hv + 1)
                act.activation(rt[:, 1, :], rt[:, 0, :], ACT.Exp).then_inc(gates_e, 1)

            def gates_copy(hv):
                act.wait_ge(comb_done, hv + 1)
                act.activation(comb_t[:, hv * HALF:(hv + 1) * HALF], bank[NT_BANK[hv]][0:K2, :], ACT.Copy)\
                    .then_inc(comb_t_ready, 1)

            def relu(q):
                e, c = q // C % E, q % C
                act.wait_ge(s1_done, q + 1)
                if q >= 3:
                    act.wait_ge(gated, q - 2)
                act.activation(act_r[:, q % 3, :], bank[HID_BANK[q % 4]][:, :], ACT.Relu,
                               bias=col("exp_b1", e * C + c)).then_inc(relu_ready, 1)

            def y_copy(hv):
                act.wait_ge(s2_done, (hv + 1) * E * C)
                act.activation(y_t[:, hv * HALF:(hv + 1) * HALF], bank[Y_BANK[hv]][:, :], ACT.Copy).then_inc(y_ready, 1)

            def queries(hv):
                act.wait_ge(q_done, hv + 1)
                if hv == 0:
                    act.wait_ge(d_late, 16)
                    act.wait_ge(s2_done, 2 * E * C)
                    for h4 in range(H4):
                        act.activation(head_b[:, h4:h4 + 1], lt("head", h4, 1), ACT.Copy, scale=col("bq"))\
                            .then_inc(act_link, 1)
                    act.wait_ge(act_link, 1 + H4)
                for h4 in range(H4):
                    ins = act.activation(qx[:, hv * BH:(hv + 1) * BH, h4, :], by_sample(bank[Q_BANK[hv]][:, :]),
                                         ACT.Identity, scale=lt("head", h4, 1), bias=head_b[:, h4:h4 + 1])
                ins.then_inc(qx_ready, 1)

            def exps(hv):
                for hg in range(HG):
                    act.wait_ge(sub_ready, hv * HG + hg + 1)
                    a = sc[:, hg, hv * BH:(hv + 1) * BH, :]
                    act.activation(a, a, ACT.Exp).then_inc(exp_ready, 1)

            def context(hv):
                a = ctx_t[:, hv * HALF:(hv + 1) * HALF]
                act.wait_ge(ctx_div, hv + 1)
                act.activation(a, a, ACT.Identity, bias=col("bv")).then_inc(ctx_ready, 1)

            def h4_scale(hv):
                act.wait_ge(n4_done, hv + 1)
                act.activation(h_t[:, hv * HALF:(hv + 1) * HALF], bank[N4_BANK[hv]][:, :], ACT.Identity,
                               scale=col("g2"), bias=col("beta2")).then_inc(h4_ready, 1)

            def ffn_gelu(hv):
                for c in range(C):
                    act.wait_ge(f1_done, hv * C + c + 1)
                    if hv:
                        act.wait_ge(f2_done, hv)
                    act.activation(ffn_h[:, c, :], bank[F1_BANK[c % 2]][:, :], ACT.Gelu_apprx_sigmoid,
                                   bias=col("ffn_b1", c)).then_inc(ffn_ready, 1)

            l2(0)
            router_exp(0)
            gates_copy(0)
            l2(1)
            for q in range(2 * E * C):
                relu(q)
                if q == 6:
                    router_exp(1)
                if q == 14:
                    gates_copy(1)
                if q == E * C + 3:
                    y_copy(0)
            y_copy(1)
            queries(0)
            queries(1)
            exps(0)
            context(0)
            exps(1)
            context(1)
            h4_scale(0)
            ffn_gelu(0)
            h4_scale(1)
            ffn_gelu(1)

        @block.vector
        def _(dve):
            def link(ins):
                link.n += 1
                ins.then_inc(dve_link, 1)
                dve.wait_ge(dve_link, link.n)
            link.n = 0

            def then(ins, ready, value):
                ins.then_inc(ready, 1)
                dve.wait_ge(ready, value)

            dve.wait_ge(d_ids, 16)
            link(dve.tensor_copy(ids_f[:, :], ids[:, :]))
            dve.wait_ge(d_early, 16)
            link(dve.tensor_scalar(ang[:, 0, 0:B], ids_f[:, 2 * B:3 * B], 0.01, 4000.0, ALU.mult, ALU.mult))
            link(dve.tensor_scalar(ang[:, 0, 0:B], ang[:, 0, 0:B], small("freq"), None, ALU.mult))
            link(dve.tensor_copy(ang[:, 0, B:ANG].rearrange("p (a c) -> p a c", c=2),
                                 small("angles").unsqueeze(2).broadcast_to([P, 2, 2])))
            link(dve.scalar_tensor_tensor(ang[:, 1, :], ang[:, 0, :], TWO_PI_INV, small("turn"), ALU.mult, ALU.add))
            link(dve.tensor_scalar(ang[:, 1, :], ang[:, 1, :], ROUND, -ROUND, ALU.add, ALU.add))
            for part in (TWO_PI_A, TWO_PI_B, TWO_PI_C):
                link(dve.scalar_tensor_tensor(ang[:, 0, :], ang[:, 1, :], -part, ang[:, 0, :], ALU.mult, ALU.add))
            link(dve.tensor_tensor(ang[:, 0, :], ang[:, 0, :], small("quarter"), ALU.add))
            dve.tensor_scalar(ang[:, 0, :], ang[:, 0, :], PI_SAFE, -PI_SAFE, ALU.min, ALU.max).then_inc(angles_ready, 1)
            dve.tensor_scalar(by_sample(onehot[:, :]), per_sample(ids_f[0:K2, 0:B]), small("expert_row", K2), None,
                              ALU.is_equal).then_inc(onehot_ready, 1)
            dve.tensor_scalar(subj[:, :], ids_f[0:B, B:2 * B], small("sample_row", B), None,
                              ALU.is_equal).then_inc(subj_ready, 1)
            dve.tensor_copy(by_sample(of_sample[:, :]), ident[0:B, 0:B].unsqueeze(2).broadcast_to([B, B, S]))\
                .then_inc(of_sample_ready, 1)
            dve.tensor_copy(pick[:, :], small("pick", K2))
            dve.wait_ge(d_table, 16)
            link(dve.tensor_copy(table[:, :], table_raw[:, :]))
            dve.tensor_tensor(table[LO:K2, :], table_raw[LO:K2, :], table[LO:K2, :].bitcast(F32),
                              ALU.subtract).then_inc(table_ready, 1)
            dve.wait_ge(trig_ready, 1)
            sin_cos = trig[0:B, 0, B:ANG].rearrange("p (a c) -> p a c", c=2)
            dve.tensor_copy(rot_row[:, 0:4].rearrange("p (a c) -> p a c", c=2),
                            sin_cos[:, :, 1:2].broadcast_to([B, 2, 2]))
            dve.tensor_copy(rot_row[:, 4:6], sin_cos[:, :, 0])
            dve.tensor_scalar(rot_row[:, 6:8], sin_cos[:, :, 0], -1.0, None, ALU.mult).then_inc(rot_row_ready, 1)

            def masked_x(t):
                src = x_t[:, t * P:(t + 1) * P].rearrange("p (j s) -> p j s", s=S)
                if t >= 2:
                    dve.wait_ge(h_done, t - 1)
                link(dve.tensor_copy(diag(xm_hi[:, t % 2, :]), src))
                dve.tensor_tensor(diag(xm_lo[:, t % 2, :]), src, diag(xm_hi[:, t % 2, :].bitcast(F32)),
                                  ALU.subtract).then_inc(xm_ready, 1)

            def masked_h_lo(t):
                dve.wait_ge(hm_hi_ready, t + 1)
                dve.tensor_tensor(diag(hm_lo[:, :, :]), by_chunk(bank[T_BANK[t % 2]][:, :]),
                                  diag(hm_hi[:, :, :].bitcast(F32)), ALU.subtract).then_inc(hm_lo_ready, 1)

            dve.wait_ge(d_xt, 16)
            dve.wait_ge(zeroed, 4)
            masked_x(0)
            masked_x(1)
            for k in range(4):
                w = slice(k * 1024, (k + 1) * 1024)
                dve.wait_ge(wi_hi_ready, k + 1)
                dve.tensor_tensor(wi_lo[:, w], stage[:, k, :], wi_hi[:, w].bitcast(F32), ALU.subtract)\
                    .then_inc(wi_lo_ready, 1)
                if k == 1:
                    dve.wait_ge(rot_done, 1)
                    dve.tensor_copy(rot_c[:, :, :], bank[6][:, 0:8 * T].rearrange("p (t c) -> p t c", c=8))
                    dve.wait_ge(ada_done, 1)
                    dve.tensor_scalar(affine[:, 2, :], bank[3][:, 0:32], col("b_ada"), 1.0, ALU.add, ALU.add)
                    dve.tensor_scalar(affine[:, 3, :], bank[3][:, 32:64], col("b_ada", 1), None, ALU.add)
                if k == 2:
                    dve.wait_ge(hyp_done, 5)
                    link(dve.tensor_scalar(hyp[:, 4, :], bank[7][:, 128:160], col("sty_b2"), None, ALU.add))
                    dve.scalar_tensor_tensor(hyp[:, 5, :], hyp[:, 4, :], -1.0, hyp[:, 4, :], ALU.mult, ALU.min)\
                        .then_inc(softplus_in, 1)
                    dve.tensor_scalar(affine[:, 1, :], bank[7][:, 160:192], col("sty_b2", 1), None, ALU.add)
            dve.wait_ge(softplus_ln, 1)
            link(dve.scalar_tensor_tensor(affine[:, 0, :], hyp[:, 4, :], 0.0, hyp[:, 5, :], ALU.max, ALU.add))
            link(dve.tensor_scalar(affine[:, 0, :], affine[:, 0, :], 1e-8, None, ALU.add))

            def normalise(out, in_, n, done, ready):
                link(dve.bn_stats(stat[:, n, 0:6], in_))
                dve.bn_aggr(stat[:, n, 6:8], stat[:, n, 0:6]).then_inc(var_ready, 1)
                dve.wait_ge(var_ready, done)
                dve.wait_ge(rstd_ready, done)
                ins = dve.tensor_scalar(out, in_, stat[:, n, 6:7], rstd[:, n:n + 1], ALU.subtract, ALU.mult)
                if ready is None:
                    link(ins)
                else:
                    ins.then_inc(ready, 1)

            def tail(t):
                dve.wait_ge(o_done, t + 1)
                dve.wait_ge(xbo_ready, t + 1)
                then(dve.tensor_tensor(row[:, :], bank[O_BANK[t % 2]][:, 0:D], x_tm[:, t, :], ALU.add), o_read, t + 1)
                normalise(row[:, :], row[:, :], 0, 2 * t + 1, None)
                link(dve.tensor_tensor(row[:, :], row[:, :], rows_tm[:, t, D:2 * D], ALU.mult))
                link(dve.tensor_tensor(row[:, :], row[:, :], rows_tm[:, t, 2 * D:3 * D], ALU.add))
                quads = row[:, :].rearrange("p (g c) -> p g c", c=4)
                pairs = row[:, :].rearrange("p (g a i) -> p g a i", a=2, i=2)
                swapped = turned[:, :].rearrange("p (g a i) -> p g a i", a=2, i=2)
                rot = rot_tm[:, t, :]
                dve.tensor_tensor(rot.rearrange("p (g c) -> p g c", c=4), quads,
                                  rot_c[:, t, 0:4].unsqueeze(1).broadcast_to([P, D // 4, 4]), ALU.mult)
                for i, k in ((0, 4), (1, 6)):
                    ins = dve.tensor_tensor(swapped[:, :, :, i], pairs[:, :, :, 1 - i],
                                            rot_c[:, t, k:k + 2].unsqueeze(1).broadcast_to([P, D // 4, 2]), ALU.mult)
                link(ins)
                link(dve.tensor_tensor(rot, rot, turned[:, :], ALU.add))
                normalise(nrm_tm[:, t, :], rot, 1, 2 * t + 2, nrm_ready)

            def l2(hv):
                c0, c1 = hv * HALF, (hv + 1) * HALF
                b0, b1 = hv * BH, (hv + 1) * BH
                h = by_sample(cen[:, c0:c1])
                out = by_sample(hf[:, c0:c1])
                dve.wait_ge(h_ready, hv + 1)
                link(dve.tensor_reduce(sums[:, 0, :], h, AX.X, ALU.add))
                dve.scalar_tensor_tensor(h, per_sample(sums[:, 0, :]), -1.0 / S, h, ALU.mult, ALU.add)\
                    .then_inc(cen_ready, 1)
                dve.wait_ge(sq_ready, hv + 1)
                link(dve.tensor_reduce(sums[:, 1, :], by_sample(sq[:, c0:c1]), AX.X, ALU.add))
                dve.tensor_scalar(sums[:, 1, :], sums[:, 1, :], 1.0 / S, None, ALU.mult).then_inc(svar_ready, 1)
                dve.wait_ge(srstd_ready, hv + 1)
                link(dve.tensor_tensor(sums[:, 2, :], sums[:, 2, :], affine[:, 0, b0:b1], ALU.mult))
                link(dve.tensor_tensor(out, h, per_sample(sums[:, 2, :]), ALU.mult))
                dve.tensor_tensor(out, out, per_sample(affine[:, 1, b0:b1]), ALU.add).then_inc(hf_ready, 1)

            def l2_lo(hv):
                c0, c1 = hv * HALF, (hv + 1) * HALF
                dve.wait_ge(hf_hi_ready, hv + 1)
                dve.tensor_tensor(hf_lo[:, c0:c1], hf[:, c0:c1], hf_hi[:, c0:c1].bitcast(F32), ALU.subtract)\
                    .then_inc(hf_lo_ready, 1)

            def router(hv):
                def v(i):
                    return rt[:, i, :].rearrange("p (t e) -> p t e", e=E)

                def s(i):
                    return rt_s[:, i, :]

                def wide(i):
                    return s(i).unsqueeze(2).broadcast_to([P, 4, E])

                prefer = small("prefer").unsqueeze(1).broadcast_to([P, 4, E])
                logits = bank[NT_BANK[hv]][:, 0:4 * E].rearrange("p (t e) -> p t e", e=E)
                dve.wait_ge(logits_done, hv + 1)
                link(dve.tensor_reduce(s(0), logits, AX.X, ALU.max))
                dve.tensor_tensor(v(0), logits, wide(0), ALU.subtract).then_inc(gates_z, 1)
                dve.wait_ge(gates_e, hv + 1)
                link(dve.tensor_reduce(s(1), v(1), AX.X, ALU.add))
                link(dve.reciprocal(s(1), s(1)))
                link(dve.tensor_tensor(v(2), v(1), wide(1), ALU.mult))

                def first_max(probs, largest, chosen):
                    link(dve.tensor_reduce(s(largest), v(probs), AX.X, ALU.max))
                    link(dve.tensor_tensor(v(chosen), v(probs), wide(largest), ALU.is_equal))
                    link(dve.tensor_tensor(v(chosen), v(chosen), prefer, ALU.mult))
                    link(dve.tensor_reduce(s(7), v(chosen), AX.X, ALU.max))
                    link(dve.tensor_tensor(v(chosen), v(chosen), wide(7), ALU.is_equal))

                first_max(2, 2, 3)
                link(dve.scalar_tensor_tensor(v(5), v(3), -2.0, v(2), ALU.mult, ALU.add))
                first_max(5, 4, 6)
                link(dve.tensor_tensor(v(3), v(3), v(6), ALU.add))
                link(dve.tensor_tensor(s(6), s(2), s(4), ALU.add))
                link(dve.reciprocal(s(6), s(6)))
                link(dve.tensor_tensor(v(3), v(3), v(2), ALU.mult))
                link(dve.tensor_tensor(v(3), v(3), wide(6), ALU.mult))
                link(dve.tensor_copy(comb_hi[:, :], rt[:, 3, :]))
                hi = comb_hi[:, :].bitcast(F32).rearrange("p (t e) -> p t e", e=E)
                if hv:
                    dve.wait_ge(comb_done, hv)
                dve.tensor_copy(comb_hl[:, :, 0:E], hi)
                dve.tensor_tensor(comb_hl[:, :, LO:K2], v(3), hi, ALU.subtract).then_inc(comb_ready, 1)

            masked_h_lo(0)
            masked_x(2)
            for t in range(1, T):
                masked_h_lo(t)
                if t + 2 < T:
                    masked_x(t + 2)
                tail(t - 1)
            l2(0)
            tail(T - 1)
            l2_lo(0)
            dve.wait_ge(w1_lo_ready, E)
            link(dve.memset(comb_hl[:, :, :], 0.0))
            router(0)
            l2(1)
            l2_lo(1)

            def gate(q):
                dve.wait_ge(relu_ready, q + 1)
                dve.wait_ge(combb_done, q // C + 1)
                if q >= 3:
                    dve.wait_ge(s2_done, q - 2)
                dve.tensor_tensor(act_g[:, q % 3, :], act_r[:, q % 3, :], bank[GATE_BANK[q // C % 2]][:, :],
                                  ALU.mult).then_inc(gated, 1)

            def norm4(rows, n, after):
                hv = n % 2
                for i in range(4):
                    ins = dve.bn_stats(stat4[:, i, 0:6], rows[:, i, :])
                link(ins)
                for i in range(4):
                    ins = dve.bn_aggr(stat4[:, i, 6:8], stat4[:, i, 0:6])
                then(ins, var4_ready, n + 1)
                after()
                dve.wait_ge(rstd4_ready, n + 1)
                for i in range(4):
                    dve.tensor_scalar(nrm_tm[:, 4 * hv + i, :], rows[:, i, :], stat4[:, i, 6:7], rstd4[:, i:i + 1],
                                      ALU.subtract, ALU.mult).then_inc(nrm_ready, 1)

            def l3_start(hv):
                rows = rot_tm[:, 4 * hv:4 * hv + 4, :]
                dve.wait_ge(ytm_done, hv + 1)
                link(dve.tensor_tensor(rows, rows, by_tile(bank[YTM_BANK[hv]][:, :]), ALU.add))
                norm4(rows, hv, lambda: None)

            def x3(hv):
                out = by_sample(x3_t[:, hv * HALF:(hv + 1) * HALF])
                b0, b1 = hv * BH, (hv + 1) * BH
                dve.wait_ge(nt3_done, hv + 1)
                link(dve.tensor_tensor(out, by_sample(bank[N3_BANK[hv]][:, :]), per_sample(affine[:, 2, b0:b1]), ALU.mult))
                dve.tensor_tensor(out, out, per_sample(affine[:, 3, b0:b1]), ALU.add).then_inc(x3_ready, 1)

            def keys(hv):
                dve.wait_ge(k_done, hv + 1)
                dve.tensor_scalar(k_t[:, hv * HALF:(hv + 1) * HALF], bank[K_BANK[hv]][:, :], col("bk"), None, ALU.add)\
                    .then_inc(k_ready, 1)

            def values(hv):
                for i in range(4):
                    b = hv * BH + 4 * i
                    dve.wait_ge(v_done, 4 * hv + i + 1)
                    dve.tensor_tensor(vb[:, b:b + 4, :], by_tile(bank[V_BANK[hv][i % 2]][:, :]),
                                      lt("block").unsqueeze(1).broadcast_to([P, 4, P]), ALU.mult).then_inc(v_ready, 1)

            def scores(hv):
                for hg in range(HG):
                    n = hv * HG + hg
                    a = sc[:, hg, hv * BH:(hv + 1) * BH, :]
                    dve.wait_ge(score_done, n + 1)
                    dve.wait_ge(bias_ready, hg + 1)
                    then(dve.tensor_tensor(a, by_sample(bank[SCORE_BANK[hg]][:, :]), bias[:, hg, hv * BH:(hv + 1) * BH, :],
                                           ALU.add), score_read, n + 1)
                    dve.tensor_reduce(smax[:, n, :], a, AX.X, ALU.max).then_inc(smax_ready, 1)

            def transposed(hv):
                for hg in range(HG):
                    w = slice(hv * BH, (hv + 1) * BH)
                    dve.wait_ge(exp_ready, hv * HG + hg + 1)
                    dve.transpose(pt[:, hg, w, :], sc[:, hg, w, :]).then_inc(pt_ready, 1)

            def divide(hv):
                dve.wait_ge(ctx_done, hv + 1)
                link(dve.reciprocal(rsum[:, :], bank[SUM_BANK[hv]][:, :]))
                dve.tensor_tensor(ctx_t[:, hv * HALF:(hv + 1) * HALF], bank[CTX_BANK[hv]][:, :], rsum[:, :], ALU.mult)\
                    .then_inc(ctx_div, 1)

            def x4(hv):
                w = slice(hv * HALF, (hv + 1) * HALF)
                dve.wait_ge(wo_done, hv + 1)
                dve.scalar_tensor_tensor(x4_t[:, w], bank[WO_BANK[hv]][:, :], col("bo"), x3_t[:, w], ALU.add, ALU.add)\
                    .then_inc(x4_ready, 1)

            def x4_norm(hv):
                rows = by_tile(bank[X4_BANK[hv]][:, :])
                dve.wait_ge(x4tm_done, hv + 1)
                norm4(rows, 2 + hv, lambda: dve.tensor_tensor(
                    x4_tm[:, 4 * hv:4 * hv + 4, :], rows, lt("b2").unsqueeze(1).broadcast_to([P, 4, P]), ALU.add)
                    .then_inc(x4_tm_ready, 1))

            def outputs(hv):
                w = slice(4 * hv, 4 * hv + 4)
                dve.wait_ge(f2_done, hv + 1)
                dve.tensor_tensor(out_tm[:, w, :], by_tile(bank[F2_BANK[hv]][:, :]), x4_tm[:, w, :], ALU.add)\
                    .then_inc(out_ready, 1)

            for q in range(2 * E * C):
                gate(q)
                if q == 4:
                    router(1)
                if q == E * C + 7:
                    l3_start(0)
                if q == E * C + 14:
                    x3(0)
            keys(0)
            l3_start(1)
            values(0)
            scores(0)
            x3(1)
            keys(1)
            values(1)
            transposed(0)
            divide(0)
            scores(1)
            x4(0)
            transposed(1)
            x4_norm(0)
            divide(1)
            x4(1)
            x4_norm(1)
            outputs(0)
            outputs(1)

        @block.tensor
        def _(pe):
            def mm(out, lhsT, rhs, start=True, stop=True):
                return pe.matmul(out, lhsT, rhs, start=start, stop=stop)

            def product(out, w_hi, w_lo, m_hi, m_lo, start, stop):
                mm(out, w_hi, m_hi, start, False)
                mm(out, w_hi, m_lo, False, False)
                return mm(out, w_lo, m_hi, False, stop)

            pe.wait_ge(onehot_ready, 1)
            pe.wait_ge(table_ready, 1)
            for t in range(T):
                if t >= 2:
                    pe.wait_ge(rows_ready, t - 1)
                mm(bank[4 + t % 2][:, 0:3 * D], onehot[:, t * P:(t + 1) * P], table[:, F:TABLE]).then_inc(rows_done, 1)
            b7 = bank[7]
            pe.wait_ge(d_early, 16)
            pe.wait_ge(subj_ready, 1)
            mm(b7[0:64, 0:32], small("subj_emb", B), subj[:, :]).then_inc(hyp_done, 1)
            pe.wait_ge(rot_row_ready, 1)
            pe.wait_ge(of_sample_ready, 1)
            for t in range(T):
                ins = mm(bank[6][:, 8 * t:8 * t + 8],
                         of_sample[:, t * P:(t + 1) * P], rot_row[:, :])
            ins.then_inc(rot_done, 1)
            pe.wait_ge(hyp_ready, 1)
            mm(b7[:, 32:64], small("hyp_w1", 64), hyp[0:64, 0, :]).then_inc(hyp_done, 1)
            pe.wait_ge(time_ready, 1)
            mm(bank[3][:, 0:32], small("w_ada", k=0, n=P), time_emb[:, :])
            mm(bank[3][:, 32:64], small("w_ada", k=P, n=P), time_emb[:, :]).then_inc(ada_done, 1)
            pe.wait_ge(hyp_ready, 2)
            mm(b7[:, 64:96], small("hyp_w2"), hyp[:, 1, :]).then_inc(hyp_done, 1)
            pe.wait_ge(hyp_ready, 3)
            mm(b7[0:64, 96:128], small("sty_w1"), hyp[:, 2, :]).then_inc(hyp_done, 1)
            pe.wait_ge(hyp_ready, 4)
            mm(b7[:, 128:160], small("sty_w2", 64, 0, P), hyp[0:64, 3, :])
            mm(b7[:, 160:192], small("sty_w2", 64, P, P), hyp[0:64, 3, :]).then_inc(hyp_done, 1)

            def experts(t):
                return [pe.value_load(ids[0:1, J * t + j:J * t + j + 1], min_val=0, max_val=E - 1) for j in range(J)]

            def l0_up(t):
                pe.wait_ge(xm_ready, t + 1)
                pe.wait_ge(wi_lo_ready, 4)
                if t >= 2:
                    pe.wait_ge(gel_ready, t - 1)
                out = bank[H_BANK[t % 2]][:, :]
                mm(out, onehot[:, t * P:(t + 1) * P], table[:, 0:F], True, False)
                for j, e in enumerate(experts(t)):
                    own = slice(j * P, (j + 1) * P)
                    ins = product(out, xm_hi[:, t % 2, own], xm_lo[:, t % 2, own],
                                  wi_hi[:, bass.ds(e * F, F)], wi_lo[:, bass.ds(e * F, F)], False, j == J - 1)
                ins.then_inc(h_done, 1)

            def l0_turn(t):
                pe.wait_ge(gel_ready, t + 1)
                if t >= 2:
                    pe.wait_ge(hm_lo_ready, t - 1)
                for c in range(C):
                    ins = pe.transpose(bank[T_BANK[t % 2]][:, c * P:(c + 1) * P], gel[:, t % 2, c * P:(c + 1) * P], ident)
                ins.then_inc(t_done, 1)

            def l0_down(t):
                pe.wait_ge(hm_lo_ready, t + 1)
                pe.wait_ge(wo_lo_ready, 4)
                if t < 2:
                    pe.wait_ge(rows_ready, T)
                else:
                    pe.wait_ge(o_read, t - 1)
                for j, e in enumerate(experts(t)):
                    own = slice(j * P, (j + 1) * P)
                    for c in range(C):
                        w = bass.ds(e * F + c * P, P)
                        ins = product(bank[O_BANK[t % 2]][:, 0:D], hm_hi[:, c, own], hm_lo[:, c, own],
                                      wo_hi[:, w], wo_lo[:, w], j == 0 and c == 0, j == J - 1 and c == C - 1)
                ins.then_inc(o_done, 1)

            def l2_turn(t):
                pe.wait_ge(nrm_ready, t + 1)
                pe.transpose(bank[NT_BANK[t // 4]][:, t % 4 * P:t % 4 * P + P], nrm_tm[:, t, :], ident)\
                    .then_inc(nt_done, 1)

            def logits(hv):
                pe.wait_ge(hf_ready, hv + 1)
                for i in range(4):
                    t = 4 * hv + i
                    ins = mm(bank[NT_BANK[hv]][:, i * E:(i + 1) * E], hf[:, t * P:(t + 1) * P], small("router_w"))
                ins.then_inc(logits_done, 1)

            def gates_turn(hv):
                pe.wait_ge(comb_ready, hv + 1)
                for i in range(4):
                    ins = pe.transpose(bank[NT_BANK[hv]][0:K2, i * P:(i + 1) * P], comb_hl[:, i, :], ident)
                ins.then_inc(comb_done, 1)

            def gates_wide(n):
                hv, e = divmod(n, E)
                pe.wait_ge(comb_t_ready, hv + 1)
                if n >= 2:
                    pe.wait_ge(gated, (n - 1) * C)
                mm(bank[GATE_BANK[n % 2]][:, :], pick[:, e:e + 1].broadcast_to([K2, P]),
                   comb_t[:, hv * HALF:(hv + 1) * HALF]).then_inc(combb_done, 1)

            def y_bias(hv):
                mm(bank[Y_BANK[hv]][:, :], small("exp_b2", K2), comb_t[:, hv * HALF:(hv + 1) * HALF].bitcast(F32),
                   True, False)

            def moe_up(q):
                hv, e, c = q // C // E, q // C % E, q % C
                w, x = slice(e * F + c * P, e * F + (c + 1) * P), slice(hv * HALF, (hv + 1) * HALF)
                pe.wait_ge(hf_lo_ready, hv + 1)
                pe.wait_ge(w1_lo_ready, e + 1)
                if q >= 4:
                    pe.wait_ge(relu_ready, q - 3)
                product(bank[HID_BANK[q % 4]][:, :], w1_hi[:, w], w1_lo[:, w], hf_hi[:, x], hf_lo[:, x], True, True)\
                    .then_inc(s1_done, 1)

            def moe_down(q):
                hv, e, c = q // C // E, q // C % E, q % C
                pe.wait_ge(gated, q + 1)
                last = e == E - 1 and c == C - 1
                ins = mm(bank[Y_BANK[hv]][:, :], w2[:, e * F + c * P:e * F + (c + 1) * P], act_g[:, q % 3, :],
                         False, last)
                ins.then_inc(s2_done, 1)

            def y_turn(hv):
                pe.wait_ge(y_ready, hv + 1)
                for i in range(4):
                    t = 4 * hv + i
                    ins = pe.transpose(bank[YTM_BANK[hv]][:, i * P:(i + 1) * P], y_t[:, t * P:(t + 1) * P], ident)
                ins.then_inc(ytm_done, 1)

            def n3_turn(hv):
                pe.wait_ge(nrm_ready, T + 4 * hv + 4)
                for i in range(4):
                    ins = pe.transpose(bank[N3_BANK[hv]][:, i * P:(i + 1) * P], nrm_tm[:, 4 * hv + i, :], ident)
                ins.then_inc(nt3_done, 1)

            def qk(hv):
                x = x3_t[:, hv * HALF:(hv + 1) * HALF]
                pe.wait_ge(x3_ready, hv + 1)
                mm(bank[Q_BANK[hv]][:, :], lt("wq"), x).then_inc(q_done, 1)
                if hv:
                    pe.wait_ge(qx_ready, 1)
                mm(bank[K_BANK[hv]][:, :], lt("wk"), x).then_inc(k_done, 1)

            def values(hv):
                pe.wait_ge(x3_rep_ready, hv + 1)
                for i in range(4):
                    if i >= 2:
                        pe.wait_ge(v_ready, 4 * hv + i - 1)
                    elif hv:
                        pe.wait_ge(v_ready, 4)
                        pe.wait_ge(k_ready, 1)
                    for k in range(4):
                        b = hv * BH + 4 * i + k
                        ins = mm(bank[V_BANK[hv][i % 2]][:, k * P:(k + 1) * P],
                                 x3_rep[:, b, :, :], lt("wv"))
                    ins.then_inc(v_done, 1)

            def scores(hv):
                pe.wait_ge(qx_ready, hv + 1)
                pe.wait_ge(k_ready, hv + 1)
                for hg in range(HG):
                    if hv:
                        pe.wait_ge(score_read, hg + 1)
                    elif hg == 3:
                        pe.wait_ge(v_ready, 4)
                    f = slice(hg * 32, hg * 32 + 32)
                    for i in range(BH):
                        b = hv * BH + i
                        ins = mm(bank[SCORE_BANK[hg]][:, i * S:(i + 1) * S], qx[f, b, :, :], k_t[f, b * S:(b + 1) * S])
                    ins.then_inc(score_done, 1)

            def context(hv):
                pe.wait_ge(v_ready, 8)
                if hv:
                    pe.wait_ge(ctx_div, hv)
                for hg in range(HG):
                    f = slice(hg * 32, hg * 32 + 32)
                    pe.wait_ge(pt_ready, hv * HG + hg + 1)
                    for i in range(BH):
                        b = hv * BH + i
                        mm(bank[CTX_BANK[hv]][f, i * S:(i + 1) * S], vb[:, b, f], pt[:, hg, b, :])
                    ins = mm(bank[SUM_BANK[hv]][f, :], lt("block", 0, 32), pt[:, hg, hv * BH:(hv + 1) * BH, :])
                ins.then_inc(ctx_done, 1)

            def project(hv):
                pe.wait_ge(ctx_ready, hv + 1)
                pe.wait_ge(qx_ready, 2)
                if hv:
                    pe.wait_ge(score_read, 8)
                mm(bank[WO_BANK[hv]][:, :], lt("wo"), ctx_t[:, hv * HALF:(hv + 1) * HALF]).then_inc(wo_done, 1)

            def x4_turn(hv):
                pe.wait_ge(x4_ready, hv + 1)
                for i in range(4):
                    t = 4 * hv + i
                    ins = pe.transpose(bank[X4_BANK[hv]][:, i * P:(i + 1) * P], x4_t[:, t * P:(t + 1) * P], ident)
                ins.then_inc(x4tm_done, 1)

            def n4_turn(hv):
                pe.wait_ge(nrm_ready, 2 * T + 4 * hv + 4)
                for i in range(4):
                    ins = pe.transpose(bank[N4_BANK[hv]][:, i * P:(i + 1) * P], nrm_tm[:, 4 * hv + i, :], ident)
                ins.then_inc(n4_done, 1)

            def ffn_up(hv):
                pe.wait_ge(h4_ready, hv + 1)
                for c in range(C):
                    n = hv * C + c
                    if n >= 2:
                        pe.wait_ge(ffn_ready, n - 1)
                    else:
                        pe.wait_ge(score_read, 8)
                    mm(bank[F1_BANK[c % 2]][:, :], lt("w1", c * P, P), h_t[:, hv * HALF:(hv + 1) * HALF]).then_inc(f1_done, 1)

            def ffn_down(hv):
                pe.wait_ge(ffn_ready, hv * C + C)
                pe.wait_ge(x4_tm_ready if hv == 0 else h4_ready, 1)
                for i in range(4):
                    for c in range(C):
                        ins = mm(bank[F2_BANK[hv]][:, i * P:(i + 1) * P], ffn_h[:, c, i * P:(i + 1) * P],
                                 lt("w2", c * P, P), c == 0, c == C - 1)
                ins.then_inc(f2_done, 1)

            pe.wait_ge(zeroed, 4)
            l0_up(0)
            for t in range(T):
                l0_turn(t)
                if t + 1 < T:
                    l0_up(t + 1)
                if t >= 2:
                    l2_turn(t - 2)
                l0_down(t)
            l2_turn(T - 2)
            logits(0)
            l2_turn(T - 1)
            gates_turn(0)
            pe.wait_ge(comb_t_ready, 1)
            y_bias(0)
            pe.wait_ge(d_w2, 16)
            LAG = 2
            for q in range(2 * E * C + LAG):
                if q < 2 * E * C:
                    if q % C == 0:
                        gates_wide(q // C)
                    if q == E * C:
                        y_bias(1)
                    moe_up(q)
                if q >= LAG:
                    moe_down(q - LAG)
                if q == 2:
                    logits(1)
                if q == 12:
                    gates_turn(1)
                if q == E * C + 5:
                    y_turn(0)
                if q == E * C + 11:
                    n3_turn(0)
            qk(0)
            y_turn(1)
            values(0)
            scores(0)
            n3_turn(1)
            qk(1)
            values(1)
            context(0)
            scores(1)
            project(0)
            x4_turn(0)
            context(1)
            n4_turn(0)
            ffn_up(0)
            project(1)
            x4_turn(1)
            ffn_down(0)
            n4_turn(1)
            ffn_up(1)
            ffn_down(1)


def laid_out(i):
    f32 = np.float32

    def columns(parts, layout_of, width, rows=P):
        a = np.zeros((rows, width), f32)
        for name, v in parts.items():
            lo, hi = layout_of[name]
            a[:v.shape[0], lo:hi] = v
        return a

    def vectors(*arrays):
        out = []
        for v in arrays:
            v = v.reshape(-1, min(v.shape[-1], P)).T
            out.append(np.concatenate([v, np.zeros((P - v.shape[0], v.shape[1]), f32)]))
        return np.concatenate(out, axis=1)

    def chunked(w):
        w = w.reshape(-1, C, P, D)
        return np.ascontiguousarray(w.transpose(2, 0, 1, 3).reshape(P, -1))

    x = np.asarray(i["x"]).reshape(N, D)
    row = np.arange(P)
    expert_row = np.where(row < E, row, np.where((row >= LO) & (row < K2), row - LO, -1))
    half = D // 2
    freqs = np.exp(np.arange(half, dtype=f32) * f32(-np.log(10000.0) / (half - 1)))
    turn = np.zeros((P, ANG), f32)
    turn[half:, :B] = 0.25
    turn[:, B + 1::2] = 0.25
    exp_b2 = np.zeros((K2, P), f32)
    exp_b2[0:E] = exp_b2[LO:K2] = i["L2_cond_exp_b2"]
    early = columns({
        "ident": np.eye(P, dtype=f32), "expert_row": expert_row[:, None], "sample_row": row[:, None],
        "freq": np.concatenate([freqs, freqs])[:, None], "turn": turn, "quarter": (turn * 4 * (np.pi / 2)).astype(f32),
        "prefer": np.tile(E - np.arange(E), (P, 1)), "pick": (expert_row[:, None] == np.arange(E)),
        "angles": np.stack([i["condB_theta"], i["condB_phi"]], axis=1),
        "cols": vectors(i["L2_cond_exp_b1"], i["L3_cond_b1"], i["L2_cond_ln_g"], i["L2_cond_ln_b"],
                        i["L2_cond_hyp_b1"], i["L2_cond_hyp_b2"], i["L2_cond_sty_b1"], i["L2_cond_sty_b2"],
                        i["L3_cond_b_ada"], i["L3_cond_bq"], i["L3_cond_bk"], i["L3_cond_bv"], i["L3_cond_bo"],
                        i["L3_cond_g2"], i["L3_cond_beta2"]),
        "subj_emb": i["L2_cond_subj_emb"], "hyp_w1": i["L2_cond_hyp_w1"], "hyp_w2": i["L2_cond_hyp_w2"],
        "sty_w1": i["L2_cond_sty_w1"], "sty_w2": i["L2_cond_sty_w2"], "w_ada": i["L3_cond_W_ada"],
        "router_w": i["L2_cond_router_w"], "exp_b2": exp_b2}, EARLY, EARLY_W)
    head = (row[:, None] % 32 // DH == np.arange(H4)) * f32(1.0 / np.sqrt(DH))
    block = np.tile(row[:, None] // 32 == np.arange(32) // DH, (1, HG))
    late = columns({
        "head": head, "block": block, "wq": i["L3_cond_Wq"], "wk": i["L3_cond_Wk"], "wv": i["L3_cond_Wv"],
        "wo": i["L3_cond_Wo"], "w1": i["L3_cond_W1"], "w2": chunked(i["L3_cond_W2"]),
        "b2": np.tile(i["L3_cond_b2"], (P, 1))}, LATE, LATE_W)
    tables = np.zeros((K2, TABLE), f32)
    tables[0:E] = tables[LO:K2] = np.concatenate(
        [i["L0_cond_bi"], i["L0_cond_bo"], i["L0_cond_gamma"], i["L0_cond_beta"]], axis=1)
    ids = np.concatenate([i["itok_B_0_7"], i["itok_B_6_14"], i["itok_B_34_63"]]).astype(np.int32)
    wide = lambda w: np.ascontiguousarray(w.transpose(1, 0, 2).reshape(P, -1))
    return {
        "x_tm": np.ascontiguousarray(x.reshape(T, P, D).transpose(1, 0, 2)), "x_t": np.ascontiguousarray(x.T),
        "ids": np.tile(ids, (P, 1)), "early": early, "late": late, "tables": tables,
        "wi": wide(i["L0_cond_Wi"]), "wo": chunked(i["L0_cond_Wo"]),
        "w1": wide(i["L2_cond_exp_w1"]), "w2": chunked(i["L2_cond_exp_w2"]),
        "fside": np.ascontiguousarray(i["fside_Bx16xSxS_0"].reshape(B, HG, H4, S, S).transpose(2, 3, 1, 0, 4)
                                      .reshape(P, HG, B, S)),
        "mask": np.tile(i["mask_Bx1xSxS_bk0"].reshape(B, S, S).transpose(1, 0, 2).reshape(S, B * S), (H4, 1)),
    }


def kernel(**inputs):
    import concourse.bacc as bacc
    from concourse.bass_utils import run_bass_kernel_spmd

    nc = bacc.Bacc("TRN2", target_bir_lowering=False, num_devices=1)
    arrays = laid_out({k: np.asarray(v) for k, v in inputs.items()})
    args = [nc.dram_tensor(f"in_{k}", a.shape, mybir.dt.from_np(a.dtype), kind="ExternalInput").ap()
            for k, a in arrays.items()]
    out = nc.dram_tensor("out", (P, T, D), F32, kind="ExternalOutput").ap()
    build(nc, *args, out)
    r = run_bass_kernel_spmd(nc, [{f"in_{k}": a for k, a in arrays.items()}], core_ids=[0])
    got = r.results[0]["out"]
    return got.transpose(1, 0, 2).reshape(B, S, D)
```

```python
from contextlib import ExitStack

import concourse.bass as bass
import numpy as np
from concourse import mybir

F32 = mybir.dt.float32
F32R = mybir.dt.float32r
I32 = mybir.dt.int32
U8 = mybir.dt.uint8
ACT = mybir.ActivationFunctionType
ALU = mybir.AluOpType
AX = mybir.AxisListType

P = 128
B, S, D = 32, 32, 128
N = B * S
T = N // P
J = P // S
E = 8
F = 512
C = F // P
H, DH = 16, 8
HG, H4 = 4, 4
HALF = N // 2
BH = B // 2
BANK = 512
LO = 32
K2 = LO + E
MASKED = P + S
TWO_PI_INV = float(np.float32(1.0 / (2.0 * np.pi)))
TWO_PI_A = 6.28125
TWO_PI_B = 0.0019350051879882812
TWO_PI_C = float(2.0 * np.pi - 6.28125 - 0.0019350051879882812)
ROUND = 12582912.0
MASKED_SCORE = -1.0e38
PI_SAFE = 3.1415925



def layout(parts):
    at, out = 0, {}
    for name, width in parts:
        out[name] = (at, at + width)
        at += width
    return out, at


COLS, NCOLS = layout([
    ("exp_b1", E * C), ("ffn_b1", C), ("ln_g", 1), ("ln_b", 1), ("hyp_b1", 1), ("hyp_b2", 1), ("sty_b1", 1),
    ("sty_b2", 2), ("b_ada", 2), ("bq", 1), ("bk", 1), ("bv", 1), ("bo", 1), ("g2", 1), ("beta2", 1)])
ANG = B + 4
EARLY, EARLY_W = layout([
    ("ident", P), ("expert_row", 1), ("sample_row", 1), ("freq", 1), ("turn", ANG), ("quarter", ANG),
    ("prefer", E), ("pick", E), ("angles", 2), ("cols", NCOLS), ("subj_emb", 64), ("hyp_w1", P), ("hyp_w2", P),
    ("sty_w1", 64), ("sty_w2", 2 * P), ("w_ada", 2 * P), ("router_w", E), ("exp_b2", P)])
LATE, LATE_W = layout([
    ("head", H4), ("block", P), ("wq", P), ("wk", P), ("wv", P), ("wo", P), ("w1", F), ("w2", F), ("b2", P)])
TABLE = F + 4 * D


def build(nc, x_tm_d, x_t_d, ids_d, early_d, late_d, tables_d, wi_d, wo_d, w1_d, w2_d, fside_d, mask_d, out_d):
    ctx = ExitStack()
    with ctx:
        free = [(nc.sbuf_base + 63) // 64 * 64]

        def sb(name, shape, dt=F32, at=None):
            size = (int(np.prod(shape[1:])) * (1 if dt == U8 else 4) + 31) // 32 * 32
            region = free if at is None else at
            offset, region[0] = region[0], region[0] + size
            return nc.alloc_sbuf_tensor_at(name, shape, dt, offset=offset)

        def sem(name):
            return ctx.enter_context(nc.semaphore(name))

        early = sb("early", [P, EARLY_W])
        ids = sb("ids", [P, 3 * B], I32)
        ids_f = sb("ids_f", [P, 3 * B])
        region_x = [free[0]]
        x_t = sb("x_t", [P, N])
        rows_tm = sb("rows_tm", [P, T, D])
        nrm_tm = sb("nrm_tm", [P, T, D])
        affine = sb("affine", [P, 4, B])
        stat = sb("stat", [P, 2, 8])
        rstd = sb("rstd", [P, 2])
        stat4 = sb("stat4", [P, 4, 8])
        rstd4 = sb("rstd4", [P, 4])
        sums = sb("sums", [P, 3, BH])
        token_veps = sb("token_veps", [P, BH])
        veps, minus_half = sb("veps", [P, BH]), sb("minus_half", [P, BH])
        hf = sb("hf", [P, HALF])
        hf_hi = sb("hf_hi", [P, N], F32R)
        hf_lo = sb("hf_lo", [P, N], F32R)
        comb_t = sb("comb_t", [K2, N], F32R)
        rt = sb("rt", [P, 7, HALF // P * E])
        rt_s = sb("rt_s", [P, 8, HALF // P])
        comb_hl = sb("comb_hl", [P, HALF // P, K2])
        comb_hi = sb("comb_hi", [P, HALF // P * E], F32R)
        region_a = [free[0]]
        wi_hi = sb("wi_hi", [P, E * F], F32R)
        wi_lo = sb("wi_lo", [P, E * F], F32R)
        region_b = [free[0]]
        wo_hl = sb("wo_hl", [P, E * C, 2, P], F32R)
        region_c = [free[0]]
        xm_hi = sb("xm_hi", [P, 2, J * MASKED], F32R)
        xm_lo = sb("xm_lo", [P, 2, J * MASKED], F32R)
        hm_hi = sb("hm_hi", [P, C, J * MASKED], F32R)
        hm_lo = sb("hm_lo", [P, C, J * MASKED], F32R)
        gel = sb("gel", [P, 2, F])
        region_d = [free[0]]
        w1_hi = sb("w1_hi", [P, E * F], F32R)
        w1_lo = sb("w1_lo", [P, E * F], F32R)
        region_e = [free[0]]
        w2 = sb("w2", [P, E * F])
        region_f = [free[0]]
        stage = sb("stage", [P, 4, 1024])
        region_g = [free[0]]
        onehot = sb("onehot", [K2, N], F32R)
        table = sb("table", [K2, TABLE], F32R)
        trig = sb("trig", [P, ANG])
        rot_c = sb("rot_c", [P, T, 8])
        pick = sb("pick", [K2, E], F32R)
        turned = sb("turned", [P, D])
        row = sb("row", [P, D])
        assert free[0] <= nc.sbuf_usable_end, (free[0], nc.sbuf_usable_end)

        def region(start, end):
            at = list(start)

            def place(name, shape, dt=F32):
                t = sb(name, shape, dt, at=at)
                assert at[0] <= end[0], (name, at[0], end[0])
                return t
            return place

        stage_wo = sb("stage_wo", [P, 4, 1024], at=list(region_e))
        place = region(region_d, region_e)
        table_raw = place("table_raw", [K2, TABLE])
        ang = place("ang", [P, 3, ANG])
        rot_row = place("rot_row", [B, 8])
        subj = place("subj", [B, B])
        hyp = place("hyp", [P, 6, B])
        time_emb = place("time_emb", [P, B])
        of_sample = place("of_sample", [B, N])
        place = region(region_x, [region_x[0] + 4 * N])
        sq = place("sq", [P, HALF])
        cen = place("cen", [P, HALF])
        place = region(region_a, region_b)
        act_r = place("act_r", [P, 3, BANK])
        act_g = place("act_g", [P, 3, BANK])
        mask_f = place("mask_f", [P, B * S])
        x3_rep0 = place("x3_rep0", [P, BH, J, S])
        qx0 = place("qx0", [P, BH, H4, S])
        place = region(region_b, region_c)
        bias = place("bias", [P, 2, HG, BH, S])
        region_sc = [region_b[0] + 4 * HG * B * S]
        sc = place("sc", [P, 2, HG, BH, S])
        place = region(region_c, region_d)
        late = place("late", [P, LATE_W])
        mask = place("mask", [P, B * S], U8)
        y_t = place("y_t", [P, N])
        x3_t = place("x3_t", [P, N])
        k_t = place("k_t", [P, N])
        ctx_t = place("ctx_t", [P, N])
        x4_t = place("x4_t", [P, N])
        h_t = place("h_t", [P, N])
        place = region(region_f, region_g)
        vb0 = place("vb0", [P, BH, P])
        pt0 = place("pt0", [P, HG, BH, S])
        place = region(region_d, region_e)
        x3_rep = [x3_rep0, place("x3_rep1", [P, BH, J, S])]
        qx = [qx0, place("qx1", [P, BH, H4, S])]
        vb = [vb0, place("vb1", [P, BH, P])]
        pt = [pt0, place("pt1", [P, HG, BH, S])]
        x4_tm = sb("x4_tm", [P, T, D], at=list(region_g))
        ffn_h = [sb(f"ffn_h{hv}", [P, C, HALF], at=[region_sc[0] + hv * 4 * C * HALF]) for hv in range(2)]
        out_tm = sb("out_tm", [P, T, D], at=list(region_b))
        smax = sb("smax", [P, 2 * HG, BH])
        head_b = sb("head_b", [P, H4])
        assert free[0] <= nc.sbuf_usable_end, (free[0], nc.sbuf_usable_end)

        bank = [ctx.enter_context(nc.psum_tensor(f"bank{i}", [P, BANK], F32)) for i in range(8)]

        ident = early[:, EARLY["ident"][0]:EARLY["ident"][1]]

        def small(name, rows=P, k=0, n=None):
            a, b = EARLY[name]
            return early[0:rows, a + k:(a + k + n if n else b)]

        def col(name, k=0, rows=P):
            a = EARLY["cols"][0] + COLS[name][0] + k
            return early[0:rows, a:a + 1]

        def lt(name, k=0, n=None):
            a, b = LATE[name]
            return late[:, a + k:(a + k + n if n else b)]

        def per_sample(a):
            return a.unsqueeze(2).broadcast_to([a.shape[0], a.shape[1], S])

        def by_sample(a):
            return a.rearrange("p (b s) -> p b s", s=S)

        def diag(a):
            if len(a.shape) == 3:
                return a.rearrange("p c (j u) -> p c j u", u=MASKED)[:, :, :, 0:S]
            return a.rearrange("p (j u) -> p j u", u=MASKED)[:, :, 0:S]

        def by_chunk(a):
            return a.rearrange("p (c j s) -> p c j s", j=J, s=S)

        def by_tile(a):
            return a.rearrange("p (t d) -> p t d", d=P)


        def repeated(hv):
            return by_sample(x3_t[:, hv * HALF:(hv + 1) * HALF]).unsqueeze(2).broadcast_to([P, BH, J, S])

        d_ids, d_early, d_table, d_xt, d_xtm = sem("d_ids"), sem("d_early"), sem("d_table"), sem("d_xt"), sem("d_xtm")
        d_wi = [sem(f"d_wi{k}") for k in range(4)]
        d_wo = [sem(f"d_wo{k}") for k in range(4)]
        d_w1 = [sem(f"d_w1{k}") for k in range(4)]
        d_w2, d_late, d_mask, d_bias, d_out = sem("d_w2"), sem("d_late"), sem("d_mask"), sem("d_bias"), sem("d_out")
        dve_link = sem("dve_link")
        onehot_ready, table_ready, subj_ready = sem("onehot_ready"), sem("table_ready"), sem("subj_ready")
        of_sample_ready = sem("of_sample_ready")
        angles_ready, rot_row_ready = sem("angles_ready"), sem("rot_row_ready")
        setup_done = sem("setup_done")
        wi_lo_ready, wo_lo_dve = sem("wi_lo_ready"), sem("wo_lo_dve")
        xm_ready, hm_lo_ready, o_read, var_ready = sem("xm_ready"), sem("hm_lo_ready"), sem("o_read"), sem("var_ready")
        nrm_ready = sem("nrm_ready")
        var4_ready, rstd4_ready = sem("var4_ready"), sem("rstd4_ready")
        softplus_in, gates_z, cen_ready, svar_ready = sem("softplus_in"), sem("gates_z"), sem("cen_ready"), sem("svar_ready")
        hf_ready, hf_lo_ready, comb_ready = sem("hf_ready"), sem("hf_lo_ready"), sem("comb_ready")
        gated = sem("gated")
        x3_ready, k_ready, v_ready, score_read = sem("x3_ready"), sem("k_ready"), sem("v_ready"), sem("score_read")
        smax_ready, pt_ready, ctx_div, x4_ready = sem("smax_ready"), sem("pt_ready"), sem("ctx_div"), sem("x4_ready")
        x4_tm_ready, out_ready = sem("x4_tm_ready"), sem("out_ready")
        act_link = sem("act_link")
        trig_ready, time_ready, hyp_ready = sem("trig_ready"), sem("time_ready"), sem("hyp_ready")
        softplus_ln = sem("softplus_ln")
        wi_hi_ready, wo_hi_ready, w1_hi_ready = sem("wi_hi_ready"), sem("wo_hi_ready"), sem("w1_hi_ready")
        gel_ready, hm_hi_ready, h_ready, sq_ready = sem("gel_ready"), sem("hm_hi_ready"), sem("h_ready"), sem("sq_ready")
        hf_hi_ready, gates_e, comb_t_ready, relu_ready = sem("hf_hi_ready"), sem("gates_e"), sem("comb_t_ready"), sem("relu_ready")
        y_ready, qx_ready, exp_ready, ctx_ready = sem("y_ready"), sem("qx_ready"), sem("exp_ready"), sem("ctx_ready")
        h4_ready, ffn_ready, x3_rep1_ready = sem("h4_ready"), sem("ffn_ready"), sem("x3_rep1_ready")
        zeroed, wo_lo_ready, w1_lo_ready = sem("zeroed"), sem("wo_lo_ready"), sem("w1_lo_ready")
        rstd_ready, srstd_ready, pool_link, bias_ready = sem("rstd_ready"), sem("srstd_ready"), sem("pool_link"), sem("bias_ready")
        sub_ready, x3_rep0_ready = sem("sub_ready"), sem("x3_rep0_ready")
        rot_done, hyp_done, ada_done = sem("rot_done"), sem("hyp_done"), sem("ada_done")
        h_done, t_done, o_done, nt_done = sem("h_done"), sem("t_done"), sem("o_done"), sem("nt_done")
        logits_done, comb_done, combb_done, s1_done = sem("logits_done"), sem("comb_done"), sem("combb_done"), sem("s1_done")
        s2_done = sem("s2_done")
        ytm_done, nt3_done, q_done, k_done = sem("ytm_done"), sem("nt3_done"), sem("q_done"), sem("k_done")
        v_done, score_done, ctx_done, wo_done = sem("v_done"), sem("score_done"), sem("ctx_done"), sem("wo_done")
        x4tm_done, n4_done, f1_done, f2_done = sem("x4tm_done"), sem("n4_done"), sem("f1_done"), sem("f2_done")

        H_BANK, T_BANK, O_BANK, NT_BANK = (0, 1), (2, 3), (4, 5), (6, 7)
        HID_BANK, GATE_BANK, Y_BANK = (0, 1, 2), (4, 5), (6, 7)
        YTM_BANK, N3_BANK = (3, 0), (6, 1)
        Q_BANK, K_BANK, V_BANK = (3, 2), (6, 4), ((3, 6), (0, 1))
        SCORE_BANK, CTX_BANK, SUM_BANK = ((3, 6, 3, 6), (0, 1, 2, 4)), (3, 7), (6, 5)
        WO_BANK, X4_BANK, N4_BANK = (5, 0), (3, 1), (6, 2)
        F1_BANK, F2_BANK = ((5, 6), (4, 0)), (3, 7)

        block = ctx.enter_context(nc.Block())

        @block.sync
        def _(sp):
            sp.dma_start(ids[:, :], ids_d).then_inc(d_ids, 16)
            sp.dma_start(early[:, :], early_d).then_inc(d_early, 16)
            for k in range(4):
                sp.dma_start(stage[:, k, :], wi_d[:, k * 1024:(k + 1) * 1024]).then_inc(d_wi[k], 16)
                if k == 0:
                    sp.dma_start(x_t[:, :], x_t_d).then_inc(d_xt, 16)
                if k == 1:
                    sp.dma_start(table_raw[:, :], tables_d).then_inc(d_table, 16)
            for k in range(4):
                sp.dma_start(stage_wo[:, k, :], wo_d[:, k * 1024:(k + 1) * 1024]).then_inc(d_wo[k], 16)
            sp.dma_start(rows_tm[:, :, :], x_tm_d).then_inc(d_xtm, 16)
            for k in range(4):
                sp.wait_ge(wi_lo_ready, k + 1)
                sp.dma_start(stage[:, k, :], w1_d[:, k * 1024:(k + 1) * 1024]).then_inc(d_w1[k], 16)
            sp.wait_ge(wo_lo_ready, 2)
            sp.wait_ge(wo_lo_dve, 2)
            sp.dma_start(w2[:, :], w2_d).then_inc(d_w2, 16)
            sp.wait_ge(o_done, T)
            sp.dma_start(mask[:, :], mask_d).then_inc(d_mask, 16)
            sp.dma_start(bias[:, :, :, :, :], fside_d).then_inc(d_bias, 16)
            sp.dma_start(late[:, :], late_d).then_inc(d_late, 16)
            for hv in range(2):
                sp.wait_ge(out_ready, hv + 1)
                sp.dma_start(out_d[:, hv * 4:hv * 4 + 4, :], out_tm[:, hv * 4:hv * 4 + 4, :]).then_inc(d_out, 16)
            sp.wait_ge(d_out, 32)

        @block.gpsimd
        def _(pool):
            def link(ins):
                link.n += 1
                ins.then_inc(pool_link, 1)
                pool.wait_ge(pool_link, link.n)
            link.n = 0

            for a in (xm_hi, xm_lo):
                pool.memset(a[:, :, :].bitcast(F32), 0.0).then_inc(zeroed, 1)
            for a in (hm_hi, hm_lo):
                pool.memset(a[:, :, :].bitcast(F32), 0.0).then_inc(zeroed, 1)
            link(pool.memset(minus_half[:, :], -0.5))
            for k in (1, 3):
                w = slice(k * E, (k + 1) * E)
                pool.wait_ge(wo_hi_ready, k + 1)
                pool.tensor_tensor(wo_hl[:, w, 1, :], by_tile(stage_wo[:, k, :]), wo_hl[:, w, 0, :].bitcast(F32),
                                   ALU.subtract).then_inc(wo_lo_ready, 1)

            def power(out, in_, eps, ready, shifted=veps):
                n = in_.shape[1]
                link(pool.tensor_scalar(shifted[:, 0:n], in_, eps, None, ALU.add))
                pool.tensor_tensor(out, shifted[:, 0:n], minus_half[:, 0:n], ALU.pow).then_inc(ready, 1)

            def w1_lo_part(p):
                w = slice(p * F, (p + 1) * F)
                pool.wait_ge(w1_hi_ready, p + 1)
                pool.tensor_tensor(w1_lo[:, w], stage[:, p // 2, p % 2 * F:p % 2 * F + F],
                                   w1_hi[:, w].bitcast(F32), ALU.subtract).then_inc(w1_lo_ready, 1)

            def token_norm(hv):
                pool.wait_ge(svar_ready, hv + 1)
                power(sums[:, 2, :], sums[:, 1, :], 1e-8, srstd_ready, token_veps)

            for t in range(T):
                for n, eps in ((0, 1e-12), (1, 1e-5)):
                    pool.wait_ge(var_ready, 2 * t + n + 1)
                    power(rstd[:, n:n + 1], stat[:, n, 7:8], eps, rstd_ready)
                if t < 4:
                    w1_lo_part(2 * t)
                    w1_lo_part(2 * t + 1)
                if t == 4:
                    token_norm(0)
            token_norm(1)
            pool.wait_ge(d_mask, 16)
            pool.wait_ge(d_bias, 16)
            link(pool.tensor_scalar(mask_f[:, :], mask[:, :], MASKED_SCORE, None, ALU.mult))
            for hv in range(2):
                a = bias[:, hv, :, :, :]
                m = by_sample(mask_f[:, hv * HALF:(hv + 1) * HALF]).unsqueeze(1).broadcast_to([P, HG, BH, S])
                pool.tensor_tensor(a, a, m, ALU.add).then_inc(bias_ready, 1)

            def norms(n):
                pool.wait_ge(var4_ready, n + 1)
                power(rstd4[:, :], stat4[:, :, 7], 1e-5, rstd4_ready)

            def subtract(hv):
                for hg in range(HG):
                    n = hv * HG + hg
                    pool.wait_ge(smax_ready, n + 1)
                    a = sc[:, hv, hg, :, :]
                    pool.tensor_tensor(a, a, per_sample(smax[:, n, :]), ALU.subtract).then_inc(sub_ready, 1)

            norms(0)
            pool.wait_ge(x3_ready, 1)
            pool.tensor_copy(x3_rep[0][:, :, :, :], repeated(0)).then_inc(x3_rep0_ready, 1)
            subtract(0)
            norms(1)
            norms(2)
            subtract(1)
            norms(3)

        @block.scalar
        def _(act):
            def wi_part(k):
                w = slice(k * 1024, (k + 1) * 1024)
                act.wait_ge(d_wi[k], 16)
                act.activation(wi_hi[:, w], stage[:, k, :], ACT.Copy).then_inc(wi_hi_ready, 1)

            def wo_part(k):
                act.wait_ge(d_wo[k], 16)
                act.activation(wo_hl[:, k * E:(k + 1) * E, 0, :], by_tile(stage_wo[:, k, :]), ACT.Copy)\
                    .then_inc(wo_hi_ready, 1)

            act.wait_ge(angles_ready, 1)
            act.activation(trig[:, :], ang[:, 0, :], ACT.Sin).then_inc(trig_ready, 1)
            act.wait_ge(trig_ready, 1)
            act.activation(time_emb[:, :], trig[:, 0:B], ACT.Silu).then_inc(time_ready, 1)
            wi_part(0)
            wi_part(1)
            b7 = bank[7]
            act.wait_ge(hyp_done, 1)
            act.activation(hyp[0:64, 0, :], b7[0:64, 0:32], ACT.Copy).then_inc(hyp_ready, 1)
            wi_part(2)
            act.wait_ge(hyp_done, 2)
            act.activation(hyp[:, 1, :], b7[:, 32:64], ACT.Relu, bias=col("hyp_b1")).then_inc(hyp_ready, 1)
            wi_part(3)
            act.wait_ge(hyp_done, 3)
            act.activation(hyp[:, 2, :], b7[:, 64:96], ACT.Identity, bias=col("hyp_b2")).then_inc(hyp_ready, 1)
            wo_part(0)
            act.wait_ge(hyp_done, 4)
            act.activation(hyp[0:64, 3, :], b7[0:64, 96:128], ACT.Relu, bias=col("sty_b1", rows=64)).then_inc(hyp_ready, 1)
            wo_part(1)
            wo_part(2)
            wo_part(3)
            act.wait_ge(softplus_in, 1)
            act.activation(hyp[:, 5, :], hyp[:, 5, :], ACT.Exp).then_inc(act_link, 1)
            act.wait_ge(act_link, 1)
            act.activation(hyp[:, 5, :], hyp[:, 5, :], ACT.Ln, bias=1.0).then_inc(softplus_ln, 1)

            def gelu(t):
                act.wait_ge(h_done, t + 1)
                if t >= 2:
                    act.wait_ge(t_done, t - 1)
                act.activation(gel[:, t % 2, :], bank[H_BANK[t % 2]][:, :], ACT.Gelu).then_inc(gel_ready, 1)

            def w1_part(p):
                if p == 0:
                    act.wait_ge(setup_done, 1)
                act.wait_ge(d_w1[p // 2], 16)
                act.activation(w1_hi[:, p * F:(p + 1) * F], stage[:, p // 2, p % 2 * F:p % 2 * F + F],
                               ACT.Copy).then_inc(w1_hi_ready, 1)

            def layer_scale(hv):
                act.wait_ge(nt_done, 4 * hv + 4)
                if hv:
                    act.wait_ge(hf_ready, 1)
                else:
                    act.wait_ge(h_done, T)
                act.activation(cen[:, :], bank[NT_BANK[hv]][:, :], ACT.Identity,
                               scale=col("ln_g"), bias=col("ln_b")).then_inc(h_ready, 1)

            def squares(hv):
                act.wait_ge(cen_ready, hv + 1)
                act.activation(sq[:, :], cen[:, :], ACT.Square).then_inc(sq_ready, 1)

            def hf_high(hv):
                act.wait_ge(hf_ready, hv + 1)
                act.activation(hf_hi[:, hv * HALF:(hv + 1) * HALF], hf[:, :], ACT.Copy).then_inc(hf_hi_ready, 1)

            def router_exp(hv):
                act.wait_ge(gates_z, hv + 1)
                act.activation(rt[:, 1, :], rt[:, 0, :], ACT.Exp).then_inc(gates_e, 1)

            def gates_copy(hv):
                act.wait_ge(comb_done, hv + 1)
                act.activation(comb_t[:, hv * HALF:(hv + 1) * HALF], bank[NT_BANK[hv]][0:K2, :], ACT.Copy)\
                    .then_inc(comb_t_ready, 1)

            def relu(q):
                e, c = q // C % E, q % C
                act.wait_ge(s1_done, q + 1)
                if q >= 3:
                    act.wait_ge(gated, q - 2)
                act.activation(act_r[:, q % 3, :], bank[HID_BANK[q % 3]][:, :], ACT.Relu,
                               bias=col("exp_b1", e * C + c)).then_inc(relu_ready, 1)

            def y_copy(hv):
                act.wait_ge(s2_done, (hv + 1) * E * C)
                act.activation(y_t[:, hv * HALF:(hv + 1) * HALF], bank[Y_BANK[hv]][:, :], ACT.Copy).then_inc(y_ready, 1)

            def queries(hv, heads):
                act.wait_ge(q_done, hv + 1)
                if hv == 0 and heads[0] == 0:
                    act.wait_ge(d_late, 16)
                    for h4 in range(H4):
                        act.activation(head_b[:, h4:h4 + 1], lt("head", h4, 1), ACT.Copy, scale=col("bq"))\
                            .then_inc(act_link, 1)
                    act.wait_ge(act_link, 1 + H4)
                for h4 in heads:
                    act.activation(qx[hv][:, :, h4, :], by_sample(bank[Q_BANK[hv]][:, :]),
                                   ACT.Identity, scale=lt("head", h4, 1), bias=head_b[:, h4:h4 + 1])\
                        .then_inc(qx_ready, 1)

            def exps(hv, hg):
                act.wait_ge(sub_ready, hv * HG + hg + 1)
                a = sc[:, hv, hg, :, :]
                act.activation(a, a, ACT.Exp).then_inc(exp_ready, 1)

            def context(hv):
                a = ctx_t[:, hv * HALF:(hv + 1) * HALF]
                act.wait_ge(ctx_div, hv + 1)
                act.activation(a, a, ACT.Identity, bias=col("bv")).then_inc(ctx_ready, 1)

            def h4_scale(hv):
                act.wait_ge(n4_done, hv + 1)
                act.activation(h_t[:, hv * HALF:(hv + 1) * HALF], bank[N4_BANK[hv]][:, :], ACT.Identity,
                               scale=col("g2"), bias=col("beta2")).then_inc(h4_ready, 1)

            def ffn_gelu(hv):
                act.wait_ge(pt_ready, (hv + 1) * HG)
                for c in range(C):
                    act.wait_ge(f1_done, hv * C + c + 1)
                    act.activation(ffn_h[hv][:, c, :], bank[F1_BANK[hv][c % 2]][:, :], ACT.Gelu_apprx_sigmoid,
                                   bias=col("ffn_b1", c)).then_inc(ffn_ready, 1)

            act.wait_ge(zeroed, 4)
            gelu(0)
            for t in range(T):
                act.wait_ge(t_done, t + 1)
                if t >= 1:
                    act.wait_ge(o_done, t)
                act.activation(diag(hm_hi[:, :, :]), by_chunk(bank[T_BANK[t % 2]][:, :]), ACT.Copy)\
                    .then_inc(hm_hi_ready, 1)
                if t + 1 < T:
                    gelu(t + 1)
                if t < 4:
                    w1_part(2 * t)
                    w1_part(2 * t + 1)
                if t == 6:
                    layer_scale(0)
                    squares(0)
                if t == 7:
                    hf_high(0)
                    router_exp(0)
            gates_copy(0)
            MOE = 2 * E * C
            R1 = E * C
            for q in range(MOE):
                relu(q)
                if q == 7:
                    layer_scale(1)
                if q == 10:
                    squares(1)
                if q == 16:
                    hf_high(1)
                if q == 20:
                    router_exp(1)
                if q == 28:
                    gates_copy(1)
                if q == R1 + 2:
                    y_copy(0)
                if q == R1 + 12:
                    queries(0, (0, 1))
                if q == R1 + 13:
                    queries(0, (2, 3))
                if q in range(R1 + 23, R1 + 31, 2):
                    exps(0, (q - R1 - 23) // 2)
            y_copy(1)
            context(0)
            act.wait_ge(x3_ready, 2)
            act.activation(x3_rep[1][:, :, :, :], repeated(1), ACT.Copy).then_inc(x3_rep1_ready, 1)
            queries(1, (0, 1, 2, 3))
            h4_scale(0)
            ffn_gelu(0)
            for hg in range(HG):
                exps(1, hg)
            context(1)
            h4_scale(1)
            ffn_gelu(1)

        @block.vector
        def _(dve):
            def link(ins):
                link.n += 1
                ins.then_inc(dve_link, 1)
                dve.wait_ge(dve_link, link.n)
            link.n = 0

            def then(ins, ready, value):
                ins.then_inc(ready, 1)
                dve.wait_ge(ready, value)

            dve.wait_ge(d_ids, 16)
            link(dve.tensor_copy(ids_f[:, :], ids[:, :]))
            dve.wait_ge(d_early, 16)
            link(dve.tensor_scalar(ang[:, 0, 0:B], ids_f[:, 2 * B:3 * B], 0.01, 4000.0, ALU.mult, ALU.mult))
            link(dve.tensor_scalar(ang[:, 0, 0:B], ang[:, 0, 0:B], small("freq"), None, ALU.mult))
            link(dve.tensor_copy(ang[:, 0, B:ANG].rearrange("p (a c) -> p a c", c=2),
                                 small("angles").unsqueeze(2).broadcast_to([P, 2, 2])))
            link(dve.scalar_tensor_tensor(ang[:, 1, :], ang[:, 0, :], TWO_PI_INV, small("turn"), ALU.mult, ALU.add))
            link(dve.tensor_scalar(ang[:, 1, :], ang[:, 1, :], ROUND, -ROUND, ALU.add, ALU.add))
            for part in (TWO_PI_A, TWO_PI_B, TWO_PI_C):
                link(dve.scalar_tensor_tensor(ang[:, 0, :], ang[:, 1, :], -part, ang[:, 0, :], ALU.mult, ALU.add))
            link(dve.tensor_tensor(ang[:, 0, :], ang[:, 0, :], small("quarter"), ALU.add))
            dve.tensor_scalar(ang[:, 0, :], ang[:, 0, :], PI_SAFE, -PI_SAFE, ALU.min, ALU.max).then_inc(angles_ready, 1)
            dve.tensor_scalar(by_sample(onehot[:, :]), per_sample(ids_f[0:K2, 0:B]), small("expert_row", K2), None,
                              ALU.is_equal).then_inc(onehot_ready, 1)
            dve.tensor_scalar(subj[:, :], ids_f[0:B, B:2 * B], small("sample_row", B), None,
                              ALU.is_equal).then_inc(subj_ready, 1)
            dve.tensor_copy(by_sample(of_sample[:, :]), ident[0:B, 0:B].unsqueeze(2).broadcast_to([B, B, S]))\
                .then_inc(of_sample_ready, 1)
            dve.tensor_copy(pick[:, :], small("pick", K2))
            dve.wait_ge(d_table, 16)
            link(dve.tensor_copy(table[:, :], table_raw[:, :]))
            dve.tensor_tensor(table[LO:K2, :], table_raw[LO:K2, :], table[LO:K2, :].bitcast(F32),
                              ALU.subtract).then_inc(table_ready, 1)
            dve.wait_ge(trig_ready, 1)
            sin_cos = trig[0:B, B:ANG].rearrange("p (a c) -> p a c", c=2)
            dve.tensor_copy(rot_row[:, 0:4].rearrange("p (a c) -> p a c", c=2),
                            sin_cos[:, :, 1:2].broadcast_to([B, 2, 2]))
            dve.tensor_copy(rot_row[:, 4:6], sin_cos[:, :, 0])
            dve.tensor_scalar(rot_row[:, 6:8], sin_cos[:, :, 0], -1.0, None, ALU.mult).then_inc(rot_row_ready, 1)

            def masked_x(t):
                src = x_t[:, t * P:(t + 1) * P].rearrange("p (j s) -> p j s", s=S)
                if t >= 2:
                    dve.wait_ge(h_done, t - 1)
                link(dve.tensor_copy(diag(xm_hi[:, t % 2, :]), src))
                dve.tensor_tensor(diag(xm_lo[:, t % 2, :]), src, diag(xm_hi[:, t % 2, :].bitcast(F32)),
                                  ALU.subtract).then_inc(xm_ready, 1)

            def masked_h_lo(t):
                dve.wait_ge(hm_hi_ready, t + 1)
                dve.tensor_tensor(diag(hm_lo[:, :, :]), by_chunk(bank[T_BANK[t % 2]][:, :]),
                                  diag(hm_hi[:, :, :].bitcast(F32)), ALU.subtract).then_inc(hm_lo_ready, 1)

            dve.wait_ge(d_xt, 16)
            dve.wait_ge(zeroed, 4)
            masked_x(0)
            masked_x(1)
            for k in range(4):
                w = slice(k * 1024, (k + 1) * 1024)
                dve.wait_ge(wi_hi_ready, k + 1)
                dve.tensor_tensor(wi_lo[:, w], stage[:, k, :], wi_hi[:, w].bitcast(F32), ALU.subtract)\
                    .then_inc(wi_lo_ready, 1)
                if k == 1:
                    dve.wait_ge(rot_done, 1)
                    dve.tensor_copy(rot_c[:, :, :], bank[6][:, 0:8 * T].rearrange("p (t c) -> p t c", c=8))
                    dve.wait_ge(ada_done, 1)
                    dve.tensor_scalar(affine[:, 2, :], bank[3][:, 0:32], col("b_ada"), 1.0, ALU.add, ALU.add)
                    dve.tensor_scalar(affine[:, 3, :], bank[3][:, 32:64], col("b_ada", 1), None, ALU.add)
                if k == 2:
                    dve.wait_ge(hyp_done, 5)
                    link(dve.tensor_scalar(hyp[:, 4, :], bank[7][:, 128:160], col("sty_b2"), None, ALU.add))
                    dve.scalar_tensor_tensor(hyp[:, 5, :], hyp[:, 4, :], -1.0, hyp[:, 4, :], ALU.mult, ALU.min)\
                        .then_inc(softplus_in, 1)
                    dve.tensor_scalar(affine[:, 1, :], bank[7][:, 160:192], col("sty_b2", 1), None, ALU.add)
            for k in (0, 2):
                w = slice(k * E, (k + 1) * E)
                dve.wait_ge(wo_hi_ready, k + 1)
                dve.tensor_tensor(wo_hl[:, w, 1, :], by_tile(stage_wo[:, k, :]), wo_hl[:, w, 0, :].bitcast(F32),
                                  ALU.subtract).then_inc(wo_lo_dve, 1)
            dve.wait_ge(softplus_ln, 1)
            link(dve.scalar_tensor_tensor(affine[:, 0, :], hyp[:, 4, :], 0.0, hyp[:, 5, :], ALU.max, ALU.add))
            then(dve.tensor_scalar(affine[:, 0, :], affine[:, 0, :], 1e-8, None, ALU.add), setup_done, 1)

            def normalise(out, in_, n, done, ready):
                link(dve.bn_stats(stat[:, n, 0:6], in_))
                dve.bn_aggr(stat[:, n, 6:8], stat[:, n, 0:6]).then_inc(var_ready, 1)
                dve.wait_ge(var_ready, done)
                dve.wait_ge(rstd_ready, done)
                ins = dve.tensor_scalar(out, in_, stat[:, n, 6:7], rstd[:, n:n + 1], ALU.subtract, ALU.mult)
                if ready is None:
                    link(ins)
                else:
                    ins.then_inc(ready, 1)

            def residual_norm(t):
                o = bank[O_BANK[t % 2]]
                dve.wait_ge(o_done, t + 1)
                link(dve.tensor_tensor(row[:, :], o[:, 0:D], rows_tm[:, t, :], ALU.add))
                link(dve.tensor_tensor(row[:, :], row[:, :], o[:, D:2 * D], ALU.add))
                normalise(row[:, :], row[:, :], 0, 2 * t + 1, None)
                link(dve.tensor_tensor(row[:, :], row[:, :], o[:, 2 * D:3 * D], ALU.mult))
                then(dve.tensor_tensor(row[:, :], row[:, :], o[:, 3 * D:4 * D], ALU.add), o_read, t + 1)

            def rotate_norm(t):
                quads = row[:, :].rearrange("p (g c) -> p g c", c=4)
                pairs = row[:, :].rearrange("p (g a i) -> p g a i", a=2, i=2)
                swapped = turned[:, :].rearrange("p (g a i) -> p g a i", a=2, i=2)
                rot = rows_tm[:, t, :]
                dve.tensor_tensor(rot.rearrange("p (g c) -> p g c", c=4), quads,
                                  rot_c[:, t, 0:4].unsqueeze(1).broadcast_to([P, D // 4, 4]), ALU.mult)
                for i, k in ((0, 4), (1, 6)):
                    ins = dve.tensor_tensor(swapped[:, :, :, i], pairs[:, :, :, 1 - i],
                                            rot_c[:, t, k:k + 2].unsqueeze(1).broadcast_to([P, D // 4, 2]), ALU.mult)
                link(ins)
                link(dve.tensor_tensor(rot, rot, turned[:, :], ALU.add))
                normalise(nrm_tm[:, t, :], rot, 1, 2 * t + 2, nrm_ready)

            def center(hv):
                h = by_sample(cen[:, :])
                dve.wait_ge(h_ready, hv + 1)
                link(dve.tensor_reduce(sums[:, 0, :], h, AX.X, ALU.add))
                dve.scalar_tensor_tensor(h, per_sample(sums[:, 0, :]), -1.0 / S, h, ALU.mult, ALU.add)\
                    .then_inc(cen_ready, 1)

            def token_variance(hv):
                dve.wait_ge(sq_ready, hv + 1)
                link(dve.tensor_reduce(sums[:, 1, :], by_sample(sq[:, :]), AX.X, ALU.add))
                dve.tensor_scalar(sums[:, 1, :], sums[:, 1, :], 1.0 / S, None, ALU.mult).then_inc(svar_ready, 1)

            def affine_rows(hv):
                b0, b1 = hv * BH, (hv + 1) * BH
                h, out = by_sample(cen[:, :]), by_sample(hf[:, :])
                dve.wait_ge(srstd_ready, hv + 1)
                link(dve.tensor_tensor(sums[:, 2, :], sums[:, 2, :], affine[:, 0, b0:b1], ALU.mult))
                link(dve.tensor_tensor(out, h, per_sample(sums[:, 2, :]), ALU.mult))
                dve.tensor_tensor(out, out, per_sample(affine[:, 1, b0:b1]), ALU.add).then_inc(hf_ready, 1)

            def l2_lo(hv):
                c0, c1 = hv * HALF, (hv + 1) * HALF
                dve.wait_ge(hf_hi_ready, hv + 1)
                dve.tensor_tensor(hf_lo[:, c0:c1], hf[:, :], hf_hi[:, c0:c1].bitcast(F32), ALU.subtract)\
                    .then_inc(hf_lo_ready, 1)

            def wide(i):
                return rt_s[:, i, :].unsqueeze(2).broadcast_to([P, 4, E])

            def rt_v(i):
                return rt[:, i, :].rearrange("p (t e) -> p t e", e=E)

            def first_max(probs, largest, chosen):
                prefer = small("prefer").unsqueeze(1).broadcast_to([P, 4, E])
                link(dve.tensor_reduce(rt_s[:, largest, :], rt_v(probs), AX.X, ALU.max))
                link(dve.tensor_tensor(rt_v(chosen), rt_v(probs), wide(largest), ALU.is_equal))
                link(dve.tensor_tensor(rt_v(chosen), rt_v(chosen), prefer, ALU.mult))
                link(dve.tensor_reduce(rt_s[:, 7, :], rt_v(chosen), AX.X, ALU.max))
                link(dve.tensor_tensor(rt_v(chosen), rt_v(chosen), wide(7), ALU.is_equal))

            def router_shift(hv):
                logits = bank[NT_BANK[hv]][:, 0:4 * E].rearrange("p (t e) -> p t e", e=E)
                dve.wait_ge(logits_done, hv + 1)
                link(dve.tensor_reduce(rt_s[:, 0, :], logits, AX.X, ALU.max))
                dve.tensor_tensor(rt_v(0), logits, wide(0), ALU.subtract).then_inc(gates_z, 1)

            def router_first(hv):
                dve.wait_ge(gates_e, hv + 1)
                link(dve.tensor_reduce(rt_s[:, 1, :], rt_v(1), AX.X, ALU.add))
                link(dve.reciprocal(rt_s[:, 1, :], rt_s[:, 1, :]))
                link(dve.tensor_tensor(rt_v(2), rt_v(1), wide(1), ALU.mult))
                first_max(2, 2, 3)

            def router_second(hv):
                link(dve.scalar_tensor_tensor(rt_v(5), rt_v(3), -2.0, rt_v(2), ALU.mult, ALU.add))
                first_max(5, 4, 6)
                link(dve.tensor_tensor(rt_v(3), rt_v(3), rt_v(6), ALU.add))
                link(dve.tensor_tensor(rt_s[:, 6, :], rt_s[:, 2, :], rt_s[:, 4, :], ALU.add))
                link(dve.reciprocal(rt_s[:, 6, :], rt_s[:, 6, :]))
                link(dve.tensor_tensor(rt_v(3), rt_v(3), rt_v(2), ALU.mult))
                link(dve.tensor_tensor(rt_v(3), rt_v(3), wide(6), ALU.mult))
                link(dve.tensor_copy(comb_hi[:, :], rt[:, 3, :]))
                hi = comb_hi[:, :].bitcast(F32).rearrange("p (t e) -> p t e", e=E)
                if hv:
                    dve.wait_ge(comb_done, hv)
                dve.tensor_copy(comb_hl[:, :, 0:E], hi)
                dve.tensor_tensor(comb_hl[:, :, LO:K2], rt_v(3), hi, ALU.subtract).then_inc(comb_ready, 1)

            link(dve.memset(comb_hl[:, :, :], 0.0))
            masked_h_lo(0)
            masked_x(2)
            dve.wait_ge(d_xtm, 16)
            for t in range(1, T):
                masked_h_lo(t)
                if t + 2 < T:
                    masked_x(t + 2)
                if t == 6:
                    center(0)
                    token_variance(0)
                if t == 7:
                    l2_lo(0)
                    router_shift(0)
                residual_norm(t - 1)
                rotate_norm(t - 1)
                if t == 6:
                    affine_rows(0)
                if t == 7:
                    router_first(0)
                    router_second(0)

            def gate(q):
                dve.wait_ge(relu_ready, q + 1)
                dve.wait_ge(combb_done, q // C + 1)
                if q >= 3:
                    dve.wait_ge(s2_done, q - 2)
                dve.tensor_tensor(act_g[:, q % 3, :], act_r[:, q % 3, :], bank[GATE_BANK[q // C % 2]][:, :],
                                  ALU.mult).then_inc(gated, 1)

            def norm4_stats(rows, n):
                for i in range(4):
                    ins = dve.bn_stats(stat4[:, i, 0:6], rows[:, i, :])
                link(ins)
                for i in range(4):
                    ins = dve.bn_aggr(stat4[:, i, 6:8], stat4[:, i, 0:6])
                then(ins, var4_ready, n + 1)

            def norm4(rows, n):
                dve.wait_ge(rstd4_ready, n + 1)
                for i in range(4):
                    dve.tensor_scalar(nrm_tm[:, 4 * (n % 2) + i, :], rows[:, i, :], stat4[:, i, 6:7], rstd4[:, i:i + 1],
                                      ALU.subtract, ALU.mult).then_inc(nrm_ready, 1)

            def l3_start(hv):
                rows = rows_tm[:, 4 * hv:4 * hv + 4, :]
                dve.wait_ge(ytm_done, hv + 1)
                link(dve.tensor_tensor(rows, rows, by_tile(bank[YTM_BANK[hv]][:, :]), ALU.add))
                norm4_stats(rows, hv)

            def x3(hv):
                out = by_sample(x3_t[:, hv * HALF:(hv + 1) * HALF])
                b0, b1 = hv * BH, (hv + 1) * BH
                dve.wait_ge(nt3_done, hv + 1)
                link(dve.tensor_tensor(out, by_sample(bank[N3_BANK[hv]][:, :]), per_sample(affine[:, 2, b0:b1]), ALU.mult))
                dve.tensor_tensor(out, out, per_sample(affine[:, 3, b0:b1]), ALU.add).then_inc(x3_ready, 1)

            def keys(hv):
                dve.wait_ge(k_done, hv + 1)
                dve.tensor_scalar(k_t[:, hv * HALF:(hv + 1) * HALF], bank[K_BANK[hv]][:, :], col("bk"), None, ALU.add)\
                    .then_inc(k_ready, 1)

            def values(hv, i):
                dve.wait_ge(v_done, 4 * hv + i + 1)
                dve.tensor_tensor(vb[hv][:, 4 * i:4 * i + 4, :], by_tile(bank[V_BANK[hv][i % 2]][:, :]),
                                  lt("block").unsqueeze(1).broadcast_to([P, 4, P]), ALU.mult).then_inc(v_ready, 1)

            def scores(hv, hg):
                n = hv * HG + hg
                a = sc[:, hv, hg, :, :]
                dve.wait_ge(score_done, n + 1)
                dve.wait_ge(bias_ready, hv + 1)
                then(dve.tensor_tensor(a, by_sample(bank[SCORE_BANK[hv][hg]][:, :]), bias[:, hv, hg, :, :],
                                       ALU.add), score_read, n + 1)
                dve.tensor_reduce(smax[:, n, :], a, AX.X, ALU.max).then_inc(smax_ready, 1)

            def transposed(hv, hg):
                dve.wait_ge(exp_ready, hv * HG + hg + 1)
                dve.transpose(pt[hv][:, hg, :, :], sc[:, hv, hg, :, :]).then_inc(pt_ready, 1)

            def divide(hv):
                a = ctx_t[:, hv * HALF:(hv + 1) * HALF]
                dve.wait_ge(ctx_done, hv + 1)
                link(dve.reciprocal(a, bank[SUM_BANK[hv]][:, :]))
                dve.tensor_tensor(a, bank[CTX_BANK[hv]][:, :], a, ALU.mult).then_inc(ctx_div, 1)

            def x4(hv):
                w = slice(hv * HALF, (hv + 1) * HALF)
                dve.wait_ge(wo_done, hv + 1)
                dve.scalar_tensor_tensor(x4_t[:, w], bank[WO_BANK[hv]][:, :], col("bo"), x3_t[:, w], ALU.add, ALU.add)\
                    .then_inc(x4_ready, 1)

            def x4_norm(hv):
                rows = by_tile(bank[X4_BANK[hv]][:, :])
                dve.wait_ge(x4tm_done, hv + 1)
                norm4_stats(rows, 2 + hv)
                dve.tensor_tensor(x4_tm[:, 4 * hv:4 * hv + 4, :], rows, lt("b2").unsqueeze(1).broadcast_to([P, 4, P]),
                                  ALU.add).then_inc(x4_tm_ready, 1)
                norm4(rows, 2 + hv)

            def outputs(hv):
                w = slice(4 * hv, 4 * hv + 4)
                dve.wait_ge(f2_done, hv + 1)
                dve.tensor_tensor(out_tm[:, w, :], by_tile(bank[F2_BANK[hv]][:, :]), x4_tm[:, w, :], ALU.add)\
                    .then_inc(out_ready, 1)

            MOE = 2 * E * C
            R1 = E * C
            for q in range(MOE):
                gate(q)
                if q == 1:
                    residual_norm(T - 1)
                if q == 3:
                    rotate_norm(T - 1)
                if q == 8:
                    center(1)
                if q == 11:
                    token_variance(1)
                if q == 14:
                    affine_rows(1)
                if q == 16:
                    l2_lo(1)
                if q == 18:
                    router_shift(1)
                if q == 20:
                    router_first(1)
                if q == 23:
                    router_second(1)
                if q == R1 + 4:
                    l3_start(0)
                if q == R1 + 6:
                    norm4(rows_tm[:, 0:4, :], 0)
                if q == R1 + 9:
                    x3(0)
                if q == R1 + 13:
                    keys(0)
                if R1 + 15 <= q < R1 + 19:
                    values(0, q - R1 - 15)
                if q in range(R1 + 21, R1 + 29, 2):
                    scores(0, (q - R1 - 21) // 2)
                if q in range(R1 + 25, R1 + 33, 2):
                    transposed(0, (q - R1 - 25) // 2)
            l3_start(1)
            norm4(rows_tm[:, 4:8, :], 1)
            divide(0)
            x3(1)
            x4(0)
            keys(1)
            for i in range(4):
                values(1, i)
            x4_norm(0)
            for hg in range(HG):
                scores(1, hg)
            outputs(0)
            for hg in range(HG):
                transposed(1, hg)
            divide(1)
            x4(1)
            x4_norm(1)
            outputs(1)

        @block.tensor
        def _(pe):
            def mm(out, lhsT, rhs, start=True, stop=True):
                return pe.matmul(out, lhsT, rhs, start=start, stop=stop)

            def product(out, w_hi, w_lo, m_hi, m_lo, start, stop):
                mm(out, w_hi, m_hi, start, False)
                mm(out, w_hi, m_lo, False, False)
                return mm(out, w_lo, m_hi, False, stop)

            b7 = bank[7]
            pe.wait_ge(d_early, 16)
            pe.wait_ge(subj_ready, 1)
            mm(b7[0:64, 0:32], small("subj_emb", B), subj[:, :]).then_inc(hyp_done, 1)
            pe.wait_ge(rot_row_ready, 1)
            pe.wait_ge(of_sample_ready, 1)
            for t in range(T):
                ins = mm(bank[6][:, 8 * t:8 * t + 8],
                         of_sample[:, t * P:(t + 1) * P], rot_row[:, :])
            ins.then_inc(rot_done, 1)
            pe.wait_ge(hyp_ready, 1)
            mm(b7[:, 32:64], small("hyp_w1", 64), hyp[0:64, 0, :]).then_inc(hyp_done, 1)
            pe.wait_ge(time_ready, 1)
            mm(bank[3][:, 0:32], small("w_ada", k=0, n=P), time_emb[:, :])
            mm(bank[3][:, 32:64], small("w_ada", k=P, n=P), time_emb[:, :]).then_inc(ada_done, 1)
            pe.wait_ge(hyp_ready, 2)
            mm(b7[:, 64:96], small("hyp_w2"), hyp[:, 1, :]).then_inc(hyp_done, 1)
            pe.wait_ge(hyp_ready, 3)
            mm(b7[0:64, 96:128], small("sty_w1"), hyp[:, 2, :]).then_inc(hyp_done, 1)
            pe.wait_ge(hyp_ready, 4)
            mm(b7[:, 128:160], small("sty_w2", 64, 0, P), hyp[0:64, 3, :])
            mm(b7[:, 160:192], small("sty_w2", 64, P, P), hyp[0:64, 3, :]).then_inc(hyp_done, 1)

            def experts(t):
                return [pe.value_load(ids[0:1, J * t + j:J * t + j + 1], min_val=0, max_val=E - 1) for j in range(J)]

            def l0_up(t):
                pe.wait_ge(xm_ready, t + 1)
                if t == 0:
                    pe.wait_ge(wi_lo_ready, 4)
                if t >= 2:
                    pe.wait_ge(gel_ready, t - 1)
                out = bank[H_BANK[t % 2]][:, :]
                mm(out, onehot[:, t * P:(t + 1) * P], table[:, 0:F], True, False)
                of_tile[t] = experts(t)
                for j, e in enumerate(of_tile[t]):
                    own = slice(j * P, (j + 1) * P)
                    ins = product(out, xm_hi[:, t % 2, own], xm_lo[:, t % 2, own],
                                  wi_hi[:, bass.ds(e * F, F)], wi_lo[:, bass.ds(e * F, F)], False, j == J - 1)
                ins.then_inc(h_done, 1)

            of_tile = {}

            def l0_turn(t):
                pe.wait_ge(gel_ready, t + 1)
                if t >= 2:
                    pe.wait_ge(hm_lo_ready, t - 1)
                for c in range(C):
                    ins = pe.transpose(bank[T_BANK[t % 2]][:, c * P:(c + 1) * P], gel[:, t % 2, c * P:(c + 1) * P], ident)
                ins.then_inc(t_done, 1)

            def l0_down(t):
                o = bank[O_BANK[t % 2]]
                pe.wait_ge(hm_lo_ready, t + 1)
                if t >= 2:
                    pe.wait_ge(o_read, t - 1)
                else:
                    pe.wait_ge(wo_lo_ready, 2)
                    pe.wait_ge(wo_lo_dve, 2)
                mm(o[:, :], onehot[:, t * P:(t + 1) * P], table[:, F:TABLE], True, False)
                for j, e in enumerate(of_tile[t]):
                    own = slice(j * P, (j + 1) * P)
                    for c in range(C):
                        at = e * (2 * F) + c * 2 * P
                        mm(o[:, 0:2 * D], hm_hi[:, c, own], wo_flat[:, bass.ds(at, 2 * P)], False, False)
                        ins = mm(o[:, 0:D], hm_lo[:, c, own], wo_flat[:, bass.ds(at, P)], False,
                                 j == J - 1 and c == C - 1)
                ins.then_inc(o_done, 1)

            wo_flat = wo_hl[:, :, :, :].rearrange("p c h d -> p (c h d)")

            def l2_turn(t):
                pe.wait_ge(nrm_ready, t + 1)
                pe.transpose(bank[NT_BANK[t // 4]][:, t % 4 * P:t % 4 * P + P], nrm_tm[:, t, :], ident)\
                    .then_inc(nt_done, 1)

            def logits(hv):
                pe.wait_ge(hf_ready, hv + 1)
                for i in range(4):
                    ins = mm(bank[NT_BANK[hv]][:, i * E:(i + 1) * E], hf[:, i * P:(i + 1) * P], small("router_w"))
                ins.then_inc(logits_done, 1)

            def gates_turn(hv):
                pe.wait_ge(comb_ready, hv + 1)
                for i in range(4):
                    ins = pe.transpose(bank[NT_BANK[hv]][0:K2, i * P:(i + 1) * P], comb_hl[:, i, :], ident)
                ins.then_inc(comb_done, 1)

            def gates_wide(n):
                hv, e = divmod(n, E)
                pe.wait_ge(comb_t_ready, hv + 1)
                if n >= 2:
                    pe.wait_ge(gated, (n - 1) * C)
                else:
                    pe.wait_ge(o_read, T - 1 + n)
                mm(bank[GATE_BANK[n % 2]][:, :], pick[:, e:e + 1].broadcast_to([K2, P]),
                   comb_t[:, hv * HALF:(hv + 1) * HALF]).then_inc(combb_done, 1)

            def y_bias(hv):
                pe.wait_ge(comb_t_ready, hv + 1)
                mm(bank[Y_BANK[hv]][:, :], small("exp_b2", K2), comb_t[:, hv * HALF:(hv + 1) * HALF].bitcast(F32),
                   True, False)

            def moe_up(q):
                hv, e, c = q // C // E, q // C % E, q % C
                w, x = slice(e * F + c * P, e * F + (c + 1) * P), slice(hv * HALF, (hv + 1) * HALF)
                pe.wait_ge(hf_lo_ready, hv + 1)
                pe.wait_ge(w1_lo_ready, e + 1)
                if q >= 3:
                    pe.wait_ge(relu_ready, q - 2)
                product(bank[HID_BANK[q % 3]][:, :], w1_hi[:, w], w1_lo[:, w], hf_hi[:, x], hf_lo[:, x], True, True)\
                    .then_inc(s1_done, 1)

            def moe_down(q):
                hv, e, c = q // C // E, q // C % E, q % C
                pe.wait_ge(gated, q + 1)
                last = e == E - 1 and c == C - 1
                ins = mm(bank[Y_BANK[hv]][:, :], w2[:, e * F + c * P:e * F + (c + 1) * P], act_g[:, q % 3, :],
                         False, last)
                ins.then_inc(s2_done, 1)

            def y_turn(hv):
                pe.wait_ge(y_ready, hv + 1)
                for i in range(4):
                    t = 4 * hv + i
                    ins = pe.transpose(bank[YTM_BANK[hv]][:, i * P:(i + 1) * P], y_t[:, t * P:(t + 1) * P], ident)
                ins.then_inc(ytm_done, 1)

            def n3_turn(hv):
                pe.wait_ge(nrm_ready, T + 4 * hv + 4)
                for i in range(4):
                    ins = pe.transpose(bank[N3_BANK[hv]][:, i * P:(i + 1) * P], nrm_tm[:, 4 * hv + i, :], ident)
                ins.then_inc(nt3_done, 1)

            def queries(hv):
                pe.wait_ge(d_late, 16)
                pe.wait_ge(x3_ready, hv + 1)
                mm(bank[Q_BANK[hv]][:, :], lt("wq"), x3_t[:, hv * HALF:(hv + 1) * HALF]).then_inc(q_done, 1)

            def keys(hv):
                mm(bank[K_BANK[hv]][:, :], lt("wk"), x3_t[:, hv * HALF:(hv + 1) * HALF]).then_inc(k_done, 1)

            def values(hv, i):
                pe.wait_ge(x3_rep1_ready if hv else x3_rep0_ready, 1)
                pe.wait_ge(qx_ready, H4 * (hv + 1))
                pe.wait_ge(k_ready, hv + 1)
                if i >= 2:
                    pe.wait_ge(v_ready, 4 * hv + i - 1)
                for k in range(4):
                    ins = mm(bank[V_BANK[hv][i % 2]][:, k * P:(k + 1) * P], x3_rep[hv][:, 4 * i + k, :, :], lt("wv"))
                ins.then_inc(v_done, 1)

            def scores(hv, hg, part=None):
                n = hv * HG + hg
                if hv == 0 and hg >= 2:
                    pe.wait_ge(score_read, n - 1)
                else:
                    pe.wait_ge(v_ready, 4 * hv + 4)
                f = slice(hg * 32, hg * 32 + 32)
                lo, hi = (0, BH) if part is None else (part * BH // 2, (part + 1) * BH // 2)
                for i in range(lo, hi):
                    k0 = (hv * BH + i) * S
                    ins = mm(bank[SCORE_BANK[hv][hg]][:, i * S:(i + 1) * S], qx[hv][f, i, :, :], k_t[f, k0:k0 + S])
                if part != 0:
                    ins.then_inc(score_done, 1)

            def context(hv, hg):
                if hv:
                    pe.wait_ge(ffn_ready, C)
                else:
                    pe.wait_ge(score_read, HG)
                f = slice(hg * 32, hg * 32 + 32)
                pe.wait_ge(pt_ready, hv * HG + hg + 1)
                for i in range(BH):
                    mm(bank[CTX_BANK[hv]][f, i * S:(i + 1) * S], vb[hv][:, i, f], pt[hv][:, hg, i, :])
                ins = mm(bank[SUM_BANK[hv]][f, :], lt("block", 0, 32), pt[hv][:, hg, :, :])
                if hg == HG - 1:
                    ins.then_inc(ctx_done, 1)

            def project(hv):
                pe.wait_ge(ctx_ready, hv + 1)
                if hv:
                    pe.wait_ge(score_read, 2 * HG)
                else:
                    pe.wait_ge(gated, 2 * E * C)
                mm(bank[WO_BANK[hv]][:, :], lt("wo"), ctx_t[:, hv * HALF:(hv + 1) * HALF]).then_inc(wo_done, 1)

            def x4_turn(hv):
                pe.wait_ge(x4_ready, hv + 1)
                for i in range(4):
                    t = 4 * hv + i
                    ins = pe.transpose(bank[X4_BANK[hv]][:, i * P:(i + 1) * P], x4_t[:, t * P:(t + 1) * P], ident)
                ins.then_inc(x4tm_done, 1)

            def n4_turn(hv):
                pe.wait_ge(nrm_ready, 2 * T + 4 * hv + 4)
                for i in range(4):
                    ins = pe.transpose(bank[N4_BANK[hv]][:, i * P:(i + 1) * P], nrm_tm[:, 4 * hv + i, :], ident)
                ins.then_inc(n4_done, 1)

            def ffn_up(hv):
                pe.wait_ge(h4_ready, hv + 1)
                for c in range(C):
                    if c >= 2:
                        pe.wait_ge(ffn_ready, hv * C + c - 1)
                    else:
                        pe.wait_ge(x4_ready, hv + 1)
                    mm(bank[F1_BANK[hv][c % 2]][:, :], lt("w1", c * P, P), h_t[:, hv * HALF:(hv + 1) * HALF])\
                        .then_inc(f1_done, 1)

            def ffn_down(hv):
                pe.wait_ge(ffn_ready, hv * C + C)
                pe.wait_ge(x4_tm_ready, hv + 1)
                for i in range(4):
                    for c in range(C):
                        ins = mm(bank[F2_BANK[hv]][:, i * P:(i + 1) * P], ffn_h[hv][:, c, i * P:(i + 1) * P],
                                 lt("w2", c * P, P), c == 0, c == C - 1)
                ins.then_inc(f2_done, 1)

            pe.wait_ge(zeroed, 4)
            l0_up(0)
            for t in range(T):
                l0_turn(t)
                if t + 1 < T:
                    l0_up(t + 1)
                if 2 <= t < T - 1:
                    l2_turn(t - 2)
                if t == T - 1:
                    logits(0)
                l0_down(t)
            MOE = 2 * E * C
            R1 = E * C
            LAG = 2
            pe.wait_ge(d_w2, 16)
            for q in range(MOE + LAG):
                if q < MOE:
                    if q == R1:
                        y_bias(1)
                    moe_up(q)
                    if q == 0:
                        gates_turn(0)
                    if q == 1:
                        y_bias(0)
                        gates_wide(0)
                    if q % C == 0 and q:
                        gates_wide(q // C)
                if q >= LAG:
                    moe_down(q - LAG)
                if q == 1:
                    l2_turn(T - 3)
                if q == 2:
                    l2_turn(T - 2)
                if q == 6:
                    l2_turn(T - 1)
                if q == 16:
                    logits(1)
                if q == 27:
                    gates_turn(1)
                if q == R1 + 3:
                    y_turn(0)
                if q == R1 + 8:
                    n3_turn(0)
                if q == R1 + 11:
                    queries(0)
                if q == R1 + 12:
                    keys(0)
                if R1 + 15 <= q < R1 + 19:
                    values(0, q - R1 - 15)
                if R1 + 19 <= q < R1 + 27:
                    scores(0, (q - R1 - 19) // 2, (q - R1 - 19) % 2)
                if R1 + 30 <= q:
                    context(0, q - R1 - 30)
            y_turn(1)
            n3_turn(1)
            project(0)
            queries(1)
            keys(1)
            x4_turn(0)
            for i in range(4):
                values(1, i)
            n4_turn(0)
            scores(1, 0)
            scores(1, 1)
            ffn_up(0)
            scores(1, 2)
            scores(1, 3)
            ffn_down(0)
            for hg in range(HG):
                context(1, hg)
            project(1)
            x4_turn(1)
            n4_turn(1)
            ffn_up(1)
            ffn_down(1)


def laid_out(i):
    f32 = np.float32

    def columns(parts, layout_of, width, rows=P):
        a = np.zeros((rows, width), f32)
        for name, v in parts.items():
            lo, hi = layout_of[name]
            a[:v.shape[0], lo:hi] = v
        return a

    def vectors(*arrays):
        out = []
        for v in arrays:
            v = v.reshape(-1, min(v.shape[-1], P)).T
            out.append(np.concatenate([v, np.zeros((P - v.shape[0], v.shape[1]), f32)]))
        return np.concatenate(out, axis=1)

    def chunked(w):
        w = w.reshape(-1, C, P, D)
        return np.ascontiguousarray(w.transpose(2, 0, 1, 3).reshape(P, -1))

    x = np.asarray(i["x"]).reshape(N, D)
    row = np.arange(P)
    expert_row = np.where(row < E, row, np.where((row >= LO) & (row < K2), row - LO, -1))
    half = D // 2
    freqs = np.exp(np.arange(half, dtype=f32) * f32(-np.log(10000.0) / (half - 1)))
    turn = np.zeros((P, ANG), f32)
    turn[half:, :B] = 0.25
    turn[:, B + 1::2] = 0.25
    exp_b2 = np.zeros((K2, P), f32)
    exp_b2[0:E] = exp_b2[LO:K2] = i["L2_cond_exp_b2"]
    early = columns({
        "ident": np.eye(P, dtype=f32), "expert_row": expert_row[:, None], "sample_row": row[:, None],
        "freq": np.concatenate([freqs, freqs])[:, None], "turn": turn, "quarter": (turn * 4 * (np.pi / 2)).astype(f32),
        "prefer": np.tile(E - np.arange(E), (P, 1)), "pick": (expert_row[:, None] == np.arange(E)),
        "angles": np.stack([i["condB_theta"], i["condB_phi"]], axis=1),
        "cols": vectors(i["L2_cond_exp_b1"], i["L3_cond_b1"], i["L2_cond_ln_g"], i["L2_cond_ln_b"],
                        i["L2_cond_hyp_b1"], i["L2_cond_hyp_b2"], i["L2_cond_sty_b1"], i["L2_cond_sty_b2"],
                        i["L3_cond_b_ada"], i["L3_cond_bq"], i["L3_cond_bk"], i["L3_cond_bv"], i["L3_cond_bo"],
                        i["L3_cond_g2"], i["L3_cond_beta2"]),
        "subj_emb": i["L2_cond_subj_emb"], "hyp_w1": i["L2_cond_hyp_w1"], "hyp_w2": i["L2_cond_hyp_w2"],
        "sty_w1": i["L2_cond_sty_w1"], "sty_w2": i["L2_cond_sty_w2"], "w_ada": i["L3_cond_W_ada"],
        "router_w": i["L2_cond_router_w"], "exp_b2": exp_b2}, EARLY, EARLY_W)
    head = (row[:, None] % 32 // DH == np.arange(H4)) * f32(1.0 / np.sqrt(DH))
    block = np.tile(row[:, None] // 32 == np.arange(32) // DH, (1, HG))
    late = columns({
        "head": head, "block": block, "wq": i["L3_cond_Wq"], "wk": i["L3_cond_Wk"], "wv": i["L3_cond_Wv"],
        "wo": i["L3_cond_Wo"], "w1": i["L3_cond_W1"], "w2": chunked(i["L3_cond_W2"]),
        "b2": np.tile(i["L3_cond_b2"], (P, 1))}, LATE, LATE_W)
    tables = np.zeros((K2, TABLE), f32)
    tables[0:E] = tables[LO:K2] = np.concatenate(
        [i["L0_cond_bi"], i["L0_cond_bo"], np.zeros((E, D), f32), i["L0_cond_gamma"], i["L0_cond_beta"]], axis=1)
    ids = np.concatenate([i["itok_B_0_7"], i["itok_B_6_14"], i["itok_B_34_63"]]).astype(np.int32)
    wide = lambda w: np.ascontiguousarray(w.transpose(1, 0, 2).reshape(P, -1))
    return {
        "x_tm": np.ascontiguousarray(x.reshape(T, P, D).transpose(1, 0, 2)), "x_t": np.ascontiguousarray(x.T),
        "ids": np.tile(ids, (P, 1)), "early": early, "late": late, "tables": tables,
        "wi": wide(i["L0_cond_Wi"]), "wo": chunked(i["L0_cond_Wo"]),
        "w1": wide(i["L2_cond_exp_w1"]), "w2": chunked(i["L2_cond_exp_w2"]),
        "fside": np.ascontiguousarray(i["fside_Bx16xSxS_0"].reshape(2, BH, HG, H4, S, S).transpose(3, 4, 0, 2, 1, 5)
                                      .reshape(P, 2, HG, BH, S)),
        "mask": np.tile(i["mask_Bx1xSxS_bk0"].reshape(B, S, S).transpose(1, 0, 2).reshape(S, B * S), (H4, 1)),
    }


def kernel(**inputs):
    import concourse.bacc as bacc
    from concourse.bass_utils import run_bass_kernel_spmd

    nc = bacc.Bacc("TRN2", target_bir_lowering=False, num_devices=1)
    arrays = laid_out({k: np.asarray(v) for k, v in inputs.items()})
    args = [nc.dram_tensor(f"in_{k}", a.shape, mybir.dt.from_np(a.dtype), kind="ExternalInput").ap()
            for k, a in arrays.items()]
    out = nc.dram_tensor("out", (P, T, D), F32, kind="ExternalOutput").ap()
    build(nc, *args, out)
    r = run_bass_kernel_spmd(nc, [{f"in_{k}": a for k, a in arrays.items()}], core_ids=[0])
    got = r.results[0]["out"]
    return got.transpose(1, 0, 2).reshape(B, S, D)
```

```python
from contextlib import ExitStack

import concourse.bass as bass
import numpy as np
from concourse import mybir

F32 = mybir.dt.float32
F32R = mybir.dt.float32r
I32 = mybir.dt.int32
U8 = mybir.dt.uint8
ACT = mybir.ActivationFunctionType
ALU = mybir.AluOpType
AX = mybir.AxisListType

P = 128
B, S, D = 32, 32, 128
N = B * S
T = N // P
J = P // S
E = 8
F = 512
C = F // P
H, DH = 16, 8
HG, H4 = 4, 4
SCALE = DH ** -0.5
HALF = N // 2
BH = B // 2
BANK = 512
LO = 32
LAG, SLOTS = 3, 4
DIGIT = 3
K2 = LO + E
MASKED = P + S
TWO_PI_INV = float(np.float32(1.0 / (2.0 * np.pi)))
TWO_PI_A = 6.28125
TWO_PI_B = 0.0019350051879882812
TWO_PI_C = float(2.0 * np.pi - 6.28125 - 0.0019350051879882812)
ROUND = 12582912.0
MASKED_SCORE = -1.0e38
PI_SAFE = 3.1415925



def layout(parts):
    at, out = 0, {}
    for name, width in parts:
        out[name] = (at, at + width)
        at += width
    return out, at


COLS, NCOLS = layout([
    ("exp_b1", E * C), ("ffn_b1", C), ("ln_g", 1), ("ln_b", 1), ("hyp_b1", 1), ("hyp_b2", 1), ("sty_b1", 1),
    ("sty_b2", 2), ("b_ada", 2), ("bq", 2), ("bk", 2), ("bv", 1), ("bo", 1), ("g2", 1), ("beta2", 1)])
ANG = B + 4
EARLY, EARLY_W = layout([
    ("ident", P), ("expert_row", 1), ("sample_row", 1), ("freq", 1), ("turn", ANG), ("quarter", ANG),
    ("prefer", E), ("pick", E), ("digit", B), ("angles", 2), ("cols", NCOLS), ("subj_emb", 64), ("hyp_w1", P), ("hyp_w2", P),
    ("sty_w1", 64), ("sty_w2", 2 * P), ("w_ada", 2 * P), ("router_w", E), ("exp_b2", P)])
LATE, LATE_W = layout([
    ("head", H4), ("block", P), ("wq", 2 * P), ("wk", 2 * P), ("wv", P), ("wo", P), ("w1", F), ("w2", F), ("b2", P)])
TABLE = F + 4 * D


def build(nc, x_tm_d, x_t_d, ids_d, early_d, late_d, tables_d, wi_d, wo_d, w1_d, w2_d, fside_d, mask_d, out_d):
    ctx = ExitStack()
    with ctx:
        free = [(nc.sbuf_base + 63) // 64 * 64]

        def sb(name, shape, dt=F32, at=None):
            size = (int(np.prod(shape[1:])) * (1 if dt == U8 else 4) + 31) // 32 * 32
            region = free if at is None else at
            offset, region[0] = region[0], region[0] + size
            return nc.alloc_sbuf_tensor_at(name, shape, dt, offset=offset)

        def sem(name):
            return ctx.enter_context(nc.semaphore(name))

        early = sb("early", [P, EARLY_W])
        ids = sb("ids", [P, 3 * B], I32)
        ids_f = sb("ids_f", [P, 3 * B])
        digits = sb("digits", [P, B])
        words_f = sb("words_f", [P, T])
        words = sb("words", [P, T], I32)
        region_x = [free[0]]
        x_t = sb("x_t", [P, N])
        rows_tm = sb("rows_tm", [P, T, D])
        nrm_tm = sb("nrm_tm", [P, T, D])
        affine = sb("affine", [P, 4, B])
        stat = sb("stat", [P, 2, 8])
        rstd = sb("rstd", [P, 2])
        stat4 = sb("stat4", [P, 4, 8])
        rstd4 = sb("rstd4", [P, 4])
        sums = sb("sums", [P, 3, BH])
        token_veps = sb("token_veps", [P, BH])
        veps, minus_half = sb("veps", [P, BH]), sb("minus_half", [P, BH])
        hf = sb("hf", [P, HALF])
        hf_hi = sb("hf_hi", [P, N], F32R)
        hf_lo = sb("hf_lo", [P, N], F32R)
        comb_t = sb("comb_t", [K2, N], F32R)
        rt = sb("rt", [P, 7, HALF // P * E])
        rt_s = sb("rt_s", [P, 8, HALF // P])
        comb_hl = sb("comb_hl", [P, HALF // P, K2])
        comb_hi = sb("comb_hi", [P, HALF // P * E], F32R)
        region_a = [free[0]]
        wi_hi = sb("wi_hi", [P, E * F], F32R)
        wi_lo = sb("wi_lo", [P, E * F], F32R)
        region_b = [free[0]]
        wo_hl = sb("wo_hl", [P, E * C, 2, P], F32R)
        region_c = [free[0]]
        xm_hi = sb("xm_hi", [P, 2, J * MASKED], F32R)
        xm_lo = sb("xm_lo", [P, 2, J * MASKED], F32R)
        hm_hi = sb("hm_hi", [P, C, J * MASKED], F32R)
        hm_lo = sb("hm_lo", [P, C, J * MASKED], F32R)
        gel = sb("gel", [P, 2, F])
        region_d = [free[0]]
        w1_hi = sb("w1_hi", [P, E * F], F32R)
        w1_lo = sb("w1_lo", [P, E * F], F32R)
        region_e = [free[0]]
        w2 = sb("w2", [P, E * F])
        region_f = [free[0]]
        stage = sb("stage", [P, 4, 1024])
        region_g = [free[0]]
        onehot = sb("onehot", [K2, N], F32R)
        table = sb("table", [K2, TABLE], F32R)
        trig = sb("trig", [P, ANG])
        rot_c = sb("rot_c", [P, T, 8])
        pick = sb("pick", [K2, E], F32R)
        turned = sb("turned", [P, D])
        row = sb("row", [P, D])
        assert free[0] <= nc.sbuf_usable_end, (free[0], nc.sbuf_usable_end)

        def region(start, end):
            at = list(start)

            def place(name, shape, dt=F32):
                t = sb(name, shape, dt, at=at)
                assert at[0] <= end[0], (name, at[0], end[0])
                return t
            return place

        stage_wo = sb("stage_wo", [P, 4, 1024], at=list(region_e))
        place = region(region_d, region_e)
        table_raw = place("table_raw", [K2, TABLE])
        ang = place("ang", [P, 3, ANG])
        rot_row = place("rot_row", [B, 8])
        subj = place("subj", [B, B])
        hyp = place("hyp", [P, 6, B])
        time_emb = place("time_emb", [P, B])
        of_sample = place("of_sample", [B, N])
        place = region(region_x, [region_x[0] + 4 * N])
        sq = place("sq", [P, HALF])
        cen = place("cen", [P, HALF])
        place = region(region_a, region_b)
        relu_r = place("relu_r", [P, SLOTS, BANK])
        gate_w = place("gate_w", [P, BANK])
        y_gated = place("y_gated", [P, BANK])
        mask_f = place("mask_f", [P, B * S])
        pt0 = place("pt0", [P, HG, BH, S])
        qx00 = place("qx00", [P, BH, H4, S], F32R)
        place = region(region_b, region_c)
        bias = place("bias", [P, 2, HG, BH, S])
        region_sc = [region_b[0] + 4 * HG * B * S]
        sc = place("sc", [P, 2, HG, BH, S])
        place = region(region_c, region_d)
        late = place("late", [P, LATE_W])
        mask = place("mask", [P, B * S], U8)
        x3_t = place("x3_t", [P, N])
        kx0 = place("kx0", [P, 2, BH, 2, S], F32R)
        ctx_t = place("ctx_t", [P, N])
        x4_t = place("x4_t", [P, N])
        h_t = place("h_t", [P, N])
        y_t = h_t
        q_t = [ctx_t, x4_t]
        place = region(region_f, region_g)
        vb0 = place("vb0", [P, BH, P])
        qx01 = place("qx01", [P, BH, H4, S], F32R)
        place = region(region_d, region_e)
        pt = [pt0, place("pt1", [P, HG, BH, S])]
        qx = [(qx00, qx01), (place("qx10", [P, BH, H4, S], F32R), place("qx11", [P, BH, H4, S], F32R))]
        vb = [vb0, place("vb1", [P, BH, P])]
        place = region(region_e, region_f)
        kx = [kx0, place("kx1", [P, 2, BH, 2, S], F32R)]
        x4_tm = place("x4_tm", [P, T, D])
        ffn_h = [sb(f"ffn_h{hv}", [P, C, HALF], at=[region_sc[0] + hv * 4 * C * HALF]) for hv in range(2)]
        out_tm = sb("out_tm", [P, T, D], at=list(region_b))
        smax = sb("smax", [P, 2 * HG, BH])
        wo_bias = sb("wo_bias", [P, 1])
        recip = sb("recip", [P, HALF], at=list(region_x))
        assert free[0] <= nc.sbuf_usable_end, (free[0], nc.sbuf_usable_end)

        bank = [ctx.enter_context(nc.psum_tensor(f"bank{i}", [P, BANK], F32)) for i in range(8)]

        ident = early[:, EARLY["ident"][0]:EARLY["ident"][1]]

        def small(name, rows=P, k=0, n=None):
            a, b = EARLY[name]
            return early[0:rows, a + k:(a + k + n if n else b)]

        def col(name, k=0, rows=P):
            a = EARLY["cols"][0] + COLS[name][0] + k
            return early[0:rows, a:a + 1]

        def lt(name, k=0, n=None):
            a, b = LATE[name]
            return late[:, a + k:(a + k + n if n else b)]

        def per_sample(a):
            return a.unsqueeze(2).broadcast_to([a.shape[0], a.shape[1], S])

        def by_sample(a):
            return a.rearrange("p (b s) -> p b s", s=S)

        def diag(a):
            if len(a.shape) == 3:
                return a.rearrange("p c (j u) -> p c j u", u=MASKED)[:, :, :, 0:S]
            return a.rearrange("p (j u) -> p j u", u=MASKED)[:, :, 0:S]

        def by_chunk(a):
            return a.rearrange("p (c j s) -> p c j s", j=J, s=S)

        def by_tile(a):
            return a.rearrange("p (t d) -> p t d", d=P)


        d_ids, d_early, d_table, d_xt, d_xtm = sem("d_ids"), sem("d_early"), sem("d_table"), sem("d_xt"), sem("d_xtm")
        d_wi = [sem(f"d_wi{k}") for k in range(4)]
        d_wo = [sem(f"d_wo{k}") for k in range(4)]
        d_w1 = [sem(f"d_w1{k}") for k in range(4)]
        d_w2, d_late, d_mask, d_bias, d_out = sem("d_w2"), sem("d_late"), sem("d_mask"), sem("d_bias"), sem("d_out")
        dve_link = sem("dve_link")
        onehot_ready, table_ready, subj_ready = sem("onehot_ready"), sem("table_ready"), sem("subj_ready")
        of_sample_ready = sem("of_sample_ready")
        angles_ready, rot_row_ready = sem("angles_ready"), sem("rot_row_ready")
        affine_ready, words_ready = sem("affine_ready"), sem("words_ready")
        setup_done, wo_bias_ready, wo_bias_done = sem("setup_done"), sem("wo_bias_ready"), sem("wo_bias_done")
        wi_lo_pool = sem("wi_lo_pool")
        wi_lo_ready, wo_lo_dve = sem("wi_lo_ready"), sem("wo_lo_dve")
        xm_ready, hm_lo_ready, o_read, var_ready = sem("xm_ready"), sem("hm_lo_ready"), sem("o_read"), sem("var_ready")
        nrm_ready = sem("nrm_ready")
        var4_ready, rstd4_ready = sem("var4_ready"), sem("rstd4_ready")
        softplus_in, gates_z, cen_ready, svar_ready = sem("softplus_in"), sem("gates_z"), sem("cen_ready"), sem("svar_ready")
        hf_ready, hf_lo_ready, comb_ready = sem("hf_ready"), sem("hf_lo_ready"), sem("comb_ready")
        z_ready, y_ready = sem("z_ready"), sem("y_ready")
        x3_ready, q_lo_ready, score_read = sem("x3_ready"), sem("q_lo_ready"), sem("score_read")
        k_lo_ready, qx_dve_ready = sem("k_lo_ready"), sem("qx_dve_ready")
        smax_ready, pt_ready, recip_ready, ctx_div, x4_ready = sem("smax_ready"), sem("pt_ready"), sem("recip_ready"), sem("ctx_div"), sem("x4_ready")
        x4_tm_ready, out_ready = sem("x4_tm_ready"), sem("out_ready")
        act_link = sem("act_link")
        trig_ready, time_ready, hyp_ready = sem("trig_ready"), sem("time_ready"), sem("hyp_ready")
        softplus_ln = sem("softplus_ln")
        wi_hi_ready, wo_hi_ready, w1_hi_ready = sem("wi_hi_ready"), sem("wo_hi_ready"), sem("w1_hi_ready")
        gel_ready, hm_hi_ready, h_ready, sq_ready = sem("gel_ready"), sem("hm_hi_ready"), sem("h_ready"), sem("sq_ready")
        hf_hi_ready, gates_e, comb_t_ready, relu_ready = sem("hf_hi_ready"), sem("gates_e"), sem("comb_t_ready"), sem("relu_ready")
        y_init, gate_ready, exp_ready = sem("y_init"), sem("gate_ready"), sem("exp_ready")
        q_hi_ready, qx_act_ready, k_hi_ready, v_ready = sem("q_hi_ready"), sem("qx_act_ready"), sem("k_hi_ready"), sem("v_ready")
        h4_ready, ffn_ready = sem("h4_ready"), sem("ffn_ready")
        zeroed, wo_lo_ready, w1_lo_ready = sem("zeroed"), sem("wo_lo_ready"), sem("w1_lo_ready")
        rstd_ready, srstd_ready, pool_link, bias_ready = sem("rstd_ready"), sem("srstd_ready"), sem("pool_link"), sem("bias_ready")
        sub_ready, v_zeroed = sem("sub_ready"), sem("v_zeroed")
        rot_done, hyp_done, ada_done = sem("rot_done"), sem("hyp_done"), sem("ada_done")
        h_done, t_done, o_done, nt_done = sem("h_done"), sem("t_done"), sem("o_done"), sem("nt_done")
        logits_done, comb_done, combb_done, s1_done = sem("logits_done"), sem("comb_done"), sem("combb_done"), sem("s1_done")
        y_bias_done = sem("y_bias_done")
        s2_done = sem("s2_done")
        ytm_done, nt3_done, q_done, k_done = sem("ytm_done"), sem("nt3_done"), sem("q_done"), sem("k_done")
        v_done, score_done, sums_done, ctx_done, wo_done = sem("v_done"), sem("score_done"), sem("sums_done"), sem("ctx_done"), sem("wo_done")
        x4tm_done, n4_done, f1_done, f2_done = sem("x4tm_done"), sem("n4_done"), sem("f1_done"), sem("f2_done")

        H_BANK, T_BANK, O_BANK, NT_BANK = (0, 1), (2, 3), (4, 5), (6, 7)
        HID_BANK, GATE_BANK, Y_BANK = (0, 1, 3), (6, 5), ((2, 4), (7, 4))
        YTM_BANK, N3_BANK = (2, 0), (6, 1)
        ACT_HEADS = (0, 1)
        Q_BANK, K_BANK, V_BANK = ((2, 2), (3, 0)), ((6, 6), (4, 1)), (2, 0)
        SCORE_BANK, SUM_BANK, CTX_BANK = ((2, 6) * HG, (3, 4, 7, 3, 4, 7, 3, 4)), (5, 2), ((2, 6), (7, 3))
        WO_BANK, X4_BANK, N4_BANK = (5, 4), (6, 0), (1, 1)
        F1_BANK, F2_BANK = (5, 6), (2, 7)

        MOE = 2 * E * C
        R1 = E * C

        block = ctx.enter_context(nc.Block())

        @block.sync
        def _(sp):
            sp.dma_start(ids[:, :], ids_d).then_inc(d_ids, 16)
            sp.dma_start(early[:, :], early_d).then_inc(d_early, 16)
            for k in range(4):
                sp.dma_start(stage[:, k, :], wi_d[:, k * 1024:(k + 1) * 1024]).then_inc(d_wi[k], 16)
                if k == 0:
                    sp.dma_start(x_t[:, :], x_t_d).then_inc(d_xt, 16)
                if k == 2:
                    sp.dma_start(table_raw[:, :], tables_d).then_inc(d_table, 16)
            for k in range(4):
                sp.dma_start(stage_wo[:, k, :], wo_d[:, k * 1024:(k + 1) * 1024]).then_inc(d_wo[k], 16)
            sp.dma_start(rows_tm[:, :, :], x_tm_d).then_inc(d_xtm, 16)
            for k in range(4):
                sp.wait_ge(wi_lo_pool if k == 1 else wi_lo_ready, (1, 1, 2, 3)[k])
                sp.dma_start(stage[:, k, :], w1_d[:, k * 1024:(k + 1) * 1024]).then_inc(d_w1[k], 16)
            sp.wait_ge(wo_lo_ready, 2)
            sp.wait_ge(wo_lo_dve, 2)
            sp.dma_start(w2[:, :], w2_d).then_inc(d_w2, 16)
            sp.wait_ge(o_done, T)
            sp.dma_start(mask[:, :], mask_d).then_inc(d_mask, 16)
            sp.dma_start(bias[:, :, :, :, :], fside_d).then_inc(d_bias, 16)
            sp.dma_start(late[:, :], late_d).then_inc(d_late, 16)
            for hv in range(2):
                sp.wait_ge(out_ready, hv + 1)
                sp.dma_start(out_d[:, hv * 4:hv * 4 + 4, :], out_tm[:, hv * 4:hv * 4 + 4, :]).then_inc(d_out, 16)
            sp.wait_ge(d_out, 32)

        @block.gpsimd
        def _(pool):
            def link(ins):
                link.n += 1
                ins.then_inc(pool_link, 1)
                pool.wait_ge(pool_link, link.n)
            link.n = 0

            pool.memset(xm_hi[:, :, :].bitcast(F32), 0.0).then_inc(zeroed, 1)
            pool.memset(xm_lo[:, :, :].bitcast(F32), 0.0).then_inc(zeroed, 1)
            pool.wait_ge(d_early, 16)
            pool.tensor_copy(by_sample(of_sample[:, :]), ident[0:B, 0:B].unsqueeze(2).broadcast_to([B, B, S]))\
                .then_inc(of_sample_ready, 1)
            pool.memset(hm_hi[:, :, :].bitcast(F32), 0.0).then_inc(zeroed, 1)
            pool.memset(hm_lo[:, :, :].bitcast(F32), 0.0).then_inc(zeroed, 1)
            link(pool.memset(minus_half[:, :], -0.5))
            pool.wait_ge(wi_hi_ready, 2)
            pool.tensor_tensor(wi_lo[:, 1024:2048], stage[:, 1, :], wi_hi[:, 1024:2048].bitcast(F32), ALU.subtract)\
                .then_inc(wi_lo_pool, 1)
            for k in (1, 3):
                w = slice(k * E, (k + 1) * E)
                pool.wait_ge(wo_hi_ready, k + 1)
                pool.tensor_tensor(wo_hl[:, w, 1, :], by_tile(stage_wo[:, k, :]), wo_hl[:, w, 0, :].bitcast(F32),
                                   ALU.subtract).then_inc(wo_lo_ready, 1)

            def power(out, in_, eps, ready, shifted=veps):
                n = in_.shape[1]
                link(pool.tensor_scalar(shifted[:, 0:n], in_, eps, None, ALU.add))
                pool.tensor_tensor(out, shifted[:, 0:n], minus_half[:, 0:n], ALU.pow).then_inc(ready, 1)

            def w1_lo_part(p):
                w = slice(p * F, (p + 1) * F)
                pool.wait_ge(w1_hi_ready, p + 1)
                pool.tensor_tensor(w1_lo[:, w], stage[:, p // 2, p % 2 * F:p % 2 * F + F],
                                   w1_hi[:, w].bitcast(F32), ALU.subtract).then_inc(w1_lo_ready, 1)

            def token_norm(hv):
                pool.wait_ge(svar_ready, hv + 1)
                power(sums[:, 2, :], sums[:, 1, :], 1e-8, srstd_ready, token_veps)

            def row_norm(t, n):
                pool.wait_ge(var_ready, 2 * t + n + 1)
                power(rstd[:, n:n + 1], stat[:, n, 7:8], (1e-12, 1e-5)[n], rstd_ready)

            for t in range(T - 2):
                row_norm(t, 0)
                row_norm(t, 1)
                if t < 4:
                    w1_lo_part(2 * t)
                    w1_lo_part(2 * t + 1)
                if t == 4:
                    token_norm(0)

            def mask_scores():
                pool.wait_ge(d_mask, 16)
                link(pool.tensor_scalar(mask_f[:, :], mask[:, :], MASKED_SCORE, None, ALU.mult))

            def add_mask(hv, hg):
                pool.wait_ge(d_bias, 16)
                a = bias[:, hv, hg, :, :]
                pool.tensor_tensor(a, a, by_sample(mask_f[:, hv * HALF:(hv + 1) * HALF]), ALU.add).then_inc(bias_ready, 1)

            def norms(n):
                pool.wait_ge(var4_ready, n + 1)
                power(rstd4[:, :], stat4[:, :, 7], 1e-5, rstd4_ready)

            def subtract(hv, hg):
                n = hv * HG + hg
                pool.wait_ge(smax_ready, 2 * n + 2)
                a = sc[:, hv, hg, :, :]
                pool.tensor_tensor(a, a, per_sample(smax[:, n, :]), ALU.subtract).then_inc(sub_ready, 1)

            for q in range(MOE):
                if q in (1, 2, 5, 6):
                    row_norm(T - 2 + q // 4, (q - 1) % 4)
                if q == 16:
                    token_norm(1)
                if q == 18:
                    pool.memset(vb[0][:, :, :], 0.0).then_inc(v_zeroed, 1)
                if q == 20:
                    mask_scores()
                if q in (22, 24, 26, 28):
                    add_mask(0, (q - 22) // 2)
                if q == R1 + 6:
                    norms(0)
                if q in range(R1 + 20, R1 + 28, 2):
                    add_mask(1, (q - R1 - 20) // 2)
                if q in range(R1 + 24, R1 + 32, 2):
                    subtract(0, (q - R1 - 24) // 2)
            pool.wait_ge(s1_done, MOE)
            pool.memset(vb[1][:, :, :], 0.0).then_inc(v_zeroed, 1)
            norms(1)
            for hg in range(HG):
                subtract(1, hg)
            norms(2)
            norms(3)

        @block.scalar
        def _(act):
            def wi_part(k):
                w = slice(k * 1024, (k + 1) * 1024)
                act.wait_ge(d_wi[k], 16)
                act.activation(wi_hi[:, w], stage[:, k, :], ACT.Copy).then_inc(wi_hi_ready, 1)

            def wo_part(k):
                act.wait_ge(d_wo[k], 16)
                act.activation(wo_hl[:, k * E:(k + 1) * E, 0, :], by_tile(stage_wo[:, k, :]), ACT.Copy)\
                    .then_inc(wo_hi_ready, 1)

            act.wait_ge(angles_ready, 1)
            act.activation(trig[:, :], ang[:, 0, :], ACT.Sin).then_inc(trig_ready, 1)
            act.wait_ge(trig_ready, 1)
            act.activation(time_emb[:, :], trig[:, 0:B], ACT.Silu).then_inc(time_ready, 1)
            b7 = bank[7]
            wi_part(0)
            act.wait_ge(hyp_done, 1)
            act.activation(hyp[0:64, 0, :], b7[0:64, 0:32], ACT.Copy).then_inc(hyp_ready, 1)
            wi_part(1)
            act.wait_ge(hyp_done, 2)
            act.activation(hyp[:, 1, :], b7[:, 32:64], ACT.Relu, bias=col("hyp_b1")).then_inc(hyp_ready, 1)
            wi_part(2)
            act.wait_ge(hyp_done, 3)
            act.activation(hyp[:, 2, :], b7[:, 64:96], ACT.Identity, bias=col("hyp_b2")).then_inc(hyp_ready, 1)
            wi_part(3)
            act.wait_ge(hyp_done, 4)
            act.activation(hyp[0:64, 3, :], b7[0:64, 96:128], ACT.Relu, bias=col("sty_b1", rows=64)).then_inc(hyp_ready, 1)
            for k in range(4):
                wo_part(k)
            act.wait_ge(softplus_in, 1)
            act.activation(hyp[:, 5, :], hyp[:, 5, :], ACT.Exp).then_inc(act_link, 1)
            act.wait_ge(act_link, 1)
            act.activation(hyp[:, 5, :], hyp[:, 5, :], ACT.Ln, bias=1.0).then_inc(softplus_ln, 1)

            def gelu(t):
                act.wait_ge(h_done, t + 1)
                if t >= 2:
                    act.wait_ge(t_done, t - 1)
                act.activation(gel[:, t % 2, :], bank[H_BANK[t % 2]][:, :], ACT.Gelu).then_inc(gel_ready, 1)

            def w1_part(p):
                if p == 0:
                    act.wait_ge(setup_done, 1)
                act.wait_ge(d_w1[p // 2], 16)
                act.activation(w1_hi[:, p * F:(p + 1) * F], stage[:, p // 2, p % 2 * F:p % 2 * F + F],
                               ACT.Copy).then_inc(w1_hi_ready, 1)

            def layer_scale(hv):
                act.wait_ge(nt_done, 4 * hv + 4)
                if hv:
                    act.wait_ge(hf_ready, 1)
                else:
                    act.wait_ge(xm_ready, T)
                act.activation(cen[:, :], bank[NT_BANK[hv]][:, :], ACT.Identity,
                               scale=col("ln_g"), bias=col("ln_b")).then_inc(h_ready, 1)

            def squares(hv):
                act.wait_ge(cen_ready, hv + 1)
                act.activation(sq[:, :], cen[:, :], ACT.Square).then_inc(sq_ready, 1)

            def hf_high(hv):
                act.wait_ge(hf_ready, hv + 1)
                act.activation(hf_hi[:, hv * HALF:(hv + 1) * HALF], hf[:, :], ACT.Copy).then_inc(hf_hi_ready, 1)

            def router_exp(hv):
                act.wait_ge(gates_z, hv + 1)
                act.activation(rt[:, 1, :], rt[:, 0, :], ACT.Exp).then_inc(gates_e, 1)

            def gates_copy(hv):
                act.wait_ge(comb_done, hv + 1)
                act.activation(comb_t[:, hv * HALF:(hv + 1) * HALF], bank[NT_BANK[hv]][0:K2, :], ACT.Copy)\
                    .then_inc(comb_t_ready, 1)

            def relu(q):
                e, c = q // C % E, q % C
                act.wait_ge(s1_done, q + 1)
                if q >= SLOTS:
                    act.wait_ge(s2_done, q - SLOTS + 1)
                act.activation(relu_r[:, q % SLOTS, :], bank[HID_BANK[q % 3]][:, :], ACT.Relu,
                               bias=col("exp_b1", e * C + c)).then_inc(relu_ready, 1)

            def y_start(hv):
                act.wait_ge(y_bias_done, hv + 1)
                act.activation(y_t[:, hv * HALF:(hv + 1) * HALF], bank[NT_BANK[hv]][:, :], ACT.Copy).then_inc(y_init, 1)

            def gate_copy(n):
                act.wait_ge(combb_done, n + 1)
                if n:
                    act.wait_ge(z_ready, n)
                act.activation(gate_w[:, :], bank[GATE_BANK[n // E]][:, :], ACT.Copy).then_inc(gate_ready, 1)

            def query_high(hv, st):
                act.wait_ge(q_done, 2 * hv + st + 1)
                act.wait_ge(d_late, 16)
                act.activation(q_t[st][:, hv * HALF:(hv + 1) * HALF].bitcast(F32R), bank[Q_BANK[hv][st]][:, :],
                               ACT.Identity, bias=col("bq", st)).then_inc(q_hi_ready, 1)

            def queries_by_head(hv, st):
                act.wait_ge(q_lo_ready, 2 * (2 * hv + st + 1))
                for h4 in ACT_HEADS:
                    act.activation(qx[hv][st][:, :, h4, :], by_sample(q_t[st][:, hv * HALF:(hv + 1) * HALF]),
                                   ACT.Copy, scale=lt("head", h4, 1)).then_inc(qx_act_ready, 1)

            def values(hv, h4):
                act.wait_ge(v_done, hv + 1)
                act.wait_ge(v_zeroed, hv + 1)
                f = slice(h4 * DH, h4 * DH + DH)
                out = vb[hv][S * h4:S * (h4 + 1), :, :].rearrange("p (t j) (g f) -> p j t g f", j=J, g=HG)
                ps = bank[V_BANK[hv]][:, :].rearrange("p (t g f) -> p t g f", t=4, g=HG)
                for j in range(J):
                    act.activation(out[:, j, :, :, f], ps[S * j:S * (j + 1), :, :, f], ACT.Copy).then_inc(v_ready, 1)

            def key_high(hv, st):
                act.wait_ge(k_done, 2 * hv + st + 1)
                act.wait_ge(d_late, 16)
                act.activation(kx[hv][:, st, :, 0, :], by_sample(bank[K_BANK[hv][st]][:, :]),
                               ACT.Identity, bias=col("bk", st)).then_inc(k_hi_ready, 1)

            def exps(hv, hg):
                act.wait_ge(sub_ready, hv * HG + hg + 1)
                a = sc[:, hv, hg, :, :]
                act.activation(a, a, ACT.Exp).then_inc(exp_ready, 1)

            def h4_scale(hv):
                act.wait_ge(n4_done, hv + 1)
                act.activation(h_t[:, hv * HALF:(hv + 1) * HALF], bank[N4_BANK[hv]][:, :], ACT.Identity,
                               scale=col("g2"), bias=col("beta2")).then_inc(h4_ready, 1)

            def ffn_gelu(hv, c):
                act.wait_ge(f1_done, hv * C + c + 1)
                act.activation(ffn_h[hv][:, c, :], bank[F1_BANK[c % 2]][:, :], ACT.Gelu_apprx_sigmoid,
                               bias=col("ffn_b1", c)).then_inc(ffn_ready, 1)

            gelu(0)
            for t in range(T):
                if t == 0:
                    act.wait_ge(zeroed, 4)
                act.wait_ge(t_done, t + 1)
                if t >= 1:
                    act.wait_ge(o_done, t)
                act.activation(diag(hm_hi[:, :, :]), by_chunk(bank[T_BANK[t % 2]][:, :]), ACT.Copy)\
                    .then_inc(hm_hi_ready, 1)
                if t + 1 < T:
                    gelu(t + 1)
                if t < 4:
                    w1_part(2 * t)
                    w1_part(2 * t + 1)
                if t == 5:
                    layer_scale(0)
                    squares(0)
                if t == 7:
                    hf_high(0)
                    router_exp(0)
            for q in range(MOE):
                relu(q)
                if q % C == 2 and q > C:
                    gate_copy(q // C - 1)
                if q == 1:
                    gates_copy(0)
                if q == 3:
                    y_start(0)
                if q == 12:
                    layer_scale(1)
                if q == 15:
                    squares(1)
                if q == 21:
                    hf_high(1)
                if q == 24:
                    router_exp(1)
                if q == 30:
                    gates_copy(1)
                if q == R1:
                    y_start(1)
                for st in range(2):
                    if q == R1 + 12 + 3 * st:
                        query_high(0, st)
                    if q == R1 + 13 + 3 * st:
                        key_high(0, st)
                        queries_by_head(0, st)
                if q in range(R1 + 18, R1 + 22):
                    values(0, q - R1 - 18)
                if q in range(R1 + 25, R1 + 33, 2):
                    exps(0, (q - R1 - 25) // 2)
            gate_copy(2 * E - 1)
            query_high(1, 0)
            key_high(1, 0)
            queries_by_head(1, 0)
            query_high(1, 1)
            key_high(1, 1)
            queries_by_head(1, 1)
            values(1, 0)
            values(1, 1)
            exps(1, 0)
            values(1, 2)
            values(1, 3)
            for hg in range(1, HG):
                exps(1, hg)
            h4_scale(0)
            for c in range(C):
                ffn_gelu(0, c)
            h4_scale(1)
            for c in range(C):
                ffn_gelu(1, c)

        @block.vector
        def _(dve):
            def link(ins):
                link.n += 1
                ins.then_inc(dve_link, 1)
                dve.wait_ge(dve_link, link.n)
            link.n = 0

            def then(ins, ready, value):
                ins.then_inc(ready, 1)
                dve.wait_ge(ready, value)

            dve.wait_ge(d_ids, 16)
            link(dve.tensor_copy(ids_f[:, :], ids[:, :]))
            dve.wait_ge(d_early, 16)
            link(dve.tensor_tensor(digits[:, :], ids_f[:, 0:B], small("digit"), ALU.mult))
            link(dve.tensor_reduce(words_f[:, :], digits[:, :].rearrange("p (t j) -> p t j", j=J), AX.X, ALU.add))
            dve.tensor_copy(words[:, :], words_f[:, :]).then_inc(words_ready, 1)
            link(dve.tensor_scalar(ang[:, 0, 0:B], ids_f[:, 2 * B:3 * B], 0.01, 4000.0, ALU.mult, ALU.mult))
            link(dve.tensor_scalar(ang[:, 0, 0:B], ang[:, 0, 0:B], small("freq"), None, ALU.mult))
            link(dve.tensor_copy(ang[:, 0, B:ANG].rearrange("p (a c) -> p a c", c=2),
                                 small("angles").unsqueeze(2).broadcast_to([P, 2, 2])))
            link(dve.scalar_tensor_tensor(ang[:, 1, :], ang[:, 0, :], TWO_PI_INV, small("turn"), ALU.mult, ALU.add))
            link(dve.tensor_scalar(ang[:, 1, :], ang[:, 1, :], ROUND, -ROUND, ALU.add, ALU.add))
            for part in (TWO_PI_A, TWO_PI_B, TWO_PI_C):
                link(dve.scalar_tensor_tensor(ang[:, 0, :], ang[:, 1, :], -part, ang[:, 0, :], ALU.mult, ALU.add))
            link(dve.tensor_tensor(ang[:, 0, :], ang[:, 0, :], small("quarter"), ALU.add))
            dve.tensor_scalar(ang[:, 0, :], ang[:, 0, :], PI_SAFE, -PI_SAFE, ALU.min, ALU.max).then_inc(angles_ready, 1)
            dve.tensor_scalar(by_sample(onehot[:, :]), per_sample(ids_f[0:K2, 0:B]), small("expert_row", K2), None,
                              ALU.is_equal).then_inc(onehot_ready, 1)
            dve.tensor_scalar(subj[:, :], ids_f[0:B, B:2 * B], small("sample_row", B), None,
                              ALU.is_equal).then_inc(subj_ready, 1)
            dve.tensor_copy(pick[:, :], small("pick", K2))
            dve.wait_ge(trig_ready, 1)
            sin_cos = trig[0:B, B:ANG].rearrange("p (a c) -> p a c", c=2)
            dve.tensor_copy(rot_row[:, 0:4].rearrange("p (a c) -> p a c", c=2),
                            sin_cos[:, :, 1:2].broadcast_to([B, 2, 2]))
            dve.tensor_copy(rot_row[:, 4:6], sin_cos[:, :, 0])
            dve.tensor_scalar(rot_row[:, 6:8], sin_cos[:, :, 0], -1.0, None, ALU.mult).then_inc(rot_row_ready, 1)

            def masked_x(t):
                src = x_t[:, t * P:(t + 1) * P].rearrange("p (j s) -> p j s", s=S)
                if t >= 2:
                    dve.wait_ge(h_done, t - 1)
                link(dve.tensor_copy(diag(xm_hi[:, t % 2, :]), src))
                dve.tensor_tensor(diag(xm_lo[:, t % 2, :]), src, diag(xm_hi[:, t % 2, :].bitcast(F32)),
                                  ALU.subtract).then_inc(xm_ready, 1)

            def masked_h_lo(t):
                dve.wait_ge(hm_hi_ready, t + 1)
                dve.tensor_tensor(diag(hm_lo[:, :, :]), by_chunk(bank[T_BANK[t % 2]][:, :]),
                                  diag(hm_hi[:, :, :].bitcast(F32)), ALU.subtract).then_inc(hm_lo_ready, 1)

            def table_halves():
                dve.wait_ge(d_table, 16)
                link(dve.tensor_copy(table[:, :], table_raw[:, :]))
                dve.tensor_tensor(table[LO:K2, :], table_raw[LO:K2, :], table[LO:K2, :].bitcast(F32),
                                  ALU.subtract).then_inc(table_ready, 1)

            dve.wait_ge(d_xt, 16)
            dve.wait_ge(zeroed, 2)
            masked_x(0)
            masked_x(1)
            for k in (0, 2, 3):
                w = slice(k * 1024, (k + 1) * 1024)
                dve.wait_ge(wi_hi_ready, k + 1)
                dve.tensor_tensor(wi_lo[:, w], stage[:, k, :], wi_hi[:, w].bitcast(F32), ALU.subtract)\
                    .then_inc(wi_lo_ready, 1)
            table_halves()
            for k in (0, 2):
                w = slice(k * E, (k + 1) * E)
                dve.wait_ge(wo_hi_ready, k + 1)
                dve.tensor_tensor(wo_hl[:, w, 1, :], by_tile(stage_wo[:, k, :]), wo_hl[:, w, 0, :].bitcast(F32),
                                  ALU.subtract).then_inc(wo_lo_dve, 1)
            dve.wait_ge(ada_done, 1)
            dve.tensor_scalar(affine[:, 2, :], bank[3][:, 0:32], col("b_ada"), 1.0, ALU.add, ALU.add)
            dve.tensor_scalar(affine[:, 3, :], bank[3][:, 32:64], col("b_ada", 1), None, ALU.add)
            dve.wait_ge(hyp_done, 5)
            link(dve.tensor_scalar(hyp[:, 4, :], bank[7][:, 128:160], col("sty_b2"), None, ALU.add))
            dve.scalar_tensor_tensor(hyp[:, 5, :], hyp[:, 4, :], -1.0, hyp[:, 4, :], ALU.mult, ALU.min)\
                .then_inc(softplus_in, 1)
            dve.tensor_scalar(affine[:, 1, :], bank[7][:, 160:192], col("sty_b2", 1), None, ALU.add)
            dve.wait_ge(softplus_ln, 1)
            link(dve.scalar_tensor_tensor(affine[:, 0, :], hyp[:, 4, :], 0.0, hyp[:, 5, :], ALU.max, ALU.add))
            then(dve.tensor_scalar(affine[:, 0, :], affine[:, 0, :], 1e-8, None, ALU.add), affine_ready, 1)

            def row_stats(in_, n):
                link(dve.bn_stats(stat[:, n, 0:6], in_))
                dve.bn_aggr(stat[:, n, 6:8], stat[:, n, 0:6]).then_inc(var_ready, 1)

            def normalised(out, in_, n, done):
                dve.wait_ge(var_ready, done)
                dve.wait_ge(rstd_ready, done)
                return dve.tensor_scalar(out, in_, stat[:, n, 6:7], rstd[:, n:n + 1], ALU.subtract, ALU.mult)

            def residual(t):
                o = bank[O_BANK[t % 2]]
                dve.wait_ge(o_done, t + 1)
                link(dve.tensor_tensor(row[:, :], o[:, 0:D], rows_tm[:, t, :], ALU.add))
                link(dve.tensor_tensor(row[:, :], row[:, :], o[:, D:2 * D], ALU.add))
                row_stats(row[:, :], 0)

            def residual_norm(t):
                o = bank[O_BANK[t % 2]]
                link(normalised(row[:, :], row[:, :], 0, 2 * t + 1))
                link(dve.tensor_tensor(row[:, :], row[:, :], o[:, 2 * D:3 * D], ALU.mult))
                then(dve.tensor_tensor(row[:, :], row[:, :], o[:, 3 * D:4 * D], ALU.add), o_read, t + 1)

            def rotate(t):
                quads = row[:, :].rearrange("p (g c) -> p g c", c=4)
                pairs = row[:, :].rearrange("p (g a i) -> p g a i", a=2, i=2)
                swapped = turned[:, :].rearrange("p (g a i) -> p g a i", a=2, i=2)
                rot = rows_tm[:, t, :]
                dve.tensor_tensor(rot.rearrange("p (g c) -> p g c", c=4), quads,
                                  rot_c[:, t, 0:4].unsqueeze(1).broadcast_to([P, D // 4, 4]), ALU.mult)
                for i, k in ((0, 4), (1, 6)):
                    ins = dve.tensor_tensor(swapped[:, :, :, i], pairs[:, :, :, 1 - i],
                                            rot_c[:, t, k:k + 2].unsqueeze(1).broadcast_to([P, D // 4, 2]), ALU.mult)
                link(ins)
                link(dve.tensor_tensor(rot, rot, turned[:, :], ALU.add))
                row_stats(rot, 1)

            def rotate_norm(t):
                normalised(nrm_tm[:, t, :], rows_tm[:, t, :], 1, 2 * t + 2).then_inc(nrm_ready, 1)

            def center(hv):
                h = by_sample(cen[:, :])
                dve.wait_ge(h_ready, hv + 1)
                link(dve.tensor_reduce(sums[:, 0, :], h, AX.X, ALU.add))
                dve.scalar_tensor_tensor(h, per_sample(sums[:, 0, :]), -1.0 / S, h, ALU.mult, ALU.add)\
                    .then_inc(cen_ready, 1)

            def token_variance(hv):
                dve.wait_ge(sq_ready, hv + 1)
                link(dve.tensor_reduce(sums[:, 1, :], by_sample(sq[:, :]), AX.X, ALU.add))
                dve.tensor_scalar(sums[:, 1, :], sums[:, 1, :], 1.0 / S, None, ALU.mult).then_inc(svar_ready, 1)

            def affine_rows(hv):
                b0, b1 = hv * BH, (hv + 1) * BH
                h, out = by_sample(cen[:, :]), by_sample(hf[:, :])
                dve.wait_ge(srstd_ready, hv + 1)
                link(dve.tensor_tensor(sums[:, 2, :], sums[:, 2, :], affine[:, 0, b0:b1], ALU.mult))
                link(dve.tensor_tensor(out, h, per_sample(sums[:, 2, :]), ALU.mult))
                dve.tensor_tensor(out, out, per_sample(affine[:, 1, b0:b1]), ALU.add).then_inc(hf_ready, 1)

            def l2_lo(hv):
                c0, c1 = hv * HALF, (hv + 1) * HALF
                dve.wait_ge(hf_hi_ready, hv + 1)
                dve.tensor_tensor(hf_lo[:, c0:c1], hf[:, :], hf_hi[:, c0:c1].bitcast(F32), ALU.subtract)\
                    .then_inc(hf_lo_ready, 1)

            def wide(i):
                return rt_s[:, i, :].unsqueeze(2).broadcast_to([P, 4, E])

            def rt_v(i):
                return rt[:, i, :].rearrange("p (t e) -> p t e", e=E)

            def first_max(probs, largest, chosen):
                prefer = small("prefer").unsqueeze(1).broadcast_to([P, 4, E])
                link(dve.tensor_reduce(rt_s[:, largest, :], rt_v(probs), AX.X, ALU.max))
                link(dve.tensor_tensor(rt_v(chosen), rt_v(probs), wide(largest), ALU.is_equal))
                link(dve.tensor_tensor(rt_v(chosen), rt_v(chosen), prefer, ALU.mult))
                link(dve.tensor_reduce(rt_s[:, 7, :], rt_v(chosen), AX.X, ALU.max))
                link(dve.tensor_tensor(rt_v(chosen), rt_v(chosen), wide(7), ALU.is_equal))

            def router_shift(hv):
                logits = bank[NT_BANK[hv]][:, 0:4 * E].rearrange("p (t e) -> p t e", e=E)
                dve.wait_ge(logits_done, hv + 1)
                link(dve.tensor_reduce(rt_s[:, 0, :], logits, AX.X, ALU.max))
                dve.tensor_tensor(rt_v(0), logits, wide(0), ALU.subtract).then_inc(gates_z, 1)

            def router_first(hv):
                dve.wait_ge(gates_e, hv + 1)
                link(dve.tensor_reduce(rt_s[:, 1, :], rt_v(1), AX.X, ALU.add))
                link(dve.reciprocal(rt_s[:, 1, :], rt_s[:, 1, :]))
                link(dve.tensor_tensor(rt_v(2), rt_v(1), wide(1), ALU.mult))
                first_max(2, 2, 3)

            def router_second(hv):
                link(dve.scalar_tensor_tensor(rt_v(5), rt_v(3), -2.0, rt_v(2), ALU.mult, ALU.add))
                first_max(5, 4, 6)
                link(dve.tensor_tensor(rt_v(3), rt_v(3), rt_v(6), ALU.add))
                link(dve.tensor_tensor(rt_s[:, 6, :], rt_s[:, 2, :], rt_s[:, 4, :], ALU.add))
                link(dve.reciprocal(rt_s[:, 6, :], rt_s[:, 6, :]))
                link(dve.tensor_tensor(rt_v(3), rt_v(3), rt_v(2), ALU.mult))
                link(dve.tensor_tensor(rt_v(3), rt_v(3), wide(6), ALU.mult))
                link(dve.tensor_copy(comb_hi[:, :], rt[:, 3, :]))
                hi = comb_hi[:, :].bitcast(F32).rearrange("p (t e) -> p t e", e=E)
                if hv:
                    dve.wait_ge(comb_done, hv)
                dve.tensor_copy(comb_hl[:, :, 0:E], hi)
                dve.tensor_tensor(comb_hl[:, :, LO:K2], rt_v(3), hi, ALU.subtract).then_inc(comb_ready, 1)

            link(dve.memset(comb_hl[:, :, :], 0.0))
            dve.wait_ge(zeroed, 4)
            dve.wait_ge(rot_done, 1)
            dve.tensor_copy(rot_c[:, :, :], bank[6][:, 0:8 * T].rearrange("p (t c) -> p t c", c=8))\
                .then_inc(setup_done, 1)
            masked_h_lo(0)
            masked_x(2)
            dve.wait_ge(d_xtm, 16)
            for t in range(1, T):
                masked_h_lo(t)
                if t + 2 < T:
                    masked_x(t + 2)
                if t == 7:
                    l2_lo(0)
                    router_shift(0)
                    rotate(t - 2)
                    rotate_norm(t - 2)
                    router_first(0)
                    router_second(0)
                if t < T - 1:
                    residual(t - 1)
                    residual_norm(t - 1)
                if t == 6:
                    affine_rows(0)
                elif t < T - 1:
                    rotate(t - 1)
                    rotate_norm(t - 1)
                if t == 5:
                    center(0)
                    token_variance(0)

            def gate(n):
                hv, e = divmod(n, E)
                y = y_t[:, hv * HALF:(hv + 1) * HALF]
                dve.wait_ge(s2_done, (n + 1) * C)
                dve.wait_ge(gate_ready, n + 1)
                if n:
                    dve.wait_ge(y_ready, n)
                then(dve.tensor_tensor(y_gated[:, :], bank[Y_BANK[hv][e % 2]][:, :], gate_w[:, :], ALU.mult), z_ready, n + 1)
                dve.wait_ge(y_init, hv + 1)
                dve.tensor_tensor(y, y, y_gated[:, :], ALU.add).then_inc(y_ready, 1)

            def norm4_stats(rows, n):
                for i in range(4):
                    ins = dve.bn_stats(stat4[:, i, 0:6], rows[:, i, :])
                link(ins)
                for i in range(4):
                    ins = dve.bn_aggr(stat4[:, i, 6:8], stat4[:, i, 0:6])
                then(ins, var4_ready, n + 1)

            def norm4(rows, n):
                dve.wait_ge(rstd4_ready, n + 1)
                for i in range(4):
                    dve.tensor_scalar(nrm_tm[:, 4 * (n % 2) + i, :], rows[:, i, :], stat4[:, i, 6:7], rstd4[:, i:i + 1],
                                      ALU.subtract, ALU.mult).then_inc(nrm_ready, 1)

            def l3_start(hv):
                rows = rows_tm[:, 4 * hv:4 * hv + 4, :]
                dve.wait_ge(ytm_done, hv + 1)
                link(dve.tensor_tensor(rows, rows, by_tile(bank[YTM_BANK[hv]][:, :]), ALU.add))
                norm4_stats(rows, hv)

            def x3(hv):
                out = by_sample(x3_t[:, hv * HALF:(hv + 1) * HALF])
                b0, b1 = hv * BH, (hv + 1) * BH
                dve.wait_ge(nt3_done, hv + 1)
                link(dve.tensor_tensor(out, by_sample(bank[N3_BANK[hv]][:, :]), per_sample(affine[:, 2, b0:b1]), ALU.mult))
                dve.tensor_tensor(out, out, per_sample(affine[:, 3, b0:b1]), ALU.add).then_inc(x3_ready, 1)

            def query_low(hv, st):
                dve.wait_ge(q_hi_ready, 2 * hv + st + 1)
                for f in (slice(32, 64), slice(96, 128)):
                    a = q_t[st][f, hv * HALF:(hv + 1) * HALF]
                    dve.scalar_tensor_tensor(a.bitcast(F32R), bank[Q_BANK[hv][st]][f, :], col("bq", st)[f, :], a,
                                             ALU.add, ALU.subtract).then_inc(q_lo_ready, 1)

            def queries_by_head(hv, st):
                dve.wait_ge(q_lo_ready, 2 * (2 * hv + st + 1))
                for h4 in range(len(ACT_HEADS), H4):
                    dve.tensor_scalar(qx[hv][st][:, :, h4, :], by_sample(q_t[st][:, hv * HALF:(hv + 1) * HALF]),
                                      lt("head", h4, 1), None, ALU.mult).then_inc(qx_dve_ready, 1)

            def key_low(hv, st):
                dve.wait_ge(k_hi_ready, 2 * hv + st + 1)
                dve.scalar_tensor_tensor(kx[hv][:, st, :, 1, :], by_sample(bank[K_BANK[hv][st]][:, :]), col("bk", st),
                                         kx[hv][:, st, :, 0, :].bitcast(F32), ALU.add, ALU.subtract)\
                    .then_inc(k_lo_ready, 1)

            def scores(hv, part):
                n = 2 * HG * hv + part
                w = slice(part % 2 * (BH // 2), (part % 2 + 1) * (BH // 2))
                a = sc[:, hv, part // 2, w, :]
                ps = bank[SCORE_BANK[hv][part]][:, :].rearrange("p (b h s) -> p b h s", h=2, s=S)
                dve.wait_ge(score_done, n + 1)
                dve.wait_ge(bias_ready, hv * HG + part // 2 + 1)
                link(dve.scalar_tensor_tensor(a, ps[:, :, 0, :], SCALE, bias[:, hv, part // 2, w, :], ALU.mult, ALU.add))
                then(dve.scalar_tensor_tensor(a, ps[:, :, 1, :], SCALE, a, ALU.mult, ALU.add), score_read, n + 1)
                dve.tensor_reduce(smax[:, hv * HG + part // 2, w], a, AX.X, ALU.max).then_inc(smax_ready, 1)

            def transposed(hv, hg):
                dve.wait_ge(exp_ready, hv * HG + hg + 1)
                dve.transpose(pt[hv][:, hg, :, :], sc[:, hv, hg, :, :]).then_inc(pt_ready, 1)

            def reciprocals(hv, part):
                c = slice(part * (HALF // 2), (part + 1) * (HALF // 2))
                dve.wait_ge(sums_done, hv + 1)
                dve.reciprocal(recip[:, c], bank[SUM_BANK[hv]][:, c]).then_inc(recip_ready, 1)

            def divide(hv, part):
                n, c = 2 * hv + part, slice(part * (HALF // 2), (part + 1) * (HALF // 2))
                dve.wait_ge(recip_ready, n + 1)
                dve.wait_ge(ctx_done, n + 1)
                dve.tensor_tensor(ctx_t[:, hv * HALF + c.start:hv * HALF + c.stop],
                                  bank[CTX_BANK[hv][part]][:, 0:HALF // 2], recip[:, c], ALU.mult).then_inc(ctx_div, 1)

            def x4(hv):
                w = slice(hv * HALF, (hv + 1) * HALF)
                dve.wait_ge(wo_done, hv + 1)
                dve.scalar_tensor_tensor(x4_t[:, w], bank[WO_BANK[hv]][:, :], wo_bias[:, :], x3_t[:, w], ALU.add, ALU.add)\
                    .then_inc(x4_ready, 1)

            def x4_stats(hv):
                rows = by_tile(bank[X4_BANK[hv]][:, :])
                dve.wait_ge(x4tm_done, hv + 1)
                norm4_stats(rows, 2 + hv)

            def x4_rows(hv):
                rows = by_tile(bank[X4_BANK[hv]][:, :])
                dve.tensor_tensor(x4_tm[:, 4 * hv:4 * hv + 4, :], rows, lt("b2").unsqueeze(1).broadcast_to([P, 4, P]),
                                  ALU.add).then_inc(x4_tm_ready, 1)

            def x4_norm(hv):
                norm4(by_tile(bank[X4_BANK[hv]][:, :]), 2 + hv)

            def outputs(hv):
                w = slice(4 * hv, 4 * hv + 4)
                dve.wait_ge(f2_done, hv + 1)
                dve.tensor_tensor(out_tm[:, w, :], by_tile(bank[F2_BANK[hv]][:, :]), x4_tm[:, w, :], ALU.add)\
                    .then_inc(out_ready, 1)

            for q in range(MOE):
                if q:
                    dve.wait_ge(relu_ready, q)
                if q % C == C - 1 and q > C:
                    gate(q // C - 1)
                for i in range(2):
                    t = T - 2 + i
                    if q == 1 + 4 * i:
                        residual(t)
                    if q == 2 + 4 * i:
                        residual_norm(t)
                        rotate(t)
                    if q == 3 + 4 * i:
                        rotate_norm(t)
                if q == 13:
                    center(1)
                if q == 16:
                    token_variance(1)
                if q == 19:
                    affine_rows(1)
                if q == 21:
                    l2_lo(1)
                if q == 22:
                    router_shift(1)
                if q == 24:
                    router_first(1)
                if q == 26:
                    router_second(1)
                if q == R1 + 6:
                    l3_start(0)
                if q == R1 + 8:
                    norm4(rows_tm[:, 0:4, :], 0)
                if q == R1 + 9:
                    dve.wait_ge(wo_bias_done, 1)
                    dve.tensor_tensor(wo_bias[:, :], bank[YTM_BANK[0]][:, 0:1], col("bo"), ALU.add)\
                        .then_inc(wo_bias_ready, 1)
                if q == R1 + 10:
                    x3(0)
                for st in range(2):
                    if q == R1 + 12 + 3 * st:
                        query_low(0, st)
                    if q == R1 + 14 + 3 * st:
                        key_low(0, st)
                        queries_by_head(0, st)
                if R1 + 22 <= q < R1 + 30:
                    scores(0, q - R1 - 22)
                if q in range(R1 + 26, R1 + 32, 2):
                    transposed(0, (q - R1 - 26) // 2)
            transposed(0, HG - 1)
            gate(2 * E - 1)
            l3_start(1)
            reciprocals(0, 0)
            norm4(rows_tm[:, 4:8, :], 1)
            x3(1)
            reciprocals(0, 1)
            divide(0, 0)
            divide(0, 1)
            query_low(1, 0)
            key_low(1, 0)
            queries_by_head(1, 0)
            query_low(1, 1)
            key_low(1, 1)
            queries_by_head(1, 1)
            scores(1, 0)
            scores(1, 1)
            x4(0)
            for part in range(2, 6):
                scores(1, part)
            transposed(1, 0)
            scores(1, 6)
            x4_stats(0)
            scores(1, 7)
            transposed(1, 1)
            transposed(1, 2)
            transposed(1, 3)
            x4_norm(0)
            reciprocals(1, 0)
            reciprocals(1, 1)
            divide(1, 0)
            divide(1, 1)
            x4_rows(0)
            x4(1)
            x4_stats(1)
            x4_rows(1)
            x4_norm(1)
            outputs(0)
            outputs(1)

        @block.tensor
        def _(pe):
            def mm(out, lhsT, rhs, start=True, stop=True):
                return pe.matmul(out, lhsT, rhs, start=start, stop=stop)

            def product(out, w_hi, w_lo, m_hi, m_lo, start, stop):
                mm(out, w_hi, m_hi, start, False)
                mm(out, w_hi, m_lo, False, False)
                return mm(out, w_lo, m_hi, False, stop)

            def experts(t):
                word = pe.value_load(words[0:1, t:t + 1], min_val=0, max_val=F * (E ** J - 1))
                return [(word >> (DIGIT * j)) & (F * (E - 1)) for j in range(J)]

            pe.wait_ge(words_ready, 1)
            of_tile = {0: experts(0)}
            b7 = bank[7]
            pe.wait_ge(d_early, 16)
            pe.wait_ge(subj_ready, 1)
            mm(b7[0:64, 0:32], small("subj_emb", B), subj[:, :]).then_inc(hyp_done, 1)
            pe.wait_ge(hyp_ready, 1)
            mm(b7[:, 32:64], small("hyp_w1", 64), hyp[0:64, 0, :]).then_inc(hyp_done, 1)
            pe.wait_ge(hyp_ready, 2)
            mm(b7[:, 64:96], small("hyp_w2"), hyp[:, 1, :]).then_inc(hyp_done, 1)
            pe.wait_ge(hyp_ready, 3)
            mm(b7[0:64, 96:128], small("sty_w1"), hyp[:, 2, :]).then_inc(hyp_done, 1)
            pe.wait_ge(hyp_ready, 4)
            mm(b7[:, 128:160], small("sty_w2", 64, 0, P), hyp[0:64, 3, :])
            mm(b7[:, 160:192], small("sty_w2", 64, P, P), hyp[0:64, 3, :]).then_inc(hyp_done, 1)
            pe.wait_ge(time_ready, 1)
            mm(bank[3][:, 0:32], small("w_ada", k=0, n=P), time_emb[:, :])
            mm(bank[3][:, 32:64], small("w_ada", k=P, n=P), time_emb[:, :]).then_inc(ada_done, 1)

            def rotation():
                pe.wait_ge(rot_row_ready, 1)
                pe.wait_ge(of_sample_ready, 1)
                for t in range(T):
                    ins = mm(bank[6][:, 8 * t:8 * t + 8], of_sample[:, t * P:(t + 1) * P], rot_row[:, :])
                ins.then_inc(rot_done, 1)

            def l0_up(t):
                pe.wait_ge(xm_ready, t + 1)
                if t == 0:
                    pe.wait_ge(onehot_ready, 1)
                    pe.wait_ge(table_ready, 1)
                    pe.wait_ge(wi_lo_ready, 3)
                    pe.wait_ge(wi_lo_pool, 1)
                if t >= 2:
                    pe.wait_ge(gel_ready, t - 1)
                out = bank[H_BANK[t % 2]][:, :]
                mm(out, onehot[:, t * P:(t + 1) * P], table[:, 0:F], True, False)
                if t:
                    of_tile[t] = experts(t)
                for j, e in enumerate(of_tile[t]):
                    own = slice(j * P, (j + 1) * P)
                    ins = product(out, xm_hi[:, t % 2, own], xm_lo[:, t % 2, own],
                                  wi_hi[:, bass.ds(e, F)], wi_lo[:, bass.ds(e, F)], False, j == J - 1)
                ins.then_inc(h_done, 1)


            def l0_turn(t):
                pe.wait_ge(gel_ready, t + 1)
                if t >= 2:
                    pe.wait_ge(hm_lo_ready, t - 1)
                for c in range(C):
                    ins = pe.transpose(bank[T_BANK[t % 2]][:, c * P:(c + 1) * P], gel[:, t % 2, c * P:(c + 1) * P], ident)
                ins.then_inc(t_done, 1)

            def l0_down(t):
                o = bank[O_BANK[t % 2]]
                pe.wait_ge(hm_lo_ready, t + 1)
                if t >= 2:
                    pe.wait_ge(o_read, t - 1)
                else:
                    pe.wait_ge(wo_lo_ready, 2)
                    pe.wait_ge(wo_lo_dve, 2)
                mm(o[:, :], onehot[:, t * P:(t + 1) * P], table[:, F:TABLE], True, False)
                for j, e in enumerate(of_tile[t]):
                    own = slice(j * P, (j + 1) * P)
                    for c in range(C):
                        at = e * 2 + c * 2 * P
                        mm(o[:, 0:2 * D], hm_hi[:, c, own], wo_flat[:, bass.ds(at, 2 * P)], False, False)
                        ins = mm(o[:, 0:D], hm_lo[:, c, own], wo_flat[:, bass.ds(at, P)], False,
                                 j == J - 1 and c == C - 1)
                ins.then_inc(o_done, 1)

            wo_flat = wo_hl[:, :, :, :].rearrange("p c h d -> p (c h d)")

            def l2_turn(t):
                pe.wait_ge(nrm_ready, t + 1)
                pe.transpose(bank[NT_BANK[t // 4]][:, t % 4 * P:t % 4 * P + P], nrm_tm[:, t, :], ident)\
                    .then_inc(nt_done, 1)

            def logits(hv):
                pe.wait_ge(hf_ready, hv + 1)
                for i in range(4):
                    ins = mm(bank[NT_BANK[hv]][:, i * E:(i + 1) * E], hf[:, i * P:(i + 1) * P], small("router_w"))
                ins.then_inc(logits_done, 1)

            def gates_turn(hv):
                pe.wait_ge(comb_ready, hv + 1)
                for i in range(4):
                    ins = pe.transpose(bank[NT_BANK[hv]][0:K2, i * P:(i + 1) * P], comb_hl[:, i, :], ident)
                ins.then_inc(comb_done, 1)

            def gates_wide(n):
                hv, e = divmod(n, E)
                pe.wait_ge(y_init, hv + 1)
                if n == E:
                    pe.wait_ge(o_read, T)
                if n:
                    pe.wait_ge(gate_ready, n)
                mm(bank[GATE_BANK[hv]][:, :], pick[:, e:e + 1].broadcast_to([K2, P]),
                   comb_t[:, hv * HALF:(hv + 1) * HALF]).then_inc(combb_done, 1)

            def y_bias(hv):
                pe.wait_ge(comb_t_ready, hv + 1)
                mm(bank[NT_BANK[hv]][:, :], small("exp_b2", K2), comb_t[:, hv * HALF:(hv + 1) * HALF].bitcast(F32))\
                    .then_inc(y_bias_done, 1)

            def moe_up(q):
                hv, e, c = q // C // E, q // C % E, q % C
                w, x = slice(e * F + c * P, e * F + (c + 1) * P), slice(hv * HALF, (hv + 1) * HALF)
                pe.wait_ge(hf_lo_ready, hv + 1)
                pe.wait_ge(w1_lo_ready, e + 1)
                if q >= 3:
                    pe.wait_ge(relu_ready, q - 2)
                product(bank[HID_BANK[q % 3]][:, :], w1_hi[:, w], w1_lo[:, w], hf_hi[:, x], hf_lo[:, x], True, True)\
                    .then_inc(s1_done, 1)

            def moe_down(q):
                n, e, c = q // C, q // C % E, q % C
                if c == 0 and n == 1:
                    pe.wait_ge(o_read, T - 1)
                if c == 0 and n >= 2:
                    pe.wait_ge(z_ready, n - 1)
                if c == 0 and n == E:
                    pe.wait_ge(y_init, 2)
                y, w = bank[Y_BANK[n // E][e % 2]][:, :], w2[:, e * F + c * P:e * F + (c + 1) * P]
                pe.wait_ge(relu_ready, q + 1)
                ins = mm(y, w, relu_r[:, q % SLOTS, :], c == 0, c == C - 1)
                ins.then_inc(s2_done, 1)

            def y_turn(hv):
                pe.wait_ge(y_ready, E * (hv + 1))
                for i in range(4):
                    t = 4 * hv + i
                    ins = pe.transpose(bank[YTM_BANK[hv]][:, i * P:(i + 1) * P], y_t[:, t * P:(t + 1) * P], ident)
                ins.then_inc(ytm_done, 1)

            def n3_turn(hv):
                pe.wait_ge(nrm_ready, T + 4 * hv + 4)
                for i in range(4):
                    ins = pe.transpose(bank[N3_BANK[hv]][:, i * P:(i + 1) * P], nrm_tm[:, 4 * hv + i, :], ident)
                ins.then_inc(nt3_done, 1)

            def queries(hv, st):
                pe.wait_ge(x3_ready, hv + 1)
                if st and hv == 0:
                    pe.wait_ge(q_lo_ready, 2)
                elif hv == 0:
                    pe.wait_ge(wo_bias_ready, 1)
                mm(bank[Q_BANK[hv][st]][:, :], lt("wq", st * P, P), x3_t[:, hv * HALF:(hv + 1) * HALF]).then_inc(q_done, 1)

            def keys(hv, st):
                if st and hv == 0:
                    pe.wait_ge(k_lo_ready, 1)
                mm(bank[K_BANK[hv][st]][:, :], lt("wk", st * P, P), x3_t[:, hv * HALF:(hv + 1) * HALF]).then_inc(k_done, 1)

            def values(hv):
                pe.wait_ge(q_lo_ready, 4 * hv + 4)
                for i in range(4):
                    ins = mm(bank[V_BANK[hv]][:, i * P:(i + 1) * P], x3_t[:, (4 * hv + i) * P:(4 * hv + i + 1) * P], lt("wv"))
                ins.then_inc(v_done, 1)

            def scores(hv, part):
                n = 2 * HG * hv + part
                st, f = part // 4, slice(part // 2 % 2 * 64, part // 2 % 2 * 64 + 64)
                o = bank[SCORE_BANK[hv][part]]
                pe.wait_ge(qx_act_ready, len(ACT_HEADS) * (2 * hv + st + 1))
                pe.wait_ge(qx_dve_ready, (H4 - len(ACT_HEADS)) * (2 * hv + st + 1))
                pe.wait_ge(k_lo_ready, 2 * hv + st + 1)
                if hv == 0 and part == 0:
                    pe.wait_ge(v_ready, H4 * J)
                elif hv == 0 and part == 1:
                    pe.wait_ge(k_lo_ready, 2)
                elif hv == 0:
                    pe.wait_ge(score_read, n - 1)
                elif hv and part >= 3:
                    pe.wait_ge(score_read, n - 2)
                for i in range(BH // 2):
                    b = part % 2 * (BH // 2) + i
                    ins = mm(o[:, 2 * S * i:2 * S * (i + 1)], qx[hv][st][f, b, :, :], kx[hv][f, st, b, :, :])
                ins.then_inc(score_done, 1)

            def prob_sums(hv):
                pe.wait_ge(pt_ready, (hv + 1) * HG)
                if hv:
                    pe.wait_ge(ctx_div, 1)
                for hg in range(HG):
                    ins = mm(bank[SUM_BANK[hv]][hg * 32:hg * 32 + 32, :], lt("block", 0, 32), pt[hv][:, hg, :, :])
                ins.then_inc(sums_done, 1)

            def context(hv, part):
                o = bank[CTX_BANK[hv][part]]
                pe.wait_ge(v_ready, (hv + 1) * H4 * J)
                if part == 0:
                    pe.wait_ge(score_read, 2 * HG * (hv + 1))
                for hg in range(HG):
                    f = slice(hg * 32, hg * 32 + 32)
                    for i in range(BH // 2):
                        b = part * (BH // 2) + i
                        ins = mm(o[f, i * S:(i + 1) * S], vb[hv][:, b, f], pt[hv][:, hg, b, :])
                ins.then_inc(ctx_done, 1)

            def project(hv):
                pe.wait_ge(ctx_div, 2 * hv + 2)
                mm(bank[WO_BANK[hv]][:, :], lt("wo"), ctx_t[:, hv * HALF:(hv + 1) * HALF]).then_inc(wo_done, 1)

            def x4_turn(hv):
                pe.wait_ge(x4_ready, hv + 1)
                for i in range(4):
                    t = 4 * hv + i
                    ins = pe.transpose(bank[X4_BANK[hv]][:, i * P:(i + 1) * P], x4_t[:, t * P:(t + 1) * P], ident)
                ins.then_inc(x4tm_done, 1)

            def n4_turn(hv):
                pe.wait_ge(nrm_ready, 2 * T + 4 * hv + 4)
                for i in range(4):
                    ins = pe.transpose(bank[N4_BANK[hv]][:, i * P:(i + 1) * P], nrm_tm[:, 4 * hv + i, :], ident)
                ins.then_inc(n4_done, 1)

            def ffn_up(hv, c):
                pe.wait_ge(h4_ready, hv + 1)
                if hv == 0 and c == 1:
                    pe.wait_ge(x4_tm_ready, 1)
                if hv * C + c >= 2:
                    pe.wait_ge(ffn_ready, hv * C + c - 1)
                mm(bank[F1_BANK[c % 2]][:, :], lt("w1", c * P, P), h_t[:, hv * HALF:(hv + 1) * HALF])\
                    .then_inc(f1_done, 1)

            def ffn_down(hv, c):
                pe.wait_ge(ffn_ready, hv * C + c + 1)
                pe.wait_ge(x4_tm_ready, hv + 1)
                for i in range(4):
                    ins = mm(bank[F2_BANK[hv]][:, i * P:(i + 1) * P], ffn_h[hv][:, c, i * P:(i + 1) * P],
                             lt("w2", c * P, P), c == 0 and i == 0, c == C - 1 and i == 3)
                if c == C - 1:
                    ins.then_inc(f2_done, 1)

            l0_up(0)
            rotation()
            pe.wait_ge(zeroed, 4)
            for t in range(T):
                l0_turn(t)
                if t + 1 < T:
                    l0_up(t + 1)
                if 2 <= t < T - 1:
                    l2_turn(t - 2)
                if t == T - 1:
                    logits(0)
                l0_down(t)
            pe.wait_ge(d_w2, 16)
            for q in range(MOE + LAG):
                if q < MOE:
                    moe_up(q)
                if q == 1:
                    gates_turn(0)
                if q == 3:
                    y_bias(0)
                if q % C == 0 and q:
                    gates_wide(q // C - 1)
                if q >= LAG:
                    moe_down(q - LAG)
                if q == 1:
                    l2_turn(T - 3)
                if q == 7:
                    l2_turn(T - 2)
                if q == 11:
                    l2_turn(T - 1)
                if q == 21:
                    logits(1)
                if q == 29:
                    gates_turn(1)
                if q == 31:
                    y_bias(1)
                if q == R1 + 5:
                    y_turn(0)
                if q == R1 + 8:
                    pe.wait_ge(d_late, 16)
                    pe.wait_ge(var4_ready, 1)
                    mm(bank[YTM_BANK[0]][:, 0:1], lt("wo"), col("bv")).then_inc(wo_bias_done, 1)
                if q == R1 + 9:
                    n3_turn(0)
                for st in range(2):
                    if q == R1 + 11 + 3 * st:
                        queries(0, st)
                    if q == R1 + 12 + 3 * st:
                        keys(0, st)
                if q == R1 + 16:
                    values(0)
                if R1 + 21 <= q < R1 + 29:
                    scores(0, q - R1 - 21)
            y_turn(1)
            prob_sums(0)
            context(0, 0)
            n3_turn(1)
            context(0, 1)
            for st in range(2):
                queries(1, st)
                keys(1, st)
            for part in range(3):
                scores(1, part)
            project(0)
            values(1)
            scores(1, 3)
            scores(1, 4)
            x4_turn(0)
            for part in range(5, 2 * HG):
                scores(1, part)
            prob_sums(1)
            context(1, 0)
            n4_turn(0)
            context(1, 1)
            ffn_up(0, 0)
            project(1)
            ffn_up(0, 1)
            x4_turn(1)
            ffn_up(0, 2)
            ffn_up(0, 3)
            ffn_down(0, 0)
            ffn_down(0, 1)
            ffn_down(0, 2)
            n4_turn(1)
            ffn_down(0, 3)
            ffn_up(1, 0)
            ffn_up(1, 1)
            ffn_down(1, 0)
            ffn_up(1, 2)
            ffn_down(1, 1)
            ffn_up(1, 3)
            ffn_down(1, 2)
            ffn_down(1, 3)


def laid_out(i):
    f32 = np.float32

    def columns(parts, layout_of, width, rows=P):
        a = np.zeros((rows, width), f32)
        for name, v in parts.items():
            lo, hi = layout_of[name]
            a[:v.shape[0], lo:hi] = v
        return a

    def vectors(*arrays):
        out = []
        for v in arrays:
            v = v.reshape(-1, min(v.shape[-1], P)).T
            out.append(np.concatenate([v, np.zeros((P - v.shape[0], v.shape[1]), f32)]))
        return np.concatenate(out, axis=1)

    def chunked(w):
        w = w.reshape(-1, C, P, D)
        return np.ascontiguousarray(w.transpose(2, 0, 1, 3).reshape(P, -1))

    x = np.asarray(i["x"]).reshape(N, D)
    row = np.arange(P)
    expert_row = np.where(row < E, row, np.where((row >= LO) & (row < K2), row - LO, -1))
    stacked = np.arange(D).reshape(HG, 1, 32).repeat(2, axis=1).reshape(-1)
    half = D // 2
    freqs = np.exp(np.arange(half, dtype=f32) * f32(-np.log(10000.0) / (half - 1)))
    turn = np.zeros((P, ANG), f32)
    turn[half:, :B] = 0.25
    turn[:, B + 1::2] = 0.25
    exp_b2 = np.zeros((K2, P), f32)
    exp_b2[0:E] = exp_b2[LO:K2] = i["L2_cond_exp_b2"]
    early = columns({
        "ident": np.eye(P, dtype=f32), "expert_row": expert_row[:, None], "sample_row": row[:, None],
        "freq": np.concatenate([freqs, freqs])[:, None], "turn": turn, "quarter": (turn * 4 * (np.pi / 2)).astype(f32),
        "prefer": np.tile(E - np.arange(E), (P, 1)), "digit": np.tile(F * E ** (np.arange(B) % J), (P, 1)), "pick": (expert_row[:, None] == np.arange(E)),
        "angles": np.stack([i["condB_theta"], i["condB_phi"]], axis=1),
        "cols": vectors(i["L2_cond_exp_b1"], i["L3_cond_b1"], i["L2_cond_ln_g"], i["L2_cond_ln_b"],
                        i["L2_cond_hyp_b1"], i["L2_cond_hyp_b2"], i["L2_cond_sty_b1"], i["L2_cond_sty_b2"],
                        i["L3_cond_b_ada"], i["L3_cond_bq"][stacked], i["L3_cond_bk"][stacked], i["L3_cond_bv"], i["L3_cond_bo"],
                        i["L3_cond_g2"], i["L3_cond_beta2"]),
        "subj_emb": i["L2_cond_subj_emb"], "hyp_w1": i["L2_cond_hyp_w1"], "hyp_w2": i["L2_cond_hyp_w2"],
        "sty_w1": i["L2_cond_sty_w1"], "sty_w2": i["L2_cond_sty_w2"], "w_ada": i["L3_cond_W_ada"],
        "router_w": i["L2_cond_router_w"], "exp_b2": exp_b2}, EARLY, EARLY_W)
    head = row[:, None] % 32 // DH == np.arange(H4)
    block = np.tile(row[:, None] // 32 == np.arange(32) // DH, (1, HG))
    late = columns({
        "head": head, "block": block,
        "wq": i["L3_cond_Wq"][:, stacked], "wk": i["L3_cond_Wk"][:, stacked], "wv": i["L3_cond_Wv"],
        "wo": i["L3_cond_Wo"], "w1": i["L3_cond_W1"], "w2": chunked(i["L3_cond_W2"]),
        "b2": np.tile(i["L3_cond_b2"], (P, 1))}, LATE, LATE_W)
    tables = np.zeros((K2, TABLE), f32)
    tables[0:E] = tables[LO:K2] = np.concatenate(
        [i["L0_cond_bi"], i["L0_cond_bo"], np.zeros((E, D), f32), i["L0_cond_gamma"], i["L0_cond_beta"]], axis=1)
    ids = np.concatenate([i["itok_B_0_7"], i["itok_B_6_14"], i["itok_B_34_63"]]).astype(np.int32)
    wide = lambda w: np.ascontiguousarray(w.transpose(1, 0, 2).reshape(P, -1))
    return {
        "x_tm": np.ascontiguousarray(x.reshape(T, P, D).transpose(1, 0, 2)), "x_t": np.ascontiguousarray(x.T),
        "ids": np.tile(ids, (P, 1)), "early": early, "late": late, "tables": tables,
        "wi": wide(i["L0_cond_Wi"]), "wo": chunked(i["L0_cond_Wo"]),
        "w1": wide(i["L2_cond_exp_w1"]), "w2": chunked(i["L2_cond_exp_w2"]),
        "fside": np.ascontiguousarray(i["fside_Bx16xSxS_0"].reshape(2, BH, HG, H4, S, S).transpose(3, 4, 0, 2, 1, 5)
                                      .reshape(P, 2, HG, BH, S)),
        "mask": np.tile(i["mask_Bx1xSxS_bk0"].reshape(B, S, S).transpose(1, 0, 2).reshape(S, B * S), (H4, 1)),
    }


def kernel(**inputs):
    import concourse.bacc as bacc
    from concourse.bass_utils import run_bass_kernel_spmd

    nc = bacc.Bacc("TRN2", target_bir_lowering=False, num_devices=1)
    arrays = laid_out({k: np.asarray(v) for k, v in inputs.items()})
    args = [nc.dram_tensor(f"in_{k}", a.shape, mybir.dt.from_np(a.dtype), kind="ExternalInput").ap()
            for k, a in arrays.items()]
    out = nc.dram_tensor("out", (P, T, D), F32, kind="ExternalOutput").ap()
    build(nc, *args, out)
    r = run_bass_kernel_spmd(nc, [{f"in_{k}": a for k, a in arrays.items()}], core_ids=[0])
    got = r.results[0]["out"]
    return got.transpose(1, 0, 2).reshape(B, S, D)
```
